# Optimizing a Trainium2 kernel written in Bass

```python
import numpy as np
import jax
import jax.numpy as jnp

def _softmax(x, axis=-1):
    return jax.nn.softmax(x, axis=axis)

def _gelu(x):
    return jax.nn.gelu(x, approximate=True)

def _silu(x):
    return jax.nn.silu(x)

def _sigmoid(x):
    return jax.nn.sigmoid(x)

def _layernorm(x, axis=-1, eps=1e-05):
    m = jnp.mean(x, axis=axis, keepdims=True)
    v = jnp.var(x, axis=axis, keepdims=True)
    return (x - m) / jnp.sqrt(v + eps)

def _scatter_add(tgt, idx, src, axis=0):
    return tgt.at[idx].add(src)

def _segment_sum(src, seg, n):
    return jax.ops.segment_sum(src, seg, n)
kernel_name = 'mk_xattn_ffn_d2_seqx_r8_c8e7ea'

def setup_inputs(seed: int=0):
    np.random.seed(seed)
    _w = jnp.asarray

    def _rec_inputs():
        import jax
        import jax.numpy as jnp
        _rk = jax.random.key(seed)
        x = 0.0003765 + 1 * jax.random.normal(jax.random.fold_in(_rk, 1), (8, 128, 256), jnp.float32)
        _lenS = 128 - jax.random.randint(jax.random.fold_in(_rk, 7), (8,), 0, max(1, 128 // 4) + 1, jnp.int32)
        _lenS2 = 128 - jax.random.randint(jax.random.fold_in(_rk, 8), (8,), 0, max(1, 128 // 4) + 1, jnp.int32)
        _ctx_2048P = jax.random.normal(jax.random.fold_in(_rk, 11), (8, 16, 256), jnp.float32)
        _ctx_2048c = jax.random.dirichlet(jax.random.fold_in(_rk, 511), 0.3 * jnp.ones((16,), jnp.float32), (8, 128))
        _ctx_2048t = jnp.einsum('bsk,bkd->bsd', _ctx_2048c, _ctx_2048P)
        _ctx_2048t = _ctx_2048t * jax.lax.rsqrt(jnp.mean(jnp.square(_ctx_2048t)) + 1e-12) * 0.953939
        ctx_2048 = -0.000292821 + 1.00034 * (_ctx_2048t + 0.3 * jax.random.normal(jax.random.fold_in(_rk, 611), (8, 128, 256), jnp.float32))
        return (x, ctx_2048)
    x, ctx_2048 = _rec_inputs()

    def _L0_xattn_setup():
        import jax, jax.numpy as jnp
        import numpy as np
        key = jax.random.key(seed)
        k1, k2, k3, k4, k5 = jax.random.split(key, 5)
        B, D_MODEL, L = (2, 128, 256)
        HEAD_DIM = 8
        H = D_MODEL // HEAD_DIM
        return {'k': jax.random.normal(k1, (B, D_MODEL, L), dtype=jnp.float32), 'v': jax.random.normal(k2, (B, D_MODEL, L), dtype=jnp.float32), 'q': jax.random.normal(k3, (B, D_MODEL, L), dtype=jnp.float32), 'ssm_kernel': jax.random.normal(k4, (H, L), dtype=jnp.float32), 'D': jax.random.normal(k5, (H,), dtype=jnp.float32), 'head_dim': HEAD_DIM}
    _L0_xattn_all = _L0_xattn_setup()
    _L0_xattn_in = {k: v for k, v in _L0_xattn_all.items() if k in ('ssm_kernel', 'D')}
    del _L0_xattn_all

    def _L0_ffn_setup():
        import jax, jax.numpy as jnp
        import numpy as np
        NUM_EXPERTS = 8
        TOP_K = 2
        HIDDEN = 256
        INTER = 256
        SWIGLU_LIMIT = 7.0
        BATCH, SEQ = (4, 256)
        key = jax.random.key(seed)
        k0, k1, k2, k3, k4 = jax.random.split(key, 5)
        x = jax.random.normal(k0, (BATCH, SEQ, HIDDEN), jnp.float32)
        Wr = jax.random.normal(k1, (HIDDEN, NUM_EXPERTS), jnp.float32) * 0.02
        Wg = jax.random.normal(k2, (NUM_EXPERTS, HIDDEN, INTER), jnp.float32) * 0.02
        Wu = jax.random.normal(k3, (NUM_EXPERTS, HIDDEN, INTER), jnp.float32) * 0.02
        Wd = jax.random.normal(k4, (NUM_EXPERTS, INTER, HIDDEN), jnp.float32) * 0.02
        return {'hidden_states': x, 'Wr': Wr, 'Wg': Wg, 'Wu': Wu, 'Wd': Wd}
    _L0_ffn_all = _L0_ffn_setup()
    _L0_ffn_in = {k: v for k, v in _L0_ffn_all.items() if k in ('Wr', 'Wg', 'Wu', 'Wd')}
    del _L0_ffn_all

    def _L1_xattn_setup():
        import jax, jax.numpy as jnp
        import numpy as np
        B, DIM1, DIM2, LATENT, T = (16, 128, 128, 64, 256)
        LN_EPS = 1e-05
        key = jax.random.key(seed)
        ks = jax.random.split(key, 8)

        def xavier(k, shape):
            fan_out, fan_in = shape
            std = float(np.sqrt(2.0 / (fan_in + fan_out)))
            return jax.random.normal(k, shape, dtype=jnp.float32) * std
        return {'input1': jax.random.normal(ks[0], (B, DIM1, T), dtype=jnp.float32), 'input2': jax.random.normal(ks[1], (B, DIM2, T), dtype=jnp.float32), 'theta_w': xavier(ks[2], (LATENT, DIM2)), 'theta_b': jnp.zeros((LATENT,), jnp.float32), 'phi_w': xavier(ks[3], (LATENT, DIM1)), 'phi_b': jnp.zeros((LATENT,), jnp.float32), 'g_w': xavier(ks[4], (LATENT, DIM1)), 'g_b': jnp.zeros((LATENT,), jnp.float32), 'ln_gamma': jnp.ones((LATENT, T), jnp.float32), 'ln_beta': jnp.zeros((LATENT, T), jnp.float32), 'out_w': xavier(ks[5], (DIM2, LATENT)), 'out_b': jnp.zeros((DIM2,), jnp.float32)}
    _L1_xattn_all = _L1_xattn_setup()
    _L1_xattn_in = {k: v for k, v in _L1_xattn_all.items() if k in ('theta_w', 'theta_b', 'phi_w', 'phi_b', 'g_w', 'g_b', 'ln_gamma', 'ln_beta', 'out_w', 'out_b')}
    del _L1_xattn_all

    def _L1_ffn_setup():
        import jax, jax.numpy as jnp
        import numpy as np
        B, S, DIM = (4, 64, 256)
        E, INTER = (32, 128)
        G, TOPK_G, TOPK = (8, 4, 6)
        ROUTE_SCALE = 2.5
        SHARED_INTER = 2 * INTER

        def _gate(xf, gate_w):
            scores = jax.nn.sigmoid(xf @ gate_w.T)
            gs = scores.reshape(-1, G, E // G)
            group_scores = gs.max(axis=-1)
            _, gidx = jax.lax.top_k(group_scores, TOPK_G)
            gmask = jnp.any(jnp.arange(G)[None, None, :] == gidx[:, :, None], axis=1)
            masked = jnp.where(gmask[:, :, None], gs, -jnp.inf).reshape(-1, E)
            _, idx = jax.lax.top_k(masked, TOPK)
            w = jnp.take_along_axis(scores, idx, axis=1)
            w = w / jnp.sum(w, axis=-1, keepdims=True) * ROUTE_SCALE
            return (w, idx)
        key = jax.random.key(seed)
        ks = jax.random.split(key, 8)
        sd = 0.02
        return {'x': jax.random.normal(ks[0], (B, S, DIM), jnp.float32), 'gate_w': jax.random.normal(ks[1], (E, DIM), jnp.float32) * sd, 'w11': jax.random.normal(ks[2], (E, INTER, DIM), jnp.float32) * sd, 'w33': jax.random.normal(ks[3], (E, INTER, DIM), jnp.float32) * sd, 'w22': jax.random.normal(ks[4], (E, DIM, INTER), jnp.float32) * sd, 'sw1': jax.random.normal(ks[5], (SHARED_INTER, DIM), jnp.float32) * sd, 'sw2': jax.random.normal(ks[6], (DIM, SHARED_INTER), jnp.float32) * sd, 'sw3': jax.random.normal(ks[7], (SHARED_INTER, DIM), jnp.float32) * sd}
    _L1_ffn_all = _L1_ffn_setup()
    _L1_ffn_in = {k: v for k, v in _L1_ffn_all.items() if k in ('gate_w', 'w11', 'w33', 'w22', 'sw1', 'sw2', 'sw3')}
    del _L1_ffn_all
    return {'x': x, 'ctx_2048': ctx_2048, 'L0_xattn_ssm_kernel': _L0_xattn_in['ssm_kernel'], 'L0_xattn_D': _L0_xattn_in['D'], 'L0_ffn_Wr': _L0_ffn_in['Wr'], 'L0_ffn_Wg': _L0_ffn_in['Wg'], 'L0_ffn_Wu': _L0_ffn_in['Wu'], 'L0_ffn_Wd': _L0_ffn_in['Wd'], 'L1_xattn_theta_w': _L1_xattn_in['theta_w'], 'L1_xattn_theta_b': _L1_xattn_in['theta_b'], 'L1_xattn_phi_w': _L1_xattn_in['phi_w'], 'L1_xattn_phi_b': _L1_xattn_in['phi_b'], 'L1_xattn_g_w': _L1_xattn_in['g_w'], 'L1_xattn_g_b': _L1_xattn_in['g_b'], 'L1_xattn_ln_gamma': _L1_xattn_in['ln_gamma'], 'L1_xattn_ln_beta': _L1_xattn_in['ln_beta'], 'L1_xattn_out_w': _L1_xattn_in['out_w'], 'L1_xattn_out_b': _L1_xattn_in['out_b'], 'L1_ffn_gate_w': _L1_ffn_in['gate_w'], 'L1_ffn_w11': _L1_ffn_in['w11'], 'L1_ffn_w33': _L1_ffn_in['w33'], 'L1_ffn_w22': _L1_ffn_in['w22'], 'L1_ffn_sw1': _L1_ffn_in['sw1'], 'L1_ffn_sw2': _L1_ffn_in['sw2'], 'L1_ffn_sw3': _L1_ffn_in['sw3']}

def reference(x, ctx_2048, L0_xattn_ssm_kernel, L0_xattn_D, L0_ffn_Wr, L0_ffn_Wg, L0_ffn_Wu, L0_ffn_Wd, L1_xattn_theta_w, L1_xattn_theta_b, L1_xattn_phi_w, L1_xattn_phi_b, L1_xattn_g_w, L1_xattn_g_b, L1_xattn_ln_gamma, L1_xattn_ln_beta, L1_xattn_out_w, L1_xattn_out_b, L1_ffn_gate_w, L1_ffn_w11, L1_ffn_w33, L1_ffn_w22, L1_ffn_sw1, L1_ffn_sw2, L1_ffn_sw3):
    import jax
    import jax.numpy as jnp

    def _L0_xattn_ref(k, v, q, ssm_kernel, D, head_dim):
        import jax, jax.numpy as jnp
        import numpy as np
        B, HD, L = k.shape
        H = HD // head_dim
        fft_size = 2 * L
        k_ = k.reshape(B, H, head_dim, L)
        v_ = v.reshape(B, H, head_dim, L)
        q_ = q.reshape(B, H, head_dim, L)
        kv = jnp.einsum('bhil,bhjl->bijhl', k_, v_)
        kv_f = jnp.fft.rfft(kv, n=fft_size)
        kernel_f = jnp.fft.rfft(ssm_kernel, n=fft_size)
        y = jnp.fft.irfft(kv_f * kernel_f, n=fft_size)[..., :L]
        out = y + kv * D[None, None, None, :, None]
        out = jnp.einsum('bijhl,bhil->bjhl', out, q_)
        out = jnp.transpose(out, (0, 2, 1, 3)).reshape(B, H * head_dim, L)
        return out.astype(k.dtype)

    def _L0_ffn_ref(hidden_states, Wr, Wg, Wu, Wd):
        import jax, jax.numpy as jnp
        import numpy as np
        NUM_EXPERTS = 8
        TOP_K = 2
        HIDDEN = 256
        INTER = 256
        SWIGLU_LIMIT = 7.0
        BATCH, SEQ = (4, 256)
        router_logits = jnp.einsum('bsh,he->bse', hidden_states, Wr)
        topk_logits, selected = jax.lax.top_k(router_logits, TOP_K)
        router_probs = jax.nn.softmax(topk_logits, axis=-1)
        out = jnp.zeros_like(hidden_states)
        for e in range(NUM_EXPERTS):
            w_e = jnp.where(selected == e, router_probs, 0.0).sum(axis=-1, keepdims=True)
            g = jnp.einsum('bsh,hi->bsi', hidden_states, Wg[e])
            g = jnp.clip(jax.nn.silu(g), -SWIGLU_LIMIT, SWIGLU_LIMIT)
            u = jnp.einsum('bsh,hi->bsi', hidden_states, Wu[e])
            h = jnp.einsum('bsi,ih->bsh', g * u, Wd[e])
            out = out + h * w_e
        return out

    def _L1_xattn_ref(input1, input2, theta_w, theta_b, phi_w, phi_b, g_w, g_b, ln_gamma, ln_beta, out_w, out_b):
        import jax, jax.numpy as jnp
        import numpy as np
        B, DIM1, DIM2, LATENT, T = (16, 128, 128, 64, 256)
        LN_EPS = 1e-05
        theta_x = jnp.einsum('ld,bdt->btl', theta_w, input2) + theta_b
        phi_x = jnp.einsum('ld,bdt->blt', phi_w, input1) + phi_b[:, None]
        scores = jnp.einsum('btl,bls->bts', theta_x, phi_x)
        p = jax.nn.softmax(scores, axis=-1)
        g_x = jnp.einsum('ld,bdt->btl', g_w, input1) + g_b
        t_x = jnp.einsum('bts,bsl->blt', p, g_x)
        mu = jnp.mean(t_x, axis=(1, 2), keepdims=True)
        var = jnp.var(t_x, axis=(1, 2), keepdims=True)
        h = (t_x - mu) * jax.lax.rsqrt(var + LN_EPS) * ln_gamma + ln_beta
        h = jax.nn.relu(h)
        w_t = jnp.einsum('ol,blt->bot', out_w, h) + out_b[None, :, None]
        return w_t + input2

    def _L1_ffn_ref(x, gate_w, w11, w33, w22, sw1, sw2, sw3):
        import jax, jax.numpy as jnp
        import numpy as np
        B, S, DIM = (4, 64, 256)
        E, INTER = (32, 128)
        G, TOPK_G, TOPK = (8, 4, 6)
        ROUTE_SCALE = 2.5
        SHARED_INTER = 2 * INTER

        def _gate(xf, gate_w):
            scores = jax.nn.sigmoid(xf @ gate_w.T)
            gs = scores.reshape(-1, G, E // G)
            group_scores = gs.max(axis=-1)
            _, gidx = jax.lax.top_k(group_scores, TOPK_G)
            gmask = jnp.any(jnp.arange(G)[None, None, :] == gidx[:, :, None], axis=1)
            masked = jnp.where(gmask[:, :, None], gs, -jnp.inf).reshape(-1, E)
            _, idx = jax.lax.top_k(masked, TOPK)
            w = jnp.take_along_axis(scores, idx, axis=1)
            w = w / jnp.sum(w, axis=-1, keepdims=True) * ROUTE_SCALE
            return (w, idx)
        xf = x.reshape(-1, DIM)
        T = xf.shape[0]
        w, idx = _gate(xf, gate_w)
        c = jnp.zeros((T, E), xf.dtype).at[jnp.arange(T)[:, None], idx].add(w)
        g = jnp.einsum('td,eid->tei', xf, w11)
        u = jnp.einsum('td,eid->tei', xf, w33)
        act = jax.nn.silu(g) * u
        y = jnp.einsum('tei,te,edi->td', act, c, w22)
        shared = jax.nn.silu(xf @ sw1.T) * (xf @ sw3.T) @ sw2.T
        return (y + shared).reshape(x.shape)
    x = x + _L0_xattn_ref(ctx_2048, ctx_2048, _layernorm(x, axis=-1), L0_xattn_ssm_kernel, L0_xattn_D, 8)
    x = x + _L0_ffn_ref(_layernorm(x, axis=-1), L0_ffn_Wr, L0_ffn_Wg, L0_ffn_Wu, L0_ffn_Wd)
    x = x + _L1_xattn_ref(_layernorm(x, axis=-1), ctx_2048, L1_xattn_theta_w, L1_xattn_theta_b, L1_xattn_phi_w, L1_xattn_phi_b, L1_xattn_g_w, L1_xattn_g_b, L1_xattn_ln_gamma, L1_xattn_ln_beta, L1_xattn_out_w, L1_xattn_out_b)
    x = x + _L1_ffn_ref(_layernorm(x, axis=-1), L1_ffn_gate_w, L1_ffn_w11, L1_ffn_w33, L1_ffn_w22, L1_ffn_sw1, L1_ffn_sw2, L1_ffn_sw3)
    return x

_drawn_inputs = setup_inputs


def setup_inputs(seed=0):
    import zlib

    import numpy as np

    out = dict(_drawn_inputs(seed))
    spreads = {'L1_xattn_theta_b': (0.0, 0.8),
     'L1_xattn_phi_b': (0.0, 2.0),
     'L1_xattn_g_b': (0.0, 2.0),
     'L1_xattn_ln_gamma': (1.0, 0.6),
     'L1_xattn_ln_beta': (0.0, 0.8),
     'L1_xattn_out_b': (0.0, 2.0)}
    factors = {'L0_ffn_Wr': 8.0,
     'L0_ffn_Wg': 8.0,
     'L0_ffn_Wu': 8.0,
     'L0_ffn_Wd': 8.0,
     'L1_xattn_theta_w': 4.151,
     'L1_xattn_phi_w': 4.151,
     'L1_xattn_g_w': 4.189,
     'L1_xattn_out_w': 3.466,
     'L1_ffn_gate_w': 8.0,
     'L1_ffn_w11': 8.0,
     'L1_ffn_w33': 8.0,
     'L1_ffn_w22': 8.0,
     'L1_ffn_sw1': 8.0,
     'L1_ffn_sw2': 8.0,
     'L1_ffn_sw3': 8.0}
    for name, (base, spread) in spreads.items():
        noise = np.random.default_rng([zlib.crc32(name.encode()), seed]).standard_normal(out[name].shape)
        drawn = base * np.exp(spread * noise) if base else spread * noise
        out[name] = jnp.asarray(drawn.astype(out[name].dtype))
    for name, factor in factors.items():
        out[name] = (out[name] * factor).astype(out[name].dtype)
    return out
```

```python
from contextlib import ExitStack

import concourse.bass as bass
from concourse import mybir

P = 128
B, S, D = 8, 128, 256
TOK = B * S
KB = D // P
HALF = TOK // 2
HEADS, HD = 16, 8
PAIRS = HD * HD
KPAD = P - 1 + D + 1
UNIT_W = 3 * D
LAT = 64
E0, UNITS0 = 8, 16
E1, UNITS1 = 32, 34
GROUPS, GSIZE, TOPG, TOPK1 = 8, 4, 4, 6
ROUTE_SCALE = 2.5
SWIGLU_LIMIT = 7.0
EPS = 1e-5
LOWEST = -3.0e38
TAKEN = 9.0
PAD = -5.0


def build(nc, x_d, ctx_d, ctxr_d, filt_d, skip_d, wr_d, unit0_d, theta_d, theta_b_d, phi_d, phi_b_d, g_d, g_b_d,
          gamma_d, beta_d, outw_d, outb_d, gate_d, unit1_d, out_d, filt_s, c0_s, c1_s):
    f32, f32r = mybir.dt.float32, mybir.dt.float32r
    ACT = mybir.ActivationFunctionType
    ALU = mybir.AluOpType
    AX = mybir.AxisListType

    def view(t, offset, dims):
        base = t[:]
        return bass.AP(base.tensor, base.offset + offset, [list(base.ap[0])] + [list(d) for d in dims])

    with ExitStack() as stack:
        def sb(name, shape, dt=f32):
            return stack.enter_context(nc.sbuf_tensor(name, shape, dt))

        def sem(name):
            return stack.enter_context(nc.semaphore(name))

        x_sb = sb("x_sb", [P, B, D])
        h_sb = sb("h_sb", [P, B, D])
        ctx_sb = sb("ctx_sb", [P, B, D])
        ctxr_sb = sb("ctxr_sb", [P, KB, B, P])
        ident = sb("ident", [P, P])
        filt_row = sb("filt_row", [HEADS, KPAD])
        skip_col = sb("skip_col", [HEADS, 1])
        toep = [sb(f"toep{i}", [P, D]) for i in range(2)]
        kv = [sb(f"kv{i}", [P, KB, B * PAIRS]) for i in range(2)]
        qT = sb("qT", [P, KB, HEADS, B * HD])
        prod = [sb(f"prod{i}", [P, KB, B * PAIRS]) for i in range(2)]
        oT = sb("oT", [P, KB, B, P])
        stats = sb("stats", [P, B, 6])
        mv = sb("mv", [P, B, 2])
        veps = sb("veps", [P, B])
        std = sb("std", [P, B])
        rstd = sb("rstd", [P, B])
        nwt = sb("nwt", [P, B])
        hT_hi = sb("hT_hi", [P, KB, TOK], f32r)
        hT_lo = sb("hT_lo", [P, KB, TOK], f32r)
        wr_sb = sb("wr_sb", [P, KB, E0])
        gate_sb = sb("gate_sb", [P, KB, E1])
        rw_hi = [sb(f"rw_hi{i}", [P, KB, e], f32r) for i, e in enumerate((E0, E1))]
        rw_lo = [sb(f"rw_lo{i}", [P, KB, e], f32r) for i, e in enumerate((E0, E1))]
        w_raw = [sb(f"w_raw{i}", [P, UNIT_W]) for i in range(2)]
        w_hi = [sb(f"w_hi{i}", [P, UNIT_W], f32r) for i in range(2)]
        w_lo = [sb(f"w_lo{i}", [P, UNIT_W], f32r) for i in range(2)]
        c_all = [sb(f"c_all{i}", [P, TOK]) for i in range(2)]
        silu_g = [sb(f"silu_g{i}", [P, HALF]) for i in range(2)]
        silu_c = [sb(f"silu_c{i}", [P, HALF]) for i in range(2)]
        hid = [sb(f"hid{i}", [P, HALF]) for i in range(2)]
        hid_hi = [sb(f"hid_hi{i}", [P, HALF], f32r) for i in range(2)]
        hid_lo = [sb(f"hid_lo{i}", [P, HALF], f32r) for i in range(2)]
        zeros = sb("zeros", [P, P], f32r)
        yT = sb("yT", [P, KB, TOK])
        logit = sb("logit", [P, B, 2 * E0])
        top8 = sb("top8", [P, B, 8])
        ex = sb("ex", [P, B, E0])
        marked = sb("marked", [P, B, 2 * E0])
        score = sb("score", [P, B, E1 + 8])
        gmax = sb("gmax", [P, B, 2 * GROUPS])
        gmask = sb("gmask", [P, B, GROUPS])
        gneg = sb("gneg", [P, B, GROUPS])
        allowed = sb("allowed", [P, B, E1 + 8])
        marked1 = sb("marked1", [P, B, E1 + 8])
        gates = [sb("gates0", [P, B, E0]), sb("gates1", [P, B, E1])]
        gsum = sb("gsum", [P, B])
        grec = sb("grec", [P, B])
        cT = sb("cT", [E1, TOK])
        ones2 = sb("ones2", [2, TOK])
        theta_sb = sb("theta_sb", [P, LAT])
        phi_sb = sb("phi_sb", [P, LAT])
        gw_sb = sb("gw_sb", [P, LAT])
        theta_b = sb("theta_b", [LAT, 1])
        phi_b = sb("phi_b", [LAT, 1])
        g_b = sb("g_b", [P, LAT])
        gamma_sb = sb("gamma_sb", [LAT, D])
        beta_sb = sb("beta_sb", [LAT, D])
        outw_sb = sb("outw_sb", [LAT, P])
        outb_sb = sb("outb_sb", [P, 1])
        thT = sb("thT", [LAT, B, D])
        phT = sb("phT", [LAT, B, D])
        gx = sb("gx", [P, B, KB, LAT])
        nmax = sb("nmax", [P, B, KB])
        psum_row = sb("psum_row", [P, B, KB])
        prec = sb("prec", [P, B, KB])
        prob = [sb(f"prob{i}", [P, KB, D]) for i in range(2)]
        probT = [sb(f"probT{i}", [P, KB, D]) for i in range(2)]
        tx = sb("tx", [LAT, B, D])
        stats2 = sb("stats2", [LAT, B, 6])
        mv2 = sb("mv2", [LAT, B, 2])
        mean_all = sb("mean_all", [LAT, B])
        dev = sb("dev", [LAT, B])
        spread = sb("spread", [LAT, B])
        veps2 = sb("veps2", [LAT, B])
        std2 = sb("std2", [LAT, B])
        rstd2 = sb("rstd2", [LAT, B])
        nwt2 = sb("nwt2", [LAT, B])
        shift2 = sb("shift2", [LAT, B])
        avg = sb("avg", [LAT, LAT])
        bank = [stack.enter_context(nc.psum_tensor(f"bank{i}", [P, 512], f32)) for i in range(8)]

        x_in, filt_in, skip_in, ctx_in, par_in, rw_in = (sem(n) for n in (
            "x_in", "filt_in", "skip_in", "ctx_in", "par_in", "rw_in"))
        ctxr_in = sem("ctxr_in")
        filt_summed, filt_out = sem("filt_summed"), sem("filt_out")
        toep_in = [sem(f"toep_in{i}") for i in range(2)]
        ident_made, consts_made, dve_consts = sem("ident_made"), sem("consts_made"), sem("dve_consts")
        dve_step = sem("dve_step")
        var_ready, std_ready, normed = sem("var_ready"), sem("std_ready"), sem("normed")
        q_turned, q_copied = sem("q_turned"), sem("q_copied")
        kv_made, conv_done, prod_made, head_done = sem("kv_made"), sem("conv_done"), sem("prod_made"), sem("head_done")
        o_turned, x_added = sem("o_turned"), sem("x_added")
        hT_turned, hT_hi_made, hT_lo_made = sem("hT_turned"), sem("hT_hi_made"), sem("hT_lo_made")
        rw_hi_made, rw_split = sem("rw_hi_made"), sem("rw_split")
        logits_done, act_gate_in, act_gate_out = sem("logits_done"), sem("act_gate_in"), sem("act_gate_out")
        gates_made, gates_turned, cT_copied, c_out = (sem(n) for n in (
            "gates_made", "gates_turned", "cT_copied", "c_out"))
        y_done, yT_copied, y_turned = sem("y_done"), sem("yT_copied"), sem("y_turned")

        class Ffn:

            def __init__(self, n):
                self.raw_in = [sem(f"raw_in{n}_{i}") for i in range(2)]
                self.raw_used = [sem(f"raw_used{n}_{i}") for i in range(2)]
                self.c_in = [sem(f"c_in{n}_{i}") for i in range(2)]
                self.c_used = [sem(f"c_used{n}_{i}") for i in range(2)]
                self.w_hi_made = sem(f"w_hi_made{n}")
                self.w_split = sem(f"w_split{n}")
                self.g_done = sem(f"g_done{n}")
                self.u_done = sem(f"u_done{n}")
                self.silu_made = sem(f"silu_made{n}")
                self.silu_c_made = sem(f"silu_c_made{n}")
                self.hid_made = sem(f"hid_made{n}")
                self.hid_hi_made = sem(f"hid_hi_made{n}")
                self.hid_split = sem(f"hid_split{n}")
                self.hid_free = sem(f"hid_free{n}")

        ffns = [Ffn(0), Ffn(1)]
        th_done, th_copied, ph_done, ph_copied, gx_done, gx_copied = (sem(n) for n in (
            "th_done", "th_copied", "ph_done", "ph_copied", "gx_done", "gx_copied"))
        sc_done, max_made, exp_made, prob_made, pT_turned, pT_copied, tx_done, tx_copied, tx_stats = (sem(n) for n in (
            "sc_done", "max_made", "exp_made", "prob_made", "pT_turned", "pT_copied", "tx_done", "tx_copied",
            "tx_stats"))
        mean_in, mean_done, dev_in, dev_done, var2_ready, std2_ready, shift_made = (sem(n) for n in (
            "mean_in", "mean_done", "dev_in", "dev_done", "var2_ready", "std2_ready", "shift_made"))
        z_made, zg_made, zb_made, relu_made, w_done, ctx_added = (sem(n) for n in (
            "z_made", "zg_made", "zb_made", "relu_made", "w_done", "ctx_added"))
        out_done = sem("out_done")

        block = stack.enter_context(nc.Block())
        NPAIR = [UNITS0 // 2, UNITS1 // 2]
        unit_d = [unit0_d, unit1_d]
        c_s = [c0_s, c1_s]

        @block.sync
        def _(sp):
            sp.dma_start(filt_row[:], filt_d).then_inc(filt_in, 16)
            sp.dma_start(skip_col[:], skip_d).then_inc(filt_in, 16)
            sp.dma_start(ctxr_sb[:, 0], ctxr_d[0]).then_inc(ctxr_in, 16)
            sp.dma_start(ctxr_sb[:, 1], ctxr_d[1]).then_inc(ctxr_in, 16)
            sp.wait_ge(filt_summed, 1)
            sp.dma_start(filt_s, filt_row[:]).then_inc(filt_out, 16)
            sp.wait_ge(filt_out, 16)

            def load_toeplitz(h, slot):
                src = bass.AP(filt_s.tensor, filt_s.offset + h * KPAD, [[1, P], [1, D]])
                sp.dma_start(toep[slot][:], src).then_inc(toep_in[slot], 16)

            load_toeplitz(0, 0)
            load_toeplitz(1, 1)

            def load_unit(n, unit, slot):
                sp.dma_start(w_raw[slot][:], unit_d[n][unit]).then_inc(ffns[n].raw_in[slot], 16)

            def load_c(n, unit, slot):
                sp.dma_start(c_all[slot][:], c_s[n][unit].partition_broadcast(P)).then_inc(ffns[n].c_in[slot], 16)

            sp.dma_start(ctx_sb[:], ctx_d.rearrange("b s d -> s b d")).then_inc(ctx_in, 16)
            load_unit(0, 0, 0)
            load_unit(0, 1, 1)
            with sp.Fori(1, HEADS // 2) as i:
                for slot in range(2):
                    sp.wait_ge(conv_done, 2 * i + slot - 1)
                    load_toeplitz(2 * i + slot, slot)

            for n in range(2):
                f = ffns[n]
                if n == 0:
                    pass
                else:
                    for slot in range(2):
                        sp.wait_ge(ffns[0].raw_used[slot], NPAIR[0])
                        load_unit(1, slot, slot)
                sp.wait_ge(cT_copied, 2 * (n + 1))
                if n == 0:
                    dst = c0_s.rearrange("(e t) k -> e t k", t=2)
                    for t in range(2):
                        sp.dma_start(dst[:, t], cT[0:E0, :]).then_inc(c_out, 16)
                    sp.wait_ge(c_out, 32)
                else:
                    sp.dma_start(c1_s[0:E1], cT[0:E1, :]).then_inc(c_out, 16)
                    sp.wait_ge(consts_made, 1)
                    sp.dma_start(c1_s[E1:UNITS1], ones2[:]).then_inc(c_out, 16)
                    sp.wait_ge(c_out, 64)
                load_c(n, 0, 0)
                load_c(n, 1, 1)
                with sp.Fori(1, NPAIR[n]) as i:
                    for slot in range(2):
                        sp.wait_ge(f.raw_used[slot], i)
                        load_unit(n, 2 * i + slot, slot)
                        sp.wait_ge(f.c_used[slot], i)
                        load_c(n, 2 * i + slot, slot)
            for q in range(4):
                sp.wait_ge(x_added, 16 + q + 1 - 4)
                sp.dma_start(out_d.rearrange("b s d -> s b d")[:, 2 * q:2 * q + 2], x_sb[:, 2 * q:2 * q + 2])\
                    .then_inc(out_done, 16)
            sp.wait_ge(out_done, 64)

        @block.gpsimd
        def _(pool):
            nc.gpsimd.memset(ident[:], 0.0).then_inc(ident_made, 1)
            pool.wait_ge(ident_made, 1)
            nc.gpsimd.affine_select(out=ident[:], in_=ident[:], compare_op=ALU.not_equal, fill=1.0, base=0,
                                    pattern=[[-1, P]], channel_multiplier=1).then_inc(ident_made, 1)
            pool.wait_ge(ctxr_in, 32)

            def products(h, slot):
                for blk in range(KB):
                    rows = ctxr_sb[:, blk].rearrange("p b (h j) -> p b h j", j=HD)[:, :, bass.ds(h, 1), :]\
                        .rearrange("p b o j -> p b (o j)")
                    k = rows.unsqueeze(3).to_broadcast([P, B, HD, HD])
                    v = rows.unsqueeze(2).to_broadcast([P, B, HD, HD])
                    last = nc.gpsimd.tensor_tensor(
                        kv[slot][:, blk].rearrange("p (b i j) -> p b i j", i=HD, j=HD), k, v, ALU.mult)
                last.then_inc(kv_made, 1)

            products(0, 0)
            products(1, 1)
            with pool.Fori(1, HEADS // 2) as i:
                for slot in range(2):
                    pool.wait_ge(conv_done, 2 * i + slot - 1)
                    products(2 * i + slot, slot)
            nc.gpsimd.memset(ones2[:], 1.0)
            nc.gpsimd.memset(avg[:], 1.0 / LAT).then_inc(consts_made, 1)

            def low_part(f, slot, lo, hi, wait):
                pool.wait_ge(f.w_hi_made, wait)
                ins = nc.gpsimd.tensor_tensor(w_lo[slot][:, lo:hi], w_raw[slot][:, lo:hi],
                                              w_hi[slot][:, lo:hi].bitcast(f32), ALU.subtract)
                ins.then_inc(f.w_split, 1)
                return ins

            def unit_low(f, unit, slot):
                low_part(f, slot, 0, 2 * D, 2 * unit + 1)
                low_part(f, slot, 2 * D, 3 * D, 2 * unit + 2)
                pool.wait_ge(f.w_split, 2 * unit + 2)
                nc.gpsimd.sem_inc(f.raw_used[slot], 1)

            for n in range(2):
                f = ffns[n]
                unit_low(f, 0, 0)
                with pool.Fori(0, NPAIR[n] - 1) as i:
                    unit_low(f, 2 * i + 1, 1)
                    unit_low(f, 2 * i + 2, 0)
                unit_low(f, 2 * NPAIR[n] - 1, 1)
                if n == 0:
                    pool.wait_ge(normed, 3 * B)
                    pool.wait_ge(ctx_in, 16)
                    nc.gpsimd.tensor_tensor(x_sb[:], x_sb[:], ctx_sb[:], ALU.add).then_inc(ctx_added, 1)
                    for c in range(4):
                        pool.wait_ge(zg_made, c + 1)
                        chunk = tx[:, 2 * c:2 * c + 2]
                        nc.gpsimd.tensor_tensor(chunk, chunk, beta_sb[:].unsqueeze(1).to_broadcast([LAT, 2, D]),
                                                ALU.add).then_inc(zb_made, 1)

        @block.scalar
        def _(act):
            act.dma_start(x_sb[:], x_d.rearrange("b s d -> s b d")).then_inc(x_in, 16)
            act.dma_start(wr_sb[:], wr_d.rearrange("(k p) e -> p k e", p=P)).then_inc(rw_in, 16)
            act.dma_start(gate_sb[:], gate_d.rearrange("(k p) e -> p k e", p=P)).then_inc(rw_in, 16)
            for dst, src in ((theta_sb[:], theta_d), (phi_sb[:], phi_d), (gw_sb[:], g_d), (theta_b[:], theta_b_d),
                             (phi_b[:], phi_b_d), (g_b[:], g_b_d.partition_broadcast(P)),
                             (gamma_sb[:], gamma_d), (beta_sb[:], beta_d), (outw_sb[:], outw_d),
                             (outb_sb[:], outb_d)):
                act.dma_start(dst, src).then_inc(par_in, 16)

            def sqrt_of_var(k):
                act.wait_ge(var_ready, k + 1)
                nc.scalar.activation(std[:], veps[:], ACT.Sqrt).then_inc(std_ready, 1)

            sqrt_of_var(0)
            act.wait_ge(rw_in, 32)
            for n, w in enumerate((wr_sb, gate_sb)):
                nc.scalar.activation(rw_hi[n][:], w[:], ACT.Copy).then_inc(rw_hi_made, 1)
            for c in range(4):
                act.wait_ge(q_turned, c + 1)
                for blk in range(KB):
                    src = bank[c][:].rearrange("p (b k h i) -> p k b h i", b=2, k=KB, i=HD)[:, blk]
                    dst = qT[:, blk].rearrange("p h (b i) -> p b h i", i=HD)[:, 2 * c:2 * c + 2]
                    last = nc.scalar.activation(dst, src, ACT.Copy)
                last.then_inc(q_copied, 1)

            def unit_high(f, unit, slot, part, raw_wait):
                lo, hi = ((0, 2 * D), (2 * D, 3 * D))[part]
                if part == 0:
                    act.wait_ge(f.raw_in[slot], raw_wait)
                nc.scalar.activation(w_hi[slot][:, lo:hi], w_raw[slot][:, lo:hi], ACT.Copy)\
                    .then_inc(f.w_hi_made, 1)

            for n in range(2):
                f = ffns[n]
                sqrt_of_var(1 if n == 0 else 3)
                unit_high(f, 0, 0, 0, 16)
                unit_high(f, 0, 0, 1, 16)
                for c in range(4):
                    act.wait_ge(hT_turned, 4 * n + c + 1)
                    half, k = c // 2, c % 2
                    nc.scalar.activation(hT_hi[:, k, half * HALF:(half + 1) * HALF], bank[c][:], ACT.Copy)\
                        .then_inc(hT_hi_made, 1)
                if n == 0:
                    act.wait_ge(act_gate_in, 1)
                    nc.scalar.activation(ex[:], ex[:], ACT.Exp).then_inc(act_gate_out, 1)
                else:
                    act.wait_ge(logits_done, 2)
                    nc.scalar.activation(score[:, :, 0:E1], bank[0][:, 0:B * E1].rearrange("p (b e) -> p b e", e=E1),
                                         ACT.Sigmoid).then_inc(act_gate_out, 1)
                ne = (E0, E1)[n]
                for c in range(2):
                    act.wait_ge(gates_turned, 2 * n + c + 1)
                    nc.scalar.activation(cT[0:ne, c * HALF:(c + 1) * HALF], bank[1 + c][0:ne, :], ACT.Copy)\
                        .then_inc(cT_copied, 1)

                def steps(i, last):
                    for j in range(4):
                        q, slot = 4 * i + j, j % 2
                        act.wait_ge(f.g_done, q + 1)
                        nc.scalar.activation(silu_g[slot][:], bank[4 + 2 * slot][:], ACT.Silu)\
                            .then_inc(f.silu_made, 1)
                        act.wait_ge(f.hid_made, q + 1)
                        act.wait_ge(f.hid_free, q + 1)
                        nc.scalar.activation(hid_hi[slot][:], hid[slot][:], ACT.Copy).then_inc(f.hid_hi_made, 1)
                        if last and j >= 2:
                            continue
                        u = 2 * i + j // 2 + 1
                        uslot = (j // 2 + 1) % 2
                        unit_high(f, u, uslot, j % 2, 16 * (i + 1 if uslot else i + 2))

                with act.Fori(0, NPAIR[n] - 1) as i:
                    steps(i, False)
                steps(NPAIR[n] - 1, True)
                for c in range(4):
                    act.wait_ge(y_done, n + 1)
                    half, k = c % 2, c // 2
                    nc.scalar.activation(yT[:, k, half * HALF:(half + 1) * HALF], bank[c][:], ACT.Copy)\
                        .then_inc(yT_copied, 1)
                if n == 1:
                    continue

                act.wait_ge(par_in, 160)
                for c in range(4):
                    act.wait_ge(th_done, c + 1)
                    nc.scalar.activation(thT[:, 2 * c:2 * c + 2].rearrange("p b t -> p (b t)"), bank[c][0:LAT, :],
                                         ACT.Identity, bias=theta_b[:]).then_inc(th_copied, 1)
                sqrt_of_var(2)
                for c in range(4):
                    act.wait_ge(ph_done, c + 1)
                    nc.scalar.activation(phT[:, 2 * c:2 * c + 2].rearrange("p b t -> p (b t)"), bank[4 + c][0:LAT, :],
                                         ACT.Identity, bias=phi_b[:]).then_inc(ph_copied, 1)

                def exps(b):
                    act.wait_ge(max_made, b + 1)
                    if b >= 2:
                        act.wait_ge(pT_turned, b - 1)
                    for t in range(KB):
                        last = nc.scalar.activation(prob[b % 2][:, t], bank[4 + b % 2][:, t * D:(t + 1) * D], ACT.Exp,
                                                    bias=nmax[:, b, t:t + 1], accum_out=psum_row[:, b, t:t + 1])
                    last.then_inc(exp_made, 1)

                def copy_pT(b):
                    act.wait_ge(pT_turned, b + 1)
                    if b >= 2:
                        act.wait_ge(tx_done, b - 1)
                    nc.scalar.activation(probT[b % 2][:].rearrange("p k t -> p (k t)"), bank[6 + b % 2][:], ACT.Copy)\
                        .then_inc(pT_copied, 1)

                def copy_tx(b):
                    act.wait_ge(tx_done, b + 1)
                    nc.scalar.activation(tx[:, b], bank[2 + b % 2][0:LAT, 0:D], ACT.Copy).then_inc(tx_copied, 1)

                exps(0)
                for b in range(B):
                    if b + 1 < B:
                        exps(b + 1)
                    copy_pT(b)
                    if b >= 1:
                        copy_tx(b - 1)
                copy_tx(B - 1)
                act.wait_ge(var2_ready, 1)
                nc.scalar.activation(std2[:], veps2[:], ACT.Sqrt).then_inc(std2_ready, 1)
                act.wait_ge(shift_made, 1)
                for b in range(B):
                    nc.scalar.activation(tx[:, b], tx[:, b], ACT.Identity, scale=rstd2[:, b:b + 1],
                                         bias=shift2[:, b:b + 1]).then_inc(z_made, 1)
                for c in range(4):
                    act.wait_ge(zb_made, c + 1)
                    nc.scalar.activation(tx[:, 2 * c:2 * c + 2], tx[:, 2 * c:2 * c + 2], ACT.Relu)\
                        .then_inc(relu_made, 1)

        @block.vector
        def _(dve):
            count = [0]

            def link(ins):
                count[0] += 1
                ins.then_inc(dve_step, 1)
                dve.wait_ge(dve_step, count[0])

            def newton(r, s, v, t):
                link(nc.vector.reciprocal(r, s))
                link(nc.vector.tensor_tensor(t, r, r, ALU.mult))
                link(nc.vector.tensor_tensor(t, t, v, ALU.mult))
                link(nc.vector.tensor_scalar(t, t, -0.5, 1.5, ALU.mult, ALU.add))
                link(nc.vector.tensor_tensor(r, r, t, ALU.mult))

            def layer_norm(k):
                for b in range(B):
                    last = nc.vector.bn_stats(stats[:, b, :], x_sb[:, b, :])
                link(last)
                for b in range(B):
                    last = nc.vector.bn_aggr(mv[:, b, :], stats[:, b, :])
                link(last)
                nc.vector.tensor_scalar(veps[:], mv[:, :, 1], EPS, None, ALU.add).then_inc(var_ready, 1)
                dve.wait_ge(std_ready, k + 1)
                newton(rstd[:], std[:], veps[:], nwt[:])
                for b in range(B):
                    nc.vector.tensor_scalar(h_sb[:, b, :], x_sb[:, b, :], mv[:, b, 0:1], rstd[:, b:b + 1],
                                            ALU.subtract, ALU.mult).then_inc(normed, 1)

            def add_banks(turned, wait, first_bank):
                for c in range(4):
                    dve.wait_ge(turned, wait + c)
                    dst = x_sb[:, 2 * c:2 * c + 2].rearrange("p b d -> p (b d)")
                    ins = nc.vector.tensor_tensor(dst, dst, bank[first_bank + c][:], ALU.add)
                    ins.then_inc(x_added, 1)

            dve.wait_ge(filt_in, 32)
            nc.vector.tensor_tensor(filt_row[:, P - 1:P], filt_row[:, P - 1:P], skip_col[:], ALU.add)\
                .then_inc(filt_summed, 1)
            dve.wait_ge(x_in, 16)
            layer_norm(0)
            nc.vector.memset(zeros[:].bitcast(f32), 0.0)
            nc.vector.memset(logit[:, :, E0:2 * E0], LOWEST)
            nc.vector.memset(gmax[:, :, GROUPS:2 * GROUPS], PAD)
            nc.vector.memset(allowed[:, :, E1:E1 + 8], PAD).then_inc(dve_consts, 1)
            for n, w in enumerate((wr_sb, gate_sb)):
                dve.wait_ge(rw_hi_made, n + 1)
                nc.vector.tensor_tensor(rw_lo[n][:], w[:], rw_hi[n][:].bitcast(f32), ALU.subtract)\
                    .then_inc(rw_split, 1)

            dve.wait_ge(q_copied, 4)

            def head(h, slot):
                dve.wait_ge(conv_done, h + 1)
                q = qT[:, :, bass.ds(h, 1), :].rearrange("p k o n -> p k (o n)").unsqueeze(3)\
                    .to_broadcast([P, KB, B * HD, HD])
                for blk in range(KB):
                    ins = nc.vector.tensor_tensor(
                        prod[slot][:, blk].rearrange("p (n j) -> p n j", j=HD),
                        bank[4 + 2 * slot + blk][:].rearrange("p (n j) -> p n j", j=HD), q[:, blk], ALU.mult)
                ins.then_inc(prod_made, 1)
                dve.wait_ge(prod_made, h + 1)
                o = oT[:].rearrange("p k b (h j) -> p (k b) h j", j=HD)[:, :, bass.ds(h, 1), :]\
                    .rearrange("p n o j -> p n (o j)")
                nc.vector.tensor_reduce(o, prod[slot][:].rearrange("p k (b i j) -> p (k b) j i", i=HD, j=HD),
                                        AX.X, ALU.add).then_inc(head_done, 1)

            with dve.Fori(0, HEADS // 2) as i:
                for slot in range(2):
                    head(2 * i + slot, slot)
            add_banks(o_turned, 1, 0)

            for n in range(2):
                f = ffns[n]
                if n == 1:
                    dve.wait_ge(x_added, 12)
                else:
                    dve.wait_ge(x_added, 4)
                layer_norm(1 if n == 0 else 3)
                for c in range(4):
                    dve.wait_ge(hT_hi_made, 4 * n + c + 1)
                    half, k = c // 2, c % 2
                    cols = slice(half * HALF, (half + 1) * HALF)
                    nc.vector.tensor_tensor(hT_lo[:, k, cols], bank[c][:], hT_hi[:, k, cols].bitcast(f32),
                                            ALU.subtract).then_inc(hT_lo_made, 1)
                g = gates[n]
                if n == 0:
                    dve.wait_ge(logits_done, 1)
                    link(nc.vector.tensor_copy(logit[:, :, 0:E0],
                                               bank[0][:, 0:B * E0].rearrange("p (b e) -> p b e", e=E0)))
                    for b in range(B):
                        last = nc.vector.max(out=top8[:, b, :], in_=logit[:, b, 0:E0])
                    link(last)
                    nc.vector.tensor_tensor(ex[:], logit[:, :, 0:E0], top8[:, :, 0:1].to_broadcast([P, B, E0]),
                                            ALU.subtract).then_inc(act_gate_in, 1)
                    dve.wait_ge(act_gate_in, 1)
                    link(nc.vector.memset(top8[:, :, 2:8], LOWEST))
                    for b in range(B):
                        last = nc.vector.match_replace(out=marked[:, b, :], in_to_replace=top8[:, b, :],
                                                       in_values=logit[:, b, :], imm_value=-LOWEST)
                    link(last)
                    dve.wait_ge(act_gate_out, 1)
                    link(nc.vector.scalar_tensor_tensor(out=g[:], in0=marked[:, :, 0:E0], scalar=-LOWEST, in1=ex[:],
                                                        op0=ALU.is_equal, op1=ALU.mult))
                    link(nc.vector.tensor_reduce(gsum[:], g[:], AX.X, ALU.add))
                    link(nc.vector.reciprocal(grec[:], gsum[:]))
                    nc.vector.tensor_tensor(g[:], g[:], grec[:].unsqueeze(2).to_broadcast([P, B, E0]), ALU.mult)\
                        .then_inc(gates_made, 1)
                else:
                    dve.wait_ge(act_gate_out, 2)
                    s4 = score[:, :, 0:E1].rearrange("p b (g i) -> p b g i", i=GSIZE)
                    link(nc.vector.tensor_reduce(gmax[:, :, 0:GROUPS], s4, AX.X, ALU.max))
                    for b in range(B):
                        last = nc.vector.max(out=top8[:, b, :], in_=gmax[:, b, 0:GROUPS])
                    link(last)
                    link(nc.vector.memset(top8[:, :, TOPG:8], PAD))
                    for b in range(B):
                        last = nc.vector.match_replace(out=marked[:, b, :], in_to_replace=top8[:, b, :],
                                                       in_values=gmax[:, b, :], imm_value=TAKEN)
                    link(last)
                    link(nc.vector.tensor_scalar(gmask[:], marked[:, :, 0:GROUPS], TAKEN, None, ALU.is_equal))
                    link(nc.vector.tensor_scalar(gneg[:], gmask[:], -1.0, None, ALU.add))
                    a4 = allowed[:, :, 0:E1].rearrange("p b (g i) -> p b g i", i=GSIZE)
                    for bh in range(2):
                        bs = slice(4 * bh, 4 * bh + 4)
                        last = nc.vector.tensor_tensor(
                            a4[:, bs], s4[:, bs],
                            gmask[:, bs].unsqueeze(3).to_broadcast([P, 4, GROUPS, GSIZE]), ALU.mult)
                    link(last)
                    for bh in range(2):
                        bs = slice(4 * bh, 4 * bh + 4)
                        last = nc.vector.tensor_tensor(
                            a4[:, bs], a4[:, bs],
                            gneg[:, bs].unsqueeze(3).to_broadcast([P, 4, GROUPS, GSIZE]), ALU.add)
                    link(last)
                    for b in range(B):
                        last = nc.vector.max(out=top8[:, b, :], in_=allowed[:, b, 0:E1])
                    link(last)
                    link(nc.vector.memset(top8[:, :, TOPK1:8], PAD))
                    for b in range(B):
                        last = nc.vector.match_replace(out=marked1[:, b, :], in_to_replace=top8[:, b, :],
                                                       in_values=allowed[:, b, :], imm_value=TAKEN)
                    link(last)
                    link(nc.vector.scalar_tensor_tensor(out=g[:], in0=marked1[:, :, 0:E1], scalar=TAKEN,
                                                        in1=score[:, :, 0:E1], op0=ALU.is_equal, op1=ALU.mult))
                    link(nc.vector.tensor_reduce(gsum[:], g[:], AX.X, ALU.add))
                    link(nc.vector.reciprocal(grec[:], gsum[:]))
                    link(nc.vector.tensor_tensor(g[:], g[:], grec[:].unsqueeze(2).to_broadcast([P, B, E1]), ALU.mult))
                    nc.vector.tensor_scalar(g[:], g[:], ROUTE_SCALE, None, ALU.mult).then_inc(gates_made, 1)

                def steps(i):
                    for j in range(4):
                        q, slot, uslot, half = 4 * i + j, j % 2, j // 2, j % 2
                        dve.wait_ge(f.silu_made, q + 1)
                        if half == 0:
                            dve.wait_ge(f.c_in[uslot], 16 * (i + 1))
                        c = c_all[uslot][:, half * HALF:(half + 1) * HALF]
                        if n == 0:
                            ins = nc.vector.scalar_tensor_tensor(out=silu_c[slot][:], in0=silu_g[slot][:],
                                                                 scalar=SWIGLU_LIMIT, in1=c, op0=ALU.min, op1=ALU.mult)
                        else:
                            ins = nc.vector.tensor_tensor(silu_c[slot][:], silu_g[slot][:], c, ALU.mult)
                        ins.then_inc(f.silu_c_made, 1)
                        dve.wait_ge(f.silu_c_made, q + 1)
                        dve.wait_ge(f.u_done, q + 1)
                        nc.vector.tensor_tensor(hid[slot][:], silu_c[slot][:], bank[5 + 2 * slot][:], ALU.mult)\
                            .then_inc(f.hid_made, 1)
                        if half == 1:
                            dve.sem_inc(f.c_used[uslot], 1)
                        dve.wait_ge(f.hid_hi_made, q + 1)
                        nc.vector.tensor_tensor(hid_lo[slot][:], hid[slot][:], hid_hi[slot][:].bitcast(f32),
                                                ALU.subtract).then_inc(f.hid_split, 1)

                with dve.Fori(0, NPAIR[n]) as i:
                    steps(i)
                add_banks(y_turned, 4 * n + 1, 4)
                if n == 1:
                    continue

                dve.wait_ge(x_added, 8)
                layer_norm(2)
                dve.wait_ge(par_in, 160)
                for c in range(2):
                    dve.wait_ge(gx_done, c + 1)
                    nc.vector.tensor_tensor(gx[:, 4 * c:4 * c + 4].rearrange("p b k l -> p (b k) l"),
                                            bank[c][:].rearrange("p (n l) -> p n l", l=LAT),
                                            g_b[:].unsqueeze(1).to_broadcast([P, 4 * KB, LAT]), ALU.add)\
                        .then_inc(gx_copied, 1)

                def row_max(b):
                    dve.wait_ge(sc_done, b + 1)
                    nc.vector.tensor_reduce(nmax[:, b, :], bank[4 + b % 2][:].rearrange("p (k t) -> p k t", k=KB),
                                            AX.X, ALU.max, negate=True).then_inc(max_made, 1)

                def normalise(b):
                    dve.wait_ge(exp_made, b + 1)
                    link(nc.vector.reciprocal(prec[:, b, :], psum_row[:, b, :]))
                    for t in range(KB):
                        last = nc.vector.tensor_scalar(prob[b % 2][:, t], prob[b % 2][:, t], prec[:, b, t:t + 1],
                                                       None, ALU.mult)
                    last.then_inc(prob_made, 1)

                def tx_statistics(b):
                    dve.wait_ge(tx_copied, b + 1)
                    nc.vector.bn_stats(stats2[:, b, :], tx[:, b, :]).then_inc(tx_stats, 1)

                row_max(0)
                for b in range(B):
                    if b + 1 < B:
                        row_max(b + 1)
                    normalise(b)
                    if b >= 2:
                        tx_statistics(b - 2)
                tx_statistics(B - 2)
                tx_statistics(B - 1)
                dve.wait_ge(tx_stats, B)
                for b in range(B):
                    last = nc.vector.bn_aggr(mv2[:, b, :], stats2[:, b, :])
                last.then_inc(mean_in, 1)
                dve.wait_ge(mean_done, 1)
                link(nc.vector.tensor_copy(mean_all[:], bank[0][0:LAT, 0:B]))
                link(nc.vector.tensor_tensor(dev[:], mv2[:, :, 0], mean_all[:], ALU.subtract))
                link(nc.vector.tensor_tensor(dev[:], dev[:], dev[:], ALU.mult))
                nc.vector.tensor_tensor(spread[:], dev[:], mv2[:, :, 1], ALU.add).then_inc(dev_in, 1)
                dve.wait_ge(dev_done, 1)
                nc.vector.tensor_scalar(veps2[:], bank[1][0:LAT, 0:B], EPS, None, ALU.add).then_inc(var2_ready, 1)
                dve.wait_ge(std2_ready, 1)
                newton(rstd2[:], std2[:], veps2[:], nwt2[:])
                nc.vector.scalar_tensor_tensor(out=shift2[:], in0=mean_all[:], scalar=-1.0, in1=rstd2[:],
                                               op0=ALU.mult, op1=ALU.mult).then_inc(shift_made, 1)
                for c in range(4):
                    dve.wait_ge(z_made, 2 * c + 2)
                    chunk = tx[:, 2 * c:2 * c + 2]
                    nc.vector.tensor_tensor(chunk, chunk, gamma_sb[:].unsqueeze(1).to_broadcast([LAT, 2, D]),
                                            ALU.mult).then_inc(zg_made, 1)
                dve.wait_ge(ctx_added, 1)
                for c in range(4):
                    dve.wait_ge(w_done, c + 1)
                    dst = x_sb[:, 2 * c:2 * c + 2].rearrange("p b d -> p (b d)")
                    nc.vector.scalar_tensor_tensor(out=dst, in0=bank[4 + c][:], scalar=outb_sb[:], in1=dst,
                                                   op0=ALU.add, op1=ALU.add).then_inc(x_added, 1)

        @block.tensor
        def _(pe):
            pe.wait_ge(ident_made, 2)
            for b in range(B):
                pe.wait_ge(normed, b + 1)
                for blk in range(KB):
                    col = (b % 2) * D + blk * P
                    last = nc.tensor.transpose(bank[b // 2][:, col:col + P], h_sb[:, b, blk * P:(blk + 1) * P],
                                               ident[:])
                if b % 2:
                    last.then_inc(q_turned, 1)

            def convolve(h, slot, toep_wait, free):
                pe.wait_ge(kv_made, h + 1)
                pe.wait_ge(toep_in[slot], toep_wait)
                if free is not None:
                    pe.wait_ge(prod_made, free)
                y0, y1 = bank[4 + 2 * slot][:], bank[5 + 2 * slot][:]
                near, far = toep[slot][:, 0:P], toep[slot][:, P:2 * P]
                nc.tensor.matmul(y0, near, kv[slot][:, 0], start=True, stop=True)
                nc.tensor.matmul(y1, near, kv[slot][:, 1], start=True, stop=False)
                nc.tensor.matmul(y1, far, kv[slot][:, 0], start=False, stop=True).then_inc(conv_done, 1)

            convolve(0, 0, 16, None)
            convolve(1, 1, 16, None)
            with pe.Fori(1, HEADS // 2) as i:
                for slot in range(2):
                    convolve(2 * i + slot, slot, 16 * (i + 1), 2 * i + slot - 1)
            pe.wait_ge(head_done, HEADS)
            pe.wait_ge(q_copied, 4)
            for b in range(B):
                for blk in range(KB):
                    col = (b % 2) * D + blk * P
                    last = nc.tensor.transpose(bank[b // 2][:, col:col + P], oT[:, blk, b, :], ident[:])
                if b % 2:
                    last.then_inc(o_turned, 1)

            def three_passes(out, w, xs, start, stop):
                (wh, wl), (xh, xl) = w, xs
                nc.tensor.matmul(out, wh, xh, start=start, stop=False)
                nc.tensor.matmul(out, wh, xl, start=False, stop=False)
                return nc.tensor.matmul(out, wl, xh, start=False, stop=stop)

            for n in range(2):
                f = ffns[n]
                ne = (E0, E1)[n]
                pe.wait_ge(x_added, 4 if n == 0 else 12)
                for c in range(4):
                    half, k = c // 2, c % 2
                    for m in range(4):
                        b = 4 * half + m
                        pe.wait_ge(normed, (8 if n == 0 else 24) + b + 1)
                        last = nc.tensor.transpose(bank[c][:, m * P:(m + 1) * P], h_sb[:, b, k * P:(k + 1) * P],
                                                   ident[:])
                    last.then_inc(hT_turned, 1)
                pe.wait_ge(hT_lo_made, 4 * n + 4)
                pe.wait_ge(rw_split, n + 1)
                for b in range(B):
                    toks = slice(b * P, (b + 1) * P)
                    for k in range(KB):
                        last = three_passes(bank[0][:, b * ne:(b + 1) * ne],
                                            (hT_hi[:, k, toks], hT_lo[:, k, toks]),
                                            (rw_hi[n][:, k], rw_lo[n][:, k]), k == 0, k == KB - 1)
                last.then_inc(logits_done, 1)

                def up(q, j, free, w_wait):
                    slot, uslot, half = j % 2, j // 2, j % 2
                    if half == 0:
                        pe.wait_ge(f.w_split, w_wait)
                    if free is not None:
                        pe.wait_ge(f.hid_made, free)
                    cols = slice(half * HALF, (half + 1) * HALF)
                    for m, done in enumerate((f.g_done, f.u_done)):
                        for k in range(KB):
                            wc = slice((m * KB + k) * P, (m * KB + k + 1) * P)
                            last = three_passes(bank[4 + 2 * slot + m][:], (w_hi[uslot][:, wc], w_lo[uslot][:, wc]),
                                                (hT_hi[:, k, cols], hT_lo[:, k, cols]), k == 0, k == KB - 1)
                        last.then_inc(done, 1)

                def down(q, j, w_wait, stop=False):
                    slot, uslot, half = j % 2, j // 2, j % 2
                    if half == 0:
                        pe.wait_ge(f.w_split, w_wait)
                    pe.wait_ge(f.hid_split, q + 1)
                    for k in range(KB):
                        wc = slice(2 * D + k * P, 2 * D + (k + 1) * P)
                        last = three_passes(bank[2 * k + half][:], (w_hi[uslot][:, wc], w_lo[uslot][:, wc]),
                                            (hid_hi[slot][:], hid_lo[slot][:]), False, stop)
                    last.then_inc(f.hid_free, 1)

                up(0, 0, None, 1)
                up(1, 1, None, 1)
                pe.wait_ge(gates_made, n + 1)
                for c in range(2):
                    for m in range(4):
                        last = nc.tensor.transpose(bank[1 + c][0:ne, m * P:(m + 1) * P], gates[n][:, 4 * c + m, :],
                                                   ident[:])
                    last.then_inc(gates_turned, 1)
                pe.wait_ge(cT_copied, 2 * n + 2)
                pe.wait_ge(dve_consts, 1)
                for c in range(4):
                    last = nc.tensor.matmul(bank[c][:], zeros[:], hT_hi[:, 0, 0:HALF], start=True, stop=False)
                last.then_inc(f.hid_free, 2)

                with pe.Fori(0, NPAIR[n] - 1) as i:
                    for j in range(4):
                        q, ahead = 4 * i + j, 4 * i + j + 2
                        up(ahead, (j + 2) % 4, q + 1, 4 * i + j + 3)
                        down(q, j, 4 * i + j + 2)
                q = 4 * (NPAIR[n] - 1)
                for j in range(2):
                    up(q + j + 2, j + 2, q + j + 1, q + j + 3)
                    down(q + j, j, q + j + 2)
                down(q + 2, 2, q + 4, True)
                down(q + 3, 3, q + 4, True)
                pe.wait_ge(f.hid_free, 4 * NPAIR[n] + 2)
                pe.sem_inc(y_done, 1)
                pe.wait_ge(yT_copied, 4 * n + 4)
                for b in range(B):
                    for k in range(KB):
                        col = (b % 2) * D + k * P
                        last = nc.tensor.transpose(bank[4 + b // 2][:, col:col + P], yT[:, k, b * P:(b + 1) * P],
                                                   ident[:])
                    if b % 2:
                        last.then_inc(y_turned, 1)
                if n == 1:
                    continue

                pe.wait_ge(par_in, 160)
                pe.wait_ge(ctx_in, 16)
                for c in range(4):
                    nc.tensor.matmul(bank[c][0:LAT, :], theta_sb[:],
                                     ctx_sb[:, 2 * c:2 * c + 2].rearrange("p b t -> p (b t)"), start=True, stop=True)\
                        .then_inc(th_done, 1)
                for c in range(4):
                    pe.wait_ge(normed, 16 + 2 * c + 2)
                    nc.tensor.matmul(bank[4 + c][0:LAT, :], phi_sb[:],
                                     h_sb[:, 2 * c:2 * c + 2].rearrange("p b t -> p (b t)"), start=True, stop=True)\
                        .then_inc(ph_done, 1)
                pe.wait_ge(th_copied, 4)
                for b in range(B):
                    for k in range(KB):
                        col = ((b % 4) * KB + k) * LAT
                        last = nc.tensor.matmul(bank[b // 4][:, col:col + LAT], h_sb[:, b, k * P:(k + 1) * P],
                                                gw_sb[:], start=True, stop=True)
                    if b % 4 == 3:
                        last.then_inc(gx_done, 1)
                pe.wait_ge(ph_copied, 4)

                def scores(b):
                    if b >= 2:
                        pe.wait_ge(exp_made, b - 1)
                    for t in range(KB):
                        last = nc.tensor.matmul(bank[4 + b % 2][:, t * D:(t + 1) * D], thT[:, b, t * P:(t + 1) * P],
                                                phT[:, b, :], start=True, stop=True)
                    last.then_inc(sc_done, 1)

                def turn_probs(b):
                    pe.wait_ge(prob_made, b + 1)
                    if b >= 2:
                        pe.wait_ge(pT_copied, b - 1)
                    for k in range(KB):
                        for t in range(KB):
                            col = k * D + t * P
                            last = nc.tensor.transpose(bank[6 + b % 2][:, col:col + P],
                                                       prob[b % 2][:, t, k * P:(k + 1) * P], ident[:])
                    last.then_inc(pT_turned, 1)

                def weigh(b):
                    pe.wait_ge(pT_copied, b + 1)
                    if b == 0:
                        pe.wait_ge(gx_copied, 2)
                    if b >= 2:
                        pe.wait_ge(tx_copied, b - 1)
                    for k in range(KB):
                        last = nc.tensor.matmul(bank[2 + b % 2][0:LAT, 0:D], gx[:, b, k, :], probT[b % 2][:, k, :],
                                                start=(k == 0), stop=(k == KB - 1))
                    last.then_inc(tx_done, 1)

                scores(0)
                for b in range(B):
                    if b + 1 < B:
                        scores(b + 1)
                    turn_probs(b)
                    if b >= 1:
                        weigh(b - 1)
                weigh(B - 1)
                pe.wait_ge(consts_made, 1)
                pe.wait_ge(mean_in, 1)
                nc.tensor.matmul(bank[0][0:LAT, 0:B], avg[:], mv2[:, :, 0], start=True, stop=True)\
                    .then_inc(mean_done, 1)
                pe.wait_ge(dev_in, 1)
                nc.tensor.matmul(bank[1][0:LAT, 0:B], avg[:], spread[:], start=True, stop=True).then_inc(dev_done, 1)
                for c in range(4):
                    pe.wait_ge(relu_made, c + 1)
                    nc.tensor.matmul(bank[4 + c][:], outw_sb[:], tx[:, 2 * c:2 * c + 2].rearrange("p b t -> p (b t)"),
                                     start=True, stop=True).then_inc(w_done, 1)


def kernel(x, ctx_2048, L0_xattn_ssm_kernel, L0_xattn_D, L0_ffn_Wr, L0_ffn_Wg, L0_ffn_Wu, L0_ffn_Wd,
           L1_xattn_theta_w, L1_xattn_theta_b, L1_xattn_phi_w, L1_xattn_phi_b, L1_xattn_g_w, L1_xattn_g_b,
           L1_xattn_ln_gamma, L1_xattn_ln_beta, L1_xattn_out_w, L1_xattn_out_b, L1_ffn_gate_w, L1_ffn_w11,
           L1_ffn_w33, L1_ffn_w22, L1_ffn_sw1, L1_ffn_sw2, L1_ffn_sw3):
    import numpy as np
    import concourse.bacc as bacc
    from concourse.bass_utils import run_bass_kernel_spmd

    def arr(a):
        return np.ascontiguousarray(np.asarray(a))

    def by_hidden(w):
        return w.reshape(-1, KB, P, P).transpose(0, 2, 1, 3).reshape(-1, P, KB * P)

    def halves(w):
        return w.reshape(-1, D, KB, P).transpose(0, 2, 1, 3).reshape(-1, D, P)

    wg, wu, wd = (np.asarray(a) for a in (L0_ffn_Wg, L0_ffn_Wu, L0_ffn_Wd))
    unit0 = np.concatenate([by_hidden(halves(wg)), by_hidden(halves(wu)), wd.reshape(UNITS0, P, D)], axis=2)
    w1, w3, w2, s1, s2, s3 = (np.asarray(a) for a in (L1_ffn_w11, L1_ffn_w33, L1_ffn_w22, L1_ffn_sw1, L1_ffn_sw2,
                                                      L1_ffn_sw3))
    gate1 = np.concatenate([by_hidden(w1.transpose(0, 2, 1)), by_hidden(halves(s1.T[None]))])
    up1 = np.concatenate([by_hidden(w3.transpose(0, 2, 1)), by_hidden(halves(s3.T[None]))])
    down1 = np.concatenate([w2.transpose(0, 2, 1), s2.T.reshape(2, P, D)])
    unit1 = np.concatenate([gate1, up1, down1], axis=2)
    ctx = np.asarray(ctx_2048)
    ctxr = ctx.transpose(2, 0, 1).reshape(KB, P, B, P)[:, ::-1]
    filt = np.pad(np.asarray(L0_xattn_ssm_kernel), ((0, 0), (P - 1, KPAD - (P - 1) - D)))
    arrays = {
        "x": arr(x), "ctx": arr(ctx), "ctxr": arr(ctxr), "filt": arr(filt),
        "skip": arr(np.asarray(L0_xattn_D).reshape(HEADS, 1)), "wr": arr(L0_ffn_Wr), "unit0": arr(unit0),
        "theta": arr(np.asarray(L1_xattn_theta_w).T), "theta_b": arr(np.asarray(L1_xattn_theta_b).reshape(LAT, 1)),
        "phi": arr(np.asarray(L1_xattn_phi_w).T), "phi_b": arr(np.asarray(L1_xattn_phi_b).reshape(LAT, 1)),
        "g": arr(np.asarray(L1_xattn_g_w).T), "g_b": arr(L1_xattn_g_b),
        "gamma": arr(L1_xattn_ln_gamma), "beta": arr(L1_xattn_ln_beta),
        "outw": arr(np.asarray(L1_xattn_out_w).T), "outb": arr(np.asarray(L1_xattn_out_b).reshape(P, 1)),
        "gate": arr(np.asarray(L1_ffn_gate_w).T), "unit1": arr(unit1),
    }
    nc = bacc.Bacc("TRN2", target_bir_lowering=False, num_devices=1)
    f32 = mybir.dt.float32
    ins = [nc.dram_tensor(f"in_{k}", a.shape, mybir.dt.from_np(a.dtype), kind="ExternalInput").ap()
           for k, a in arrays.items()]
    out = nc.dram_tensor("out", (B, S, D), f32, kind="ExternalOutput").ap()
    scratch = [nc.dram_tensor(name, shape, f32, kind="Internal").ap() for name, shape in (
        ("filt_s", (HEADS, KPAD)), ("c0_s", (UNITS0, TOK)), ("c1_s", (UNITS1, TOK)))]
    build(nc, *ins, out, *scratch)
    r = run_bass_kernel_spmd(nc, [{f"in_{k}": a for k, a in arrays.items()}], core_ids=[0])
    return r.results[0]["out"]
```

```python
from contextlib import ExitStack

import concourse.bass as bass
from concourse import mybir

P = 128
B, S, D = 8, 128, 256
TOK = B * S
KB = D // P
HALF = TOK // 2
HEADS, HD = 16, 8
PAIRS = HD * HD
KPAD = P - 1 + D + 1
UP_W = 2 * D
LAT = 64
E0, UNITS0 = 8, 16
E1, UNITS1 = 32, 34
GROUPS, GSIZE, TOPG, TOPK1 = 8, 4, 4, 6
ROUTE_SCALE = 2.5
SWIGLU_LIMIT = 7.0
EPS = 1e-5
CHUNK, TILES = 256, 2
TOPK = (2, TOPK1)
EXPERTS = (E0, E1)
UPE = (2, 1)
MAXC = tuple(-(-(TOK * k // CHUNK + e) * u // 4) * 4 // u for k, e, u in zip(TOPK, EXPERTS, UPE))
BASEC = (0, MAXC[0])
ROW = D + 4
NOWHERE = 1 << 24
LOWEST = -3.0e38
TAKEN = 9.0
PAD = -5.0


def build(nc, x_d, ctx_d, ctxr_d, filt_d, skip_d, wr_d, up0_d, down0_d, theta_d, theta_b_d, phi_d, phi_b_d, g_d, g_b_d,
          gamma_d, beta_d, outw_d, outb_d, gate_d, up1_d, down1_d, out_d, filt_s, rows_s, y0_s, y1_s):
    f32, f32r, i32 = mybir.dt.float32, mybir.dt.float32r, mybir.dt.int32
    ACT = mybir.ActivationFunctionType
    ALU = mybir.AluOpType
    AX = mybir.AxisListType

    def view(t, offset, dims):
        base = t[:]
        return bass.AP(base.tensor, base.offset + offset, [list(base.ap[0])] + [list(d) for d in dims])

    with ExitStack() as stack:
        def sb(name, shape, dt=f32):
            return stack.enter_context(nc.sbuf_tensor(name, shape, dt))

        def sem(name):
            return stack.enter_context(nc.semaphore(name))

        x_sb = sb("x_sb", [P, B, D])
        h_sb = sb("h_sb", [P, B, D])
        ctx_sb = sb("ctx_sb", [P, B, D])
        ident = sb("ident", [P, P])
        filt_row = sb("filt_row", [HEADS, KPAD])
        skip_col = sb("skip_col", [HEADS, 1])
        stats = sb("stats", [P, B, 6])
        mv = sb("mv", [P, B, 2])
        veps = sb("veps", [P, B])
        std = sb("std", [P, B])
        rstd = sb("rstd", [P, B])
        nwt = sb("nwt", [P, B])
        hT_hi = sb("hT_hi", [P, KB, TOK], f32r)
        hT_lo = sb("hT_lo", [P, KB, TOK], f32r)
        wr_sb = sb("wr_sb", [P, KB, E0])
        gate_sb = sb("gate_sb", [P, KB, E1])
        rw = [sb(f"rw{i}", [P, KB, 2 * e], f32r) for i, e in enumerate(EXPERTS)]
        up_raw = [sb(f"up_raw{i}", [P, UP_W]) for i in range(4)]
        down_raw = [sb(f"down_raw{i}", [P, D]) for i in range(4)]
        w_hi = [sb(f"w_hi{i}", [P, UP_W], f32r) for i in range(2)]
        w_lo = [sb(f"w_lo{i}", [P, UP_W], f32r) for i in range(2)]
        yT = sb("yT", [P, KB, TOK])
        oT = yT[:].rearrange("p k (b c) -> p k b c", b=B)
        logit = sb("logit", [P, B, 2 * E0])
        top8 = sb("top8", [P, B, 8])
        ex = sb("ex", [P, B, E0])
        marked = sb("marked", [P, B, 2 * E0])
        score = sb("score", [P, B, E1 + 8])
        gmax = sb("gmax", [P, B, 2 * GROUPS])
        gmask = sb("gmask", [P, B, GROUPS])
        gneg = sb("gneg", [P, B, GROUPS])
        allowed = sb("allowed", [P, B, E1 + 8])
        marked1 = sb("marked1", [P, B, E1 + 8])
        gates = [sb("gates0", [P, B, E0]), sb("gates1", [P, B, E1])]
        gsum = sb("gsum", [P, B])
        grec = sb("grec", [P, B])
        lgT = sb("lgT", [2 * E1, TOK])
        mask = sb("mask", [P, B, E1])
        rank = [sb(f"rank{i}", [P, B, 16 + E1]) for i in range(2)]
        nth = sb("nth", [P, B, E1])
        cnt = sb("cnt", [P, B, E1])
        cum = [sb(f"cum{i}", [P, 4 + B, E1]) for i in range(2)]
        chunks = sb("chunks", [P, E1])
        cend = sb("cend", [P, E1])
        csum = sb("csum", [P, MAXC[1] + 2, E1])
        past = csum[0:1]
        sbase = sb("sbase", [P, E1])
        upto = sb("upto", [P, E1, E1])
        before = sb("before", [P, P])
        ones = sb("ones", [P, P])
        slot_f = sb("slot_f", [P, B, E1])
        pick = [sb(f"pick{i}", [P, B, E1]) for i in range(2)]
        slot_k = sb("slot_k", [P, B])
        slot_i = sb("slot_i", [P, TOPK1, B], i32)
        chunk_no = sb("chunk_no", [1, MAXC[1] + 2])
        expert_f = sb("expert_f", [1, MAXC[1] + 2])
        experts_i = [sb(f"experts_i{i}", [1, MAXC[1]], i32) for i in range(2)]
        more_f = sb("more_f", [1, 1])
        more_i = [sb(f"more_i{i}", [1, 1], i32) for i in range(2)]
        staged = sb("staged", [P, B, TOPK1, ROW])
        empty = sb("empty", [P, ROW])
        y_in = [h_sb[:], yT[:].rearrange("p k (b c) -> p (k b c)", b=B).rearrange("p (b d) -> p b d", b=B)]
        theta_sb = sb("theta_sb", [P, LAT])
        phi_sb = sb("phi_sb", [P, LAT])
        gw_sb = sb("gw_sb", [P, LAT])
        theta_b = sb("theta_b", [LAT, 1])
        phi_b = sb("phi_b", [LAT, 1])
        g_b = sb("g_b", [P, LAT])
        gamma_sb = sb("gamma_sb", [LAT, D])
        beta_sb = sb("beta_sb", [LAT, D])
        outw_sb = sb("outw_sb", [LAT, P])
        outb_sb = sb("outb_sb", [P, 1])
        nmax = sb("nmax", [P, B, KB])
        psum_row = sb("psum_row", [P, B, KB])
        prec = sb("prec", [P, B, KB])
        tick = sb("tick", [1, 1])
        stats2 = sb("stats2", [LAT, B, 6])
        mv2 = sb("mv2", [LAT, B, 2])
        mean_all = sb("mean_all", [LAT, B])
        dev = sb("dev", [LAT, B])
        spread = sb("spread", [LAT, B])
        veps2 = sb("veps2", [LAT, B])
        std2 = sb("std2", [LAT, B])
        rstd2 = sb("rstd2", [LAT, B])
        nwt2 = sb("nwt2", [LAT, B])
        shift2 = sb("shift2", [LAT, B])
        avg = sb("avg", [LAT, LAT])

        scope = stack.enter_context(ExitStack())

        def scoped(name, shape, dt=f32):
            return scope.enter_context(nc.sbuf_tensor(name, shape, dt))

        ctxr_sb = scoped("ctxr_sb", [P, KB, B, P])
        toep = [scoped(f"toep{i}", [P, D]) for i in range(2)]
        kv = [scoped(f"kv{i}", [P, KB, B * PAIRS]) for i in range(2)]
        qT = scoped("qT", [P, KB, HEADS, B * HD])
        prod = [scoped(f"prod{i}", [P, KB, B * PAIRS]) for i in range(2)]
        scope.close()
        thT = scoped("thT", [LAT, B, D])
        phT = scoped("phT", [LAT, B, D])
        gx = scoped("gx", [P, B, KB, LAT])
        prob = [scoped(f"prob{i}", [P, KB, D]) for i in range(2)]
        probT = [scoped(f"probT{i}", [P, KB, D]) for i in range(2)]
        tx = scoped("tx", [LAT, B, D])
        scope.close()
        silu_g = [scoped(f"silu_g{i}", [P, HALF]) for i in range(2)]
        hid = [scoped(f"hid{i}", [P, HALF]) for i in range(2)]
        rowbuf = [scoped(f"rowbuf{i}", [P, TILES, ROW]) for i in range(4)]
        meta = [scoped(f"meta{i}", [P, TILES, 2]) for i in range(4)]
        place = [scoped(f"place{i}", [P, TILES], i32) for i in range(4)]
        xT_hi = [scoped(f"xT_hi{i}", [P, KB, TILES * P], f32r) for i in range(2)]
        xT_lo = [scoped(f"xT_lo{i}", [P, KB, TILES * P], f32r) for i in range(2)]
        y_sb = [scoped(f"y_sb{i}", [P, TILES, D]) for i in range(4)]

        bank = [stack.enter_context(nc.psum_tensor(f"bank{i}", [P, 512], f32)) for i in range(8)]

        x_in, filt_in, skip_in, ctx_in, par_in, rw_in = (sem(n) for n in (
            "x_in", "filt_in", "skip_in", "ctx_in", "par_in", "rw_in"))
        ctxr_in = sem("ctxr_in")
        filt_summed, filt_out = sem("filt_summed"), sem("filt_out")
        toep_in = [sem(f"toep_in{i}") for i in range(2)]
        ident_made, consts_made, dve_consts = sem("ident_made"), sem("consts_made"), sem("dve_consts")
        dve_step = sem("dve_step")
        var_ready, std_ready, normed = sem("var_ready"), sem("std_ready"), sem("normed")
        q_turned, q_copied = sem("q_turned"), sem("q_copied")
        kv_made, conv_done, prod_made, head_done = sem("kv_made"), sem("conv_done"), sem("prod_made"), sem("head_done")
        o_turned, x_added = sem("o_turned"), sem("x_added")
        hT_turned, hT_hi_made, hT_lo_made = sem("hT_turned"), sem("hT_hi_made"), sem("hT_lo_made")
        rw_hi_made, rw_split = sem("rw_hi_made"), sem("rw_split")
        lgT_done, lgT_copied, mask_made, ranked = sem("lgT_done"), sem("lgT_copied"), sem("mask_made"), sem("ranked")
        table_made, h_staged, slots_made, rows_sent = (sem(n) for n in (
            "table_made", "h_staged", "slots_made", "rows_sent"))
        rows_init, init_made, ids_made = sem("rows_init"), sem("init_made"), sem("ids_made")
        logits_done, act_gate_in, act_gate_out = sem("logits_done"), sem("act_gate_in"), sem("act_gate_out")
        y_in_done, y_in_used = [sem(f"y_in_done{i}") for i in range(2)], sem("y_in_used")
        s_up_in, s_w_hi, s_w_split, s_g_done, s_u_done, s_silu, s_hid, s_down, yT_copied, y_turned = (sem(n) for n in (
            "s_up_in", "s_w_hi", "s_w_split", "s_g_done", "s_u_done", "s_silu", "s_hid", "s_down", "yT_copied",
            "y_turned"))

        class Ffn:

            def __init__(self, n):
                self.up_in = [sem(f"up_in{n}_{i}") for i in range(4)]
                self.down_in = [sem(f"down_in{n}_{i}") for i in range(4)]
                self.rows_in = [sem(f"rows_in{n}_{i}") for i in range(4)]
                self.sent = [sem(f"sent{n}_{i}") for i in range(4)]
                (self.w_hi_made, self.w_split, self.xT_turned, self.x_hi_made, self.x_split, self.up_done,
                 self.silu_made, self.hid_made, self.down_done, self.y_made, self.ticked) = (
                    sem(f"{name}{n}") for name in (
                        "w_hi_made", "w_split", "xT_turned", "x_hi_made", "x_split", "up_done", "silu_made",
                        "hid_made", "down_done", "y_made", "ticked"))

        ffns = [Ffn(0), Ffn(1)]
        th_done, th_copied, ph_done, ph_copied, gx_done, gx_copied = (sem(n) for n in (
            "th_done", "th_copied", "ph_done", "ph_copied", "gx_done", "gx_copied"))
        sc_done, max_made, exp_made, prob_made, pT_turned, pT_copied, tx_done, tx_copied, tx_stats = (sem(n) for n in (
            "sc_done", "max_made", "exp_made", "prob_made", "pT_turned", "pT_copied", "tx_done", "tx_copied",
            "tx_stats"))
        mean_in, mean_done, dev_in, dev_done, var2_ready, std2_ready, shift_made = (sem(n) for n in (
            "mean_in", "mean_done", "dev_in", "dev_done", "var2_ready", "std2_ready", "shift_made"))
        z_made, zg_made, zb_made, relu_made, w_done, ctx_added = (sem(n) for n in (
            "z_made", "zg_made", "zb_made", "relu_made", "w_done", "ctx_added"))
        out_done = sem("out_done")

        block = stack.enter_context(nc.Block())
        up_d, down_d, y_s = [up0_d, up1_d], [down0_d, down1_d], [y0_s, y1_s]
        MAXT = [MAXC[n] * UPE[n] // 4 for n in range(2)]
        MINT = [EXPERTS[n] * UPE[n] // 4 for n in range(2)]

        def step_slot(i, r, ahead):
            return (r + ahead) % 4, i + (r + ahead) // 4

        def chunk_of(n, i, r, ahead):
            t = r + ahead
            if UPE[n] == 1:
                return 4 * i + t, True, True, t % 4, i + t // 4
            return 2 * i + t // 2, t % 2 == 0, t % 2 == 1, (t // 2) % 2, i + t // 4

        def run_steps(eng, n, step, more):
            peeled = UPE[n]
            for i in range(peeled):
                for r in range(4):
                    step(i, r, i == 0, False)
            with eng.Fori(peeled, more + (MINT[n] - 1)) as i:
                for r in range(4):
                    step(i, r, False, False)
            for r in range(4):
                step(more + (MINT[n] - 1), r, False, True)

        def is_zero(count):
            return isinstance(count, int) and count == 0

        def load_turns(eng, n):
            eng.wait_ge(table_made, n + 1)
            more = eng.value_load(more_i[n][0:1, 0:1], min_val=0, max_val=MAXT[n] - MINT[n])
            return more + MINT[n], more

        X_ATT0, X_FFN0, X_ATT1, X_END = 4, 8, 12, 20

        @block.sync
        def _(sp):
            sp.dma_start(filt_row[:], filt_d).then_inc(filt_in, 16)
            sp.dma_start(skip_col[:], skip_d).then_inc(filt_in, 16)
            sp.dma_start(ctxr_sb[:, 0], ctxr_d[0]).then_inc(ctxr_in, 16)
            sp.dma_start(ctxr_sb[:, 1], ctxr_d[1]).then_inc(ctxr_in, 16)
            sp.wait_ge(filt_summed, 1)
            sp.dma_start(filt_s, filt_row[:]).then_inc(filt_out, 16)
            sp.wait_ge(filt_out, 16)

            def load_toeplitz(h, slot):
                src = bass.AP(filt_s.tensor, filt_s.offset + h * KPAD, [[1, P], [1, D]])
                sp.dma_start(toep[slot][:], src).then_inc(toep_in[slot], 16)

            load_toeplitz(0, 0)
            load_toeplitz(1, 1)

            sp.dma_start(ctx_sb[:], ctx_d.rearrange("b s d -> s b d")).then_inc(ctx_in, 16)

            rows_v = rows_s.rearrange("(c t p) w -> p (c t) w", t=TILES, p=P)

            def empty_rows(chunk, count):
                sp.dma_start(rows_v[:, bass.ds(chunk * TILES, count * TILES)],
                             empty[:].unsqueeze(1).to_broadcast([P, count * TILES, ROW])).then_inc(rows_init, 16)

            INIT = MAXC[0] // (HEADS // 2)
            sp.wait_ge(init_made, 1)
            empty_rows(0, INIT)
            with sp.Fori(1, HEADS // 2) as i:
                for slot in range(2):
                    sp.wait_ge(conv_done, 2 * i + slot - 1)
                    load_toeplitz(2 * i + slot, slot)
                empty_rows(i * INIT, INIT)

            for n in range(2):
                f, upe = ffns[n], UPE[n]
                if n == 1:
                    for u in range(2):
                        sp.dma_start(up_raw[u][:], up1_d[E1 + u]).then_inc(s_up_in, 16)
                        sp.dma_start(down_raw[u][:], down1_d[E1 + u]).then_inc(s_up_in, 16)
                    for c in range(0, MAXC[1], 8):
                        empty_rows(BASEC[1] + c, 8)
                turns, more = load_turns(sp, n)
                sp.wait_ge(rows_sent, 16 * B * (TOPK[0] + n * TOPK[1]))
                if n == 1:
                    sp.wait_ge(s_w_split, 2)
                    sp.wait_ge(s_down, 4)
                rows = rows_s.rearrange("(c t p) w -> c p t w", t=TILES, p=P)
                def units(i, r):
                    c = chunk_of(n, i, r, 0)[0]
                    both = sp.value_load(experts_i[n][0:1, bass.ds(c, 1)], min_val=0, max_val=EXPERTS[n] ** 2 - 1)
                    return (both % EXPERTS[n]) * upe, (both // EXPERTS[n]) * upe

                def of_unit(w, u):
                    return w[n][bass.ds(u, 1)].squeeze(0)

                def rows_of(i, r, ahead):
                    return rows[bass.ds(BASEC[n] + chunk_of(n, i, r, ahead)[0], 1)].squeeze(0)

                def load(dst, src, done):
                    sp.dma_start(dst[:], src).then_inc(done, 16)

                for r in range(2):
                    if r < 2 // upe:
                        load(rowbuf[r], rows_of(0, r * upe, 0), f.rows_in[r])
                    load(up_raw[r], of_unit(up_d, units(0, r)[0] + r % upe), f.up_in[r])

                held = [None]

                def step(i, r, first, last):
                    s = 4 * i + r
                    if r % upe == 0:
                        held[0] = units(i, r)
                    here, later = held[0]
                    down_src = of_unit(down_d, here + r % upe)
                    if not (last and r >= 2):
                        c, first_unit, _, cslot, _ = chunk_of(n, i, r, 2)
                        slot, _ = step_slot(i, r, 2)
                        up_src, rows_src = of_unit(up_d, later + r % upe), rows_of(i, r, 2)
                        if not first:
                            sp.wait_ge(f.w_split, s - 1)
                            sp.wait_ge(f.x_split, c - (3 if upe == 1 else 1))
                        elif r >= 2:
                            sp.wait_ge(f.w_split, r - 1)
                            if upe == 1:
                                sp.wait_ge(f.x_split, r - 1)
                            else:
                                sp.wait_ge(f.x_split, 1)
                        if first_unit:
                            load(rowbuf[cslot], rows_src, f.rows_in[cslot])
                        load(up_raw[slot], up_src, f.up_in[slot])
                    if not first:
                        sp.wait_ge(f.down_done, s - 3)
                    load(down_raw[r], down_src, f.down_in[r])

                run_steps(sp, n, step, more)
                for slot in range(4 // upe):
                    sp.wait_ge(f.sent[slot], 32 * turns)
                base = n * TOPK[0]
                for k in range(TOPK[n]):
                    if k >= 2:
                        sp.wait_ge(y_in_used, base + k - 1)
                    sp.dma_start(y_in[k % 2], y_s[n][k * TOK:(k + 1) * TOK].rearrange("(b p) d -> p b d", p=P))\
                        .then_inc(y_in_done[k % 2], 16)
            for q in range(4):
                sp.wait_ge(x_added, X_END - 3 + q)
                sp.dma_start(out_d.rearrange("b s d -> s b d")[:, 2 * q:2 * q + 2], x_sb[:, 2 * q:2 * q + 2])\
                    .then_inc(out_done, 16)
            sp.wait_ge(out_done, 64)

        @block.gpsimd
        def _(pool):
            nc.gpsimd.memset(ident[:], 0.0).then_inc(ident_made, 1)
            pool.wait_ge(ident_made, 1)
            nc.gpsimd.affine_select(out=ident[:], in_=ident[:], compare_op=ALU.not_equal, fill=1.0, base=0,
                                    pattern=[[-1, P]], channel_multiplier=1).then_inc(ident_made, 1)
            nc.gpsimd.memset(empty[:], 0.0).then_inc(ids_made, 1)
            pool.wait_ge(ids_made, 1)
            nc.gpsimd.memset(empty[:, D + 1:D + 2].bitcast(i32), NOWHERE).then_inc(init_made, 1)
            pool.wait_ge(ctxr_in, 32)

            def products(h, slot):
                for blk in range(KB):
                    rows = ctxr_sb[:, blk].rearrange("p b (h j) -> p b h j", j=HD)[:, :, bass.ds(h, 1), :]\
                        .rearrange("p b o j -> p b (o j)")
                    k = rows.unsqueeze(3).to_broadcast([P, B, HD, HD])
                    v = rows.unsqueeze(2).to_broadcast([P, B, HD, HD])
                    last = nc.gpsimd.tensor_tensor(
                        kv[slot][:, blk].rearrange("p (b i j) -> p b i j", i=HD, j=HD), k, v, ALU.mult)
                last.then_inc(kv_made, 1)

            products(0, 0)
            products(1, 1)
            with pool.Fori(1, HEADS // 2) as i:
                for slot in range(2):
                    pool.wait_ge(conv_done, 2 * i + slot - 1)
                    products(2 * i + slot, slot)
            nc.gpsimd.memset(ones[:], 1.0).then_inc(ids_made, 1)
            nc.gpsimd.memset(upto[:], 1.0).then_inc(ids_made, 1)
            pool.wait_ge(ids_made, 3)
            nc.gpsimd.affine_select(out=before[:], in_=ones[:], compare_op=ALU.is_gt, fill=0.0, base=0,
                                    pattern=[[1, P]], channel_multiplier=-1)
            nc.gpsimd.affine_select(out=upto[:], in_=upto[:], compare_op=ALU.is_ge, fill=0.0, base=0,
                                    pattern=[[1, E1], [-1, E1]], channel_multiplier=0)
            nc.gpsimd.iota(chunk_no[:], pattern=[[1, MAXC[1] + 2]], base=0, channel_multiplier=0,
                           allow_small_or_imprecise_dtypes=True)
            nc.gpsimd.iota(staged[:, :, :, D + 1].bitcast(i32), pattern=[[P, B], [TOK, TOPK1]], base=0,
                           channel_multiplier=1)
            nc.gpsimd.memset(staged[:, :, :, D + 2:ROW], 0.0)
            nc.gpsimd.memset(avg[:], 1.0 / LAT).then_inc(consts_made, 1)

            for n in range(2):
                f = ffns[n]
                pool.wait_ge(rows_init, 16 * (HEADS // 2 + n * MAXC[1] // 8))
                for k in range(TOPK[n]):
                    pool.wait_ge(slots_made, n * TOPK[0] + k + 1)
                    for b in range(B):
                        if k == 0:
                            pool.wait_ge(h_staged, n * B + b + 1)
                        nc.gpsimd.indirect_dma_start(
                            out=rows_s, out_offset=bass.IndirectOffsetOnAxis(ap=slot_i[:, k, b:b + 1], axis=0),
                            in_=staged[:, b, k, :], in_offset=None).then_inc(rows_sent, 16)
                turns, more = load_turns(pool, n)

                def send(i, r, ahead):
                    c, _, last_unit, slot, _ = chunk_of(n, i, r, ahead)
                    if not last_unit:
                        return
                    if not is_zero(c):
                        pool.wait_ge(f.ticked, c)
                    pool.wait_ge(f.y_made, c + 1)
                    nc.gpsimd.tensor_tensor(tick[:], ident[0:1, 0:1], ident[0:1, 0:1], ALU.mult).then_inc(f.ticked, 1)
                    for t in range(TILES):
                        nc.gpsimd.indirect_dma_start(
                            out=y_s[n], out_offset=bass.IndirectOffsetOnAxis(ap=place[slot][:, t:t + 1], axis=0),
                            in_=y_sb[slot][:, t, :], in_offset=None, bounds_check=TOPK[n] * TOK - 1,
                            oob_is_err=False).then_inc(f.sent[slot], 16)

                def step(i, r, first, last):
                    if not (first and r == 0):
                        send(i, r, -1)

                run_steps(pool, n, step, more)
                send(turns, 0, -1)
                if n == 0:
                    pool.wait_ge(normed, 3 * B)
                    pool.wait_ge(ctx_in, 16)
                    nc.gpsimd.tensor_tensor(x_sb[:], x_sb[:], ctx_sb[:], ALU.add).then_inc(ctx_added, 1)
                    for c in range(4):
                        pool.wait_ge(zg_made, c + 1)
                        chunk = tx[:, 2 * c:2 * c + 2]
                        nc.gpsimd.tensor_tensor(chunk, chunk, beta_sb[:].unsqueeze(1).to_broadcast([LAT, 2, D]),
                                                ALU.add).then_inc(zb_made, 1)

        @block.scalar
        def _(act):
            act.dma_start(x_sb[:], x_d.rearrange("b s d -> s b d")).then_inc(x_in, 16)
            act.dma_start(wr_sb[:], wr_d.rearrange("(k p) e -> p k e", p=P)).then_inc(rw_in, 16)
            act.dma_start(gate_sb[:], gate_d.rearrange("(k p) e -> p k e", p=P)).then_inc(rw_in, 16)
            for dst, src in ((theta_sb[:], theta_d), (phi_sb[:], phi_d), (gw_sb[:], g_d), (theta_b[:], theta_b_d),
                             (phi_b[:], phi_b_d), (g_b[:], g_b_d.partition_broadcast(P)),
                             (gamma_sb[:], gamma_d), (beta_sb[:], beta_d), (outw_sb[:], outw_d),
                             (outb_sb[:], outb_d)):
                act.dma_start(dst, src).then_inc(par_in, 16)

            def sqrt_of_var(k):
                act.wait_ge(var_ready, k + 1)
                nc.scalar.activation(std[:], veps[:], ACT.Sqrt).then_inc(std_ready, 1)

            sqrt_of_var(0)
            act.wait_ge(rw_in, 32)
            for n, w in enumerate((wr_sb, gate_sb)):
                nc.scalar.activation(rw[n][:, :, 0:EXPERTS[n]], w[:], ACT.Copy).then_inc(rw_hi_made, 1)
            for c in range(4):
                act.wait_ge(q_turned, c + 1)
                for blk in range(KB):
                    src = bank[c][:].rearrange("p (b k h i) -> p k b h i", b=2, k=KB, i=HD)[:, blk]
                    dst = qT[:, blk].rearrange("p h (b i) -> p b h i", i=HD)[:, 2 * c:2 * c + 2]
                    last = nc.scalar.activation(dst, src, ACT.Copy)
                last.then_inc(q_copied, 1)

            for n in range(2):
                f, ne = ffns[n], EXPERTS[n]
                sqrt_of_var(1 if n == 0 else 3)
                for c in range(4):
                    act.wait_ge(hT_turned, 4 * n + c + 1)
                    half, k = c // 2, c % 2
                    nc.scalar.activation(hT_hi[:, k, half * HALF:(half + 1) * HALF], bank[c][:], ACT.Copy)\
                        .then_inc(hT_hi_made, 1)
                for c in range(2):
                    act.wait_ge(lgT_done, 2 * n + c + 1)
                    nc.scalar.activation(lgT[0:2 * ne, c * HALF:(c + 1) * HALF], bank[4 + c][0:2 * ne, :], ACT.Copy)\
                        .then_inc(lgT_copied, 1)
                if n == 0:
                    act.wait_ge(act_gate_in, 1)
                    nc.scalar.activation(ex[:], ex[:], ACT.Exp).then_inc(act_gate_out, 1)
                else:
                    act.wait_ge(act_gate_in, 2)
                    nc.scalar.activation(score[:, :, 0:E1], score[:, :, 0:E1], ACT.Sigmoid).then_inc(act_gate_out, 1)
                for b in range(B):
                    nc.scalar.activation(staged[:, b, 0:TOPK[n], 0:D],
                                         h_sb[:, b].unsqueeze(1).to_broadcast([P, TOPK[n], D]), ACT.Copy)\
                        .then_inc(h_staged, 1)
                if n == 1:
                    act.wait_ge(s_up_in, 64)
                    for u in range(2):
                        nc.scalar.activation(w_hi[u][:], up_raw[u][:], ACT.Copy).then_inc(s_w_hi, 1)
                    for q in range(4):
                        act.wait_ge(s_g_done, q + 1)
                        nc.scalar.activation(silu_g[q % 2][:], bank[4][:], ACT.Silu).then_inc(s_silu, 1)
                    for c in range(4):
                        act.wait_ge(s_down, 4)
                        half, k = c % 2, c // 2
                        nc.scalar.activation(yT[:, k, half * HALF:(half + 1) * HALF], bank[c][:], ACT.Copy)\
                            .then_inc(yT_copied, 1)
                turns, more = load_turns(act, n)

                def high_parts(i, r, ahead):
                    c, first_unit, _, cslot, _ = chunk_of(n, i, r, ahead)
                    if first_unit:
                        act.wait_ge(f.xT_turned, c + 1)
                        par = cslot % 2
                        nc.scalar.activation(xT_hi[par][:].rearrange("p k c -> p (k c)"), bank[2 + par][:], ACT.Copy)\
                            .then_inc(f.x_hi_made, 1)
                    slot, filled = step_slot(i, r, ahead)
                    act.wait_ge(f.up_in[slot], 16 * filled + 16)
                    nc.scalar.activation(w_hi[slot % 2][:], up_raw[slot][:], ACT.Copy).then_inc(f.w_hi_made, 1)

                def take_y(i, r, ahead):
                    c, _, last_unit, slot, _ = chunk_of(n, i, r, ahead)
                    if not last_unit:
                        return
                    act.wait_ge(f.down_done, 4 * i + r + ahead + 1)
                    for t in range(TILES):
                        last = nc.scalar.activation(y_sb[slot][:, t], bank[4 + slot % 2][:, t * D:(t + 1) * D],
                                                    ACT.Copy, scale=meta[slot][:, t, 0:1])
                    last.then_inc(f.y_made, 1)

                high_parts(0, 0, 0)
                high_parts(0, 1, 0)

                def step(i, r, first, last):
                    s = 4 * i + r
                    act.wait_ge(f.up_done, s + 1)
                    nc.scalar.activation(silu_g[r % 2][:, 0:TILES * P], bank[r % 2][:, 0:TILES * P], ACT.Silu)\
                        .then_inc(f.silu_made, 1)
                    if not (last and r >= 2):
                        high_parts(i, r, 2)
                    if not (first and r == 0):
                        take_y(i, r, -1)

                run_steps(act, n, step, more)
                take_y(turns, 0, -1)
                if n == 1:
                    continue

                act.wait_ge(par_in, 160)
                for c in range(4):
                    act.wait_ge(th_done, c + 1)
                    nc.scalar.activation(thT[:, 2 * c:2 * c + 2].rearrange("p b t -> p (b t)"), bank[c][0:LAT, :],
                                         ACT.Identity, bias=theta_b[:]).then_inc(th_copied, 1)
                sqrt_of_var(2)
                for c in range(4):
                    act.wait_ge(ph_done, c + 1)
                    nc.scalar.activation(phT[:, 2 * c:2 * c + 2].rearrange("p b t -> p (b t)"), bank[4 + c][0:LAT, :],
                                         ACT.Identity, bias=phi_b[:]).then_inc(ph_copied, 1)

                def exps(b):
                    act.wait_ge(max_made, b + 1)
                    if b >= 2:
                        act.wait_ge(pT_turned, b - 1)
                    for t in range(KB):
                        last = nc.scalar.activation(prob[b % 2][:, t], bank[4 + b % 2][:, t * D:(t + 1) * D], ACT.Exp,
                                                    bias=nmax[:, b, t:t + 1], accum_out=psum_row[:, b, t:t + 1])
                    last.then_inc(exp_made, 1)

                def copy_pT(b):
                    act.wait_ge(pT_turned, b + 1)
                    if b >= 2:
                        act.wait_ge(tx_done, b - 1)
                    nc.scalar.activation(probT[b % 2][:].rearrange("p k t -> p (k t)"), bank[6 + b % 2][:], ACT.Copy)\
                        .then_inc(pT_copied, 1)

                def copy_tx(b):
                    act.wait_ge(tx_done, b + 1)
                    nc.scalar.activation(tx[:, b], bank[2 + b % 2][0:LAT, 0:D], ACT.Copy).then_inc(tx_copied, 1)

                exps(0)
                for b in range(B):
                    if b + 1 < B:
                        exps(b + 1)
                    copy_pT(b)
                    if b >= 1:
                        copy_tx(b - 1)
                copy_tx(B - 1)
                act.wait_ge(var2_ready, 1)
                nc.scalar.activation(std2[:], veps2[:], ACT.Sqrt).then_inc(std2_ready, 1)
                act.wait_ge(shift_made, 1)
                for b in range(B):
                    nc.scalar.activation(tx[:, b], tx[:, b], ACT.Identity, scale=rstd2[:, b:b + 1],
                                         bias=shift2[:, b:b + 1]).then_inc(z_made, 1)
                for c in range(4):
                    act.wait_ge(zb_made, c + 1)
                    nc.scalar.activation(tx[:, 2 * c:2 * c + 2], tx[:, 2 * c:2 * c + 2], ACT.Relu)\
                        .then_inc(relu_made, 1)

        @block.vector
        def _(dve):
            count = [0]

            def link(ins):
                count[0] += 1
                ins.then_inc(dve_step, 1)
                dve.wait_ge(dve_step, count[0])

            def newton(r, s, v, t):
                link(nc.vector.reciprocal(r, s))
                link(nc.vector.tensor_tensor(t, r, r, ALU.mult))
                link(nc.vector.tensor_tensor(t, t, v, ALU.mult))
                link(nc.vector.tensor_scalar(t, t, -0.5, 1.5, ALU.mult, ALU.add))
                link(nc.vector.tensor_tensor(r, r, t, ALU.mult))

            def layer_norm(k):
                for b in range(B):
                    last = nc.vector.bn_stats(stats[:, b, :], x_sb[:, b, :])
                link(last)
                for b in range(B):
                    last = nc.vector.bn_aggr(mv[:, b, :], stats[:, b, :])
                link(last)
                nc.vector.tensor_scalar(veps[:], mv[:, :, 1], EPS, None, ALU.add).then_inc(var_ready, 1)
                dve.wait_ge(std_ready, k + 1)
                newton(rstd[:], std[:], veps[:], nwt[:])
                for b in range(B):
                    nc.vector.tensor_scalar(h_sb[:, b, :], x_sb[:, b, :], mv[:, b, 0:1], rstd[:, b:b + 1],
                                            ALU.subtract, ALU.mult).then_inc(normed, 1)

            def add_banks(turned, wait, first_bank):
                for c in range(4):
                    dve.wait_ge(turned, wait + c)
                    dst = x_sb[:, 2 * c:2 * c + 2].rearrange("p b d -> p (b d)")
                    ins = nc.vector.tensor_tensor(dst, dst, bank[first_bank + c][:], ALU.add)
                    ins.then_inc(x_added, 1)

            dve.wait_ge(filt_in, 32)
            nc.vector.tensor_tensor(filt_row[:, P - 1:P], filt_row[:, P - 1:P], skip_col[:], ALU.add)\
                .then_inc(filt_summed, 1)
            dve.wait_ge(x_in, 16)
            layer_norm(0)
            nc.vector.memset(logit[:, :, E0:2 * E0], LOWEST)
            for i in range(2):
                nc.vector.memset(rank[i][:, :, 0:16], 0.0)
                nc.vector.memset(cum[i][:, 0:4, :], 0.0)
            nc.vector.memset(gmax[:, :, GROUPS:2 * GROUPS], PAD)
            nc.vector.memset(allowed[:, :, E1:E1 + 8], PAD).then_inc(dve_consts, 1)
            for n, w in enumerate((wr_sb, gate_sb)):
                dve.wait_ge(rw_hi_made, n + 1)
                e = EXPERTS[n]
                nc.vector.tensor_tensor(rw[n][:, :, e:2 * e], w[:], rw[n][:, :, 0:e].bitcast(f32), ALU.subtract)\
                    .then_inc(rw_split, 1)

            dve.wait_ge(q_copied, 4)

            def head(h, slot):
                dve.wait_ge(conv_done, h + 1)
                q = qT[:, :, bass.ds(h, 1), :].rearrange("p k o n -> p k (o n)").unsqueeze(3)\
                    .to_broadcast([P, KB, B * HD, HD])
                for blk in range(KB):
                    ins = nc.vector.tensor_tensor(
                        prod[slot][:, blk].rearrange("p (n j) -> p n j", j=HD),
                        bank[4 + 2 * slot + blk][:].rearrange("p (n j) -> p n j", j=HD), q[:, blk], ALU.mult)
                ins.then_inc(prod_made, 1)
                dve.wait_ge(prod_made, h + 1)
                o = oT.rearrange("p k b (h j) -> p (k b) h j", j=HD)[:, :, bass.ds(h, 1), :]\
                    .rearrange("p n o j -> p n (o j)")
                nc.vector.tensor_reduce(o, prod[slot][:].rearrange("p k (b i j) -> p (k b) j i", i=HD, j=HD),
                                        AX.X, ALU.add).then_inc(head_done, 1)

            with dve.Fori(0, HEADS // 2) as i:
                for slot in range(2):
                    head(2 * i + slot, slot)
            add_banks(o_turned, 1, 0)

            for n in range(2):
                f, upe = ffns[n], UPE[n]
                dve.wait_ge(x_added, (X_ATT0, X_ATT1)[n])
                layer_norm(1 if n == 0 else 3)
                for c in range(4):
                    dve.wait_ge(hT_hi_made, 4 * n + c + 1)
                    half, k = c // 2, c % 2
                    cols = slice(half * HALF, (half + 1) * HALF)
                    nc.vector.tensor_tensor(hT_lo[:, k, cols], bank[c][:], hT_hi[:, k, cols].bitcast(f32),
                                            ALU.subtract).then_inc(hT_lo_made, 1)
                g = gates[n]
                if n == 0:
                    dve.wait_ge(logits_done, 1)
                    lg = bank[6][:, 0:2 * B * E0].rearrange("p (b m e) -> p b m e", m=2, e=E0)
                    link(nc.vector.tensor_copy(logit[:, :, 0:E0], lg[:, :, 0]))
                    link(nc.vector.tensor_tensor(logit[:, :, 0:E0], logit[:, :, 0:E0], lg[:, :, 1], ALU.add))
                    for b in range(B):
                        last = nc.vector.max(out=top8[:, b, :], in_=logit[:, b, 0:E0])
                    link(last)
                    nc.vector.tensor_tensor(ex[:], logit[:, :, 0:E0], top8[:, :, 0:1].to_broadcast([P, B, E0]),
                                            ALU.subtract).then_inc(act_gate_in, 1)
                    dve.wait_ge(act_gate_in, 1)
                    link(nc.vector.memset(top8[:, :, 2:8], LOWEST))
                    for b in range(B):
                        last = nc.vector.match_replace(out=marked[:, b, :], in_to_replace=top8[:, b, :],
                                                       in_values=logit[:, b, :], imm_value=-LOWEST)
                    link(last)
                    nc.vector.tensor_scalar(mask[:, :, 0:E0], marked[:, :, 0:E0], -LOWEST, None, ALU.is_equal)\
                        .then_inc(mask_made, 1)
                    dve.wait_ge(act_gate_out, 1)
                    link(nc.vector.scalar_tensor_tensor(out=g[:], in0=marked[:, :, 0:E0], scalar=-LOWEST, in1=ex[:],
                                                        op0=ALU.is_equal, op1=ALU.mult))
                    link(nc.vector.tensor_reduce(gsum[:], g[:], AX.X, ALU.add))
                    link(nc.vector.reciprocal(grec[:], gsum[:]))
                    link(nc.vector.tensor_tensor(g[:], g[:], grec[:].unsqueeze(2).to_broadcast([P, B, E0]), ALU.mult))
                else:
                    dve.wait_ge(logits_done, 2)
                    lg = bank[6][:].rearrange("p (b m e) -> p b m e", m=2, e=E1)
                    link(nc.vector.tensor_copy(score[:, :, 0:E1], lg[:, :, 0]))
                    nc.vector.tensor_tensor(score[:, :, 0:E1], score[:, :, 0:E1], lg[:, :, 1], ALU.add)\
                        .then_inc(act_gate_in, 1)
                    dve.wait_ge(act_gate_out, 2)
                    s4 = score[:, :, 0:E1].rearrange("p b (g i) -> p b g i", i=GSIZE)
                    link(nc.vector.tensor_reduce(gmax[:, :, 0:GROUPS], s4, AX.X, ALU.max))
                    for b in range(B):
                        last = nc.vector.max(out=top8[:, b, :], in_=gmax[:, b, 0:GROUPS])
                    link(last)
                    link(nc.vector.memset(top8[:, :, TOPG:8], PAD))
                    for b in range(B):
                        last = nc.vector.match_replace(out=marked[:, b, :], in_to_replace=top8[:, b, :],
                                                       in_values=gmax[:, b, :], imm_value=TAKEN)
                    link(last)
                    link(nc.vector.tensor_scalar(gmask[:], marked[:, :, 0:GROUPS], TAKEN, None, ALU.is_equal))
                    link(nc.vector.tensor_scalar(gneg[:], gmask[:], -1.0, None, ALU.add))
                    a4 = allowed[:, :, 0:E1].rearrange("p b (g i) -> p b g i", i=GSIZE)
                    for bh in range(2):
                        bs = slice(4 * bh, 4 * bh + 4)
                        last = nc.vector.tensor_tensor(
                            a4[:, bs], s4[:, bs],
                            gmask[:, bs].unsqueeze(3).to_broadcast([P, 4, GROUPS, GSIZE]), ALU.mult)
                    link(last)
                    for bh in range(2):
                        bs = slice(4 * bh, 4 * bh + 4)
                        last = nc.vector.tensor_tensor(
                            a4[:, bs], a4[:, bs],
                            gneg[:, bs].unsqueeze(3).to_broadcast([P, 4, GROUPS, GSIZE]), ALU.add)
                    link(last)
                    for b in range(B):
                        last = nc.vector.max(out=top8[:, b, :], in_=allowed[:, b, 0:E1])
                    link(last)
                    link(nc.vector.memset(top8[:, :, TOPK1:8], PAD))
                    for b in range(B):
                        last = nc.vector.match_replace(out=marked1[:, b, :], in_to_replace=top8[:, b, :],
                                                       in_values=allowed[:, b, :], imm_value=TAKEN)
                    link(last)
                    nc.vector.tensor_scalar(mask[:], marked1[:, :, 0:E1], TAKEN, None, ALU.is_equal)\
                        .then_inc(mask_made, 1)
                    link(nc.vector.scalar_tensor_tensor(out=g[:], in0=marked1[:, :, 0:E1], scalar=TAKEN,
                                                        in1=score[:, :, 0:E1], op0=ALU.is_equal, op1=ALU.mult))
                    link(nc.vector.tensor_reduce(gsum[:], g[:], AX.X, ALU.add))
                    link(nc.vector.reciprocal(grec[:], gsum[:]))
                    link(nc.vector.tensor_tensor(g[:], g[:], grec[:].unsqueeze(2).to_broadcast([P, B, E1]), ALU.mult))
                    link(nc.vector.tensor_scalar(g[:], g[:], ROUTE_SCALE, None, ALU.mult))

                ne = EXPERTS[n]
                dve.wait_ge(mask_made, n + 1)
                m = mask[:, :, 0:ne]
                link(nc.vector.tensor_copy(rank[0][:, :, 16:16 + ne], m))
                at, far = 0, 1
                while far < ne:
                    link(nc.vector.tensor_tensor(rank[1 - at][:, :, 16:16 + ne], rank[at][:, :, 16:16 + ne],
                                                 rank[at][:, :, 16 - far:16 - far + ne], ALU.add))
                    at, far = 1 - at, 2 * far
                link(nc.vector.tensor_tensor(nth[:, :, 0:ne], rank[at][:, :, 16:16 + ne], m, ALU.mult))
                dve.wait_ge(ranked, n + 1)
                dve.wait_ge(consts_made, 1)
                within = bank[7][:, 0:B * ne].rearrange("p (b e) -> p b e", e=ne)
                total = bank[7][:, 256:256 + B * ne].rearrange("p (b e) -> p b e", e=ne)
                nc.vector.tensor_copy(cnt[:, :, 0:ne], total)
                link(nc.vector.tensor_copy(cum[0][:, 4:4 + B, 0:ne], total))
                for at, far in ((0, 1), (1, 2), (0, 4)):
                    link(nc.vector.tensor_tensor(cum[1 - at][:, 4:4 + B, 0:ne], cum[at][:, 4:4 + B, 0:ne],
                                                 cum[at][:, 4 - far:4 - far + B, 0:ne], ALU.add))
                have = cum[1][:, 4 + B - 1, 0:ne]
                ch, ce, base = chunks[:, 0:ne], cend[:, 0:ne], sbase[:, 0:ne]
                link(nc.vector.tensor_scalar(ch, have, float(CHUNK), 1.0, ALU.is_gt, ALU.add))
                for more in range(2, TOK // CHUNK):
                    link(nc.vector.scalar_tensor_tensor(out=ch, in0=have, scalar=float(more * CHUNK), in1=ch,
                                                        op0=ALU.is_gt, op1=ALU.add))
                link(nc.vector.tensor_tensor(csum[:, 0:ne, 0:ne], upto[:, 0:ne, 0:ne],
                                             ch.unsqueeze(1).to_broadcast([P, ne, ne]), ALU.mult))
                link(nc.vector.tensor_reduce(ce, csum[:, 0:ne, 0:ne], AX.X, ALU.add))
                link(nc.vector.tensor_tensor(base, ce, ch, ALU.subtract))
                link(nc.vector.tensor_scalar(base, base, float(CHUNK), float(BASEC[n] * CHUNK), ALU.mult, ALU.add))
                sf = slot_f[:, :, 0:ne]
                link(nc.vector.tensor_tensor(sf, cum[1][:, 4:4 + B, 0:ne], cnt[:, :, 0:ne], ALU.subtract))
                link(nc.vector.tensor_tensor(sf, sf, base.unsqueeze(1).to_broadcast([P, B, ne]), ALU.add))
                link(nc.vector.tensor_tensor(sf, sf, within, ALU.add))
                for k in range(TOPK[n]):
                    for values, buf in ((sf, pick[0]), (g[:], pick[1])):
                        pk = buf[:, :, 0:ne]
                        link(nc.vector.scalar_tensor_tensor(out=pk, in0=nth[:, :, 0:ne], scalar=float(k + 1),
                                                            in1=values, op0=ALU.is_equal, op1=ALU.mult))
                        if values is sf:
                            link(nc.vector.tensor_reduce(slot_k[:], pk, AX.X, ALU.add))
                            link(nc.vector.tensor_copy(slot_i[:, k, :], slot_k[:]))
                        else:
                            nc.vector.tensor_reduce(staged[:, :, k, D], pk, AX.X, ALU.add).then_inc(slots_made, 1)
                ahead = 2 // UPE[n]
                maxc = MAXC[n] + ahead
                link(nc.vector.tensor_tensor(past[:, 0:maxc, 0:ne], cend[0:1, 0:ne].unsqueeze(1)
                                             .to_broadcast([1, maxc, ne]),
                                             chunk_no[:, 0:maxc].unsqueeze(2).to_broadcast([1, maxc, ne]), ALU.is_le))
                link(nc.vector.tensor_reduce(expert_f[:, 0:maxc], past[:, 0:maxc, 0:ne], AX.X, ALU.add))
                link(nc.vector.tensor_scalar(expert_f[:, 0:maxc], expert_f[:, 0:maxc], float(ne - 1), None, ALU.min))
                link(nc.vector.scalar_tensor_tensor(out=experts_i[n][:, 0:MAXC[n]], in0=expert_f[:, ahead:maxc],
                                                    scalar=float(ne), in1=expert_f[:, 0:MAXC[n]],
                                                    op0=ALU.mult, op1=ALU.add))
                per_turn = 4 // UPE[n]
                link(nc.vector.tensor_scalar(expert_f[:, 0:MAXT[n]], chunk_no[:, 0:MAXT[n]], float(per_turn),
                                             None, ALU.mult))
                link(nc.vector.tensor_scalar(expert_f[:, 0:MAXT[n]], expert_f[:, 0:MAXT[n]],
                                             cend[0:1, ne - 1:ne], None, ALU.is_lt))
                link(nc.vector.tensor_reduce(more_f[:], expert_f[:, MINT[n]:MAXT[n]], AX.X, ALU.add))
                nc.vector.tensor_copy(more_i[n][:], more_f[:]).then_inc(table_made, 1)

                if n == 1:
                    for u in range(2):
                        dve.wait_ge(s_w_hi, u + 1)
                        nc.vector.tensor_tensor(w_lo[u][:], up_raw[u][:], w_hi[u][:].bitcast(f32), ALU.subtract)\
                            .then_inc(s_w_split, 1)
                    for q in range(4):
                        dve.wait_ge(s_silu, q + 1)
                        dve.wait_ge(s_u_done, q + 1)
                        nc.vector.tensor_tensor(hid[q % 2][:], silu_g[q % 2][:], bank[5][:], ALU.mult)\
                            .then_inc(s_hid, 1)
                    add_banks(y_turned, 1, 4)

                turns, more = load_turns(dve, n)

                def low_parts(i, r, ahead):
                    c, first_unit, _, cslot, _ = chunk_of(n, i, r, ahead)
                    if first_unit:
                        dve.wait_ge(f.x_hi_made, c + 1)
                        par = cslot % 2
                        if not (isinstance(c, int) and c < 4 // upe):
                            dve.wait_ge(f.y_made, c - 4 // upe + 1)
                        nc.vector.tensor_copy(meta[cslot][:], rowbuf[cslot][:, :, D:D + 2])
                        nc.vector.tensor_tensor(xT_lo[par][:].rearrange("p k c -> p (k c)"), bank[2 + par][:],
                                                xT_hi[par][:].rearrange("p k c -> p (k c)").bitcast(f32),
                                                ALU.subtract).then_inc(f.x_split, 1)
                    slot, _ = step_slot(i, r, ahead)
                    dve.wait_ge(f.w_hi_made, 4 * i + r + ahead + 1)
                    nc.vector.tensor_tensor(w_lo[slot % 2][:], up_raw[slot][:], w_hi[slot % 2][:].bitcast(f32),
                                            ALU.subtract).then_inc(f.w_split, 1)

                low_parts(0, 0, 0)
                low_parts(0, 1, 0)

                def step(i, r, first, last):
                    s = 4 * i + r
                    _, _, last_unit, cslot, filled = chunk_of(n, i, r, 0)
                    dve.wait_ge(f.silu_made, s + 1)
                    if last_unit:
                        if not is_zero(filled):
                            dve.wait_ge(f.sent[cslot], 32 * filled)
                        nc.vector.tensor_copy(place[cslot][:], meta[cslot][:, :, 1].bitcast(i32))
                    up_v, sg = bank[r % 2][:, TILES * P:2 * TILES * P], silu_g[r % 2][:, 0:TILES * P]
                    out = hid[r % 2][:, 0:TILES * P]
                    if n == 0:
                        ins = nc.vector.scalar_tensor_tensor(out=out, in0=sg, scalar=SWIGLU_LIMIT, in1=up_v,
                                                             op0=ALU.min, op1=ALU.mult)
                    else:
                        ins = nc.vector.tensor_tensor(out, sg, up_v, ALU.mult)
                    ins.then_inc(f.hid_made, 1)
                    if not (last and r >= 2):
                        low_parts(i, r, 2)

                run_steps(dve, n, step, more)
                base_k = n * TOPK[0]
                for k in range(TOPK[n]):
                    dve.wait_ge(y_in_done[k % 2], 16 * (n * TOPK[0] // 2 + k // 2 + 1))
                    if k:
                        dve.wait_ge(y_in_used, base_k + k)
                    if k < TOPK[n] - 1:
                        ins = nc.vector.tensor_tensor(x_sb[:], x_sb[:], y_in[k % 2], ALU.add)
                        ins.then_inc(y_in_used, 1)
                    else:
                        for c in range(4):
                            part = x_sb[:, 2 * c:2 * c + 2]
                            nc.vector.tensor_tensor(part, part, y_in[k % 2][:, 2 * c:2 * c + 2], ALU.add)\
                                .then_inc(x_added, 1)
                        dve.sem_inc(y_in_used, 1)
                if n == 1:
                    continue

                dve.wait_ge(x_added, X_FFN0)
                layer_norm(2)
                dve.wait_ge(par_in, 160)
                for c in range(2):
                    dve.wait_ge(gx_done, c + 1)
                    nc.vector.tensor_tensor(gx[:, 4 * c:4 * c + 4].rearrange("p b k l -> p (b k) l"),
                                            bank[c][:].rearrange("p (n l) -> p n l", l=LAT),
                                            g_b[:].unsqueeze(1).to_broadcast([P, 4 * KB, LAT]), ALU.add)\
                        .then_inc(gx_copied, 1)

                def row_max(b):
                    dve.wait_ge(sc_done, b + 1)
                    nc.vector.tensor_reduce(nmax[:, b, :], bank[4 + b % 2][:].rearrange("p (k t) -> p k t", k=KB),
                                            AX.X, ALU.max, negate=True).then_inc(max_made, 1)

                def normalise(b):
                    dve.wait_ge(exp_made, b + 1)
                    link(nc.vector.reciprocal(prec[:, b, :], psum_row[:, b, :]))
                    for t in range(KB):
                        last = nc.vector.tensor_scalar(prob[b % 2][:, t], prob[b % 2][:, t], prec[:, b, t:t + 1],
                                                       None, ALU.mult)
                    last.then_inc(prob_made, 1)

                def tx_statistics(b):
                    dve.wait_ge(tx_copied, b + 1)
                    nc.vector.bn_stats(stats2[:, b, :], tx[:, b, :]).then_inc(tx_stats, 1)

                row_max(0)
                for b in range(B):
                    if b + 1 < B:
                        row_max(b + 1)
                    normalise(b)
                    if b >= 2:
                        tx_statistics(b - 2)
                tx_statistics(B - 2)
                tx_statistics(B - 1)
                dve.wait_ge(tx_stats, B)
                for b in range(B):
                    last = nc.vector.bn_aggr(mv2[:, b, :], stats2[:, b, :])
                last.then_inc(mean_in, 1)
                dve.wait_ge(mean_done, 1)
                link(nc.vector.tensor_copy(mean_all[:], bank[0][0:LAT, 0:B]))
                link(nc.vector.tensor_tensor(dev[:], mv2[:, :, 0], mean_all[:], ALU.subtract))
                link(nc.vector.tensor_tensor(dev[:], dev[:], dev[:], ALU.mult))
                nc.vector.tensor_tensor(spread[:], dev[:], mv2[:, :, 1], ALU.add).then_inc(dev_in, 1)
                dve.wait_ge(dev_done, 1)
                nc.vector.tensor_scalar(veps2[:], bank[1][0:LAT, 0:B], EPS, None, ALU.add).then_inc(var2_ready, 1)
                dve.wait_ge(std2_ready, 1)
                newton(rstd2[:], std2[:], veps2[:], nwt2[:])
                nc.vector.scalar_tensor_tensor(out=shift2[:], in0=mean_all[:], scalar=-1.0, in1=rstd2[:],
                                               op0=ALU.mult, op1=ALU.mult).then_inc(shift_made, 1)
                for c in range(4):
                    dve.wait_ge(z_made, 2 * c + 2)
                    chunk = tx[:, 2 * c:2 * c + 2]
                    nc.vector.tensor_tensor(chunk, chunk, gamma_sb[:].unsqueeze(1).to_broadcast([LAT, 2, D]),
                                            ALU.mult).then_inc(zg_made, 1)
                dve.wait_ge(ctx_added, 1)
                for c in range(4):
                    dve.wait_ge(w_done, c + 1)
                    dst = x_sb[:, 2 * c:2 * c + 2].rearrange("p b d -> p (b d)")
                    nc.vector.scalar_tensor_tensor(out=dst, in0=bank[4 + c][:], scalar=outb_sb[:], in1=dst,
                                                   op0=ALU.add, op1=ALU.add).then_inc(x_added, 1)

        @block.tensor
        def _(pe):
            pe.wait_ge(ident_made, 2)
            for b in range(B):
                pe.wait_ge(normed, b + 1)
                for blk in range(KB):
                    col = (b % 2) * D + blk * P
                    last = nc.tensor.transpose(bank[b // 2][:, col:col + P], h_sb[:, b, blk * P:(blk + 1) * P],
                                               ident[:])
                if b % 2:
                    last.then_inc(q_turned, 1)

            def convolve(h, slot, toep_wait, free):
                pe.wait_ge(kv_made, h + 1)
                pe.wait_ge(toep_in[slot], toep_wait)
                if free is not None:
                    pe.wait_ge(prod_made, free)
                y0, y1 = bank[4 + 2 * slot][:], bank[5 + 2 * slot][:]
                near, far = toep[slot][:, 0:P], toep[slot][:, P:2 * P]
                nc.tensor.matmul(y0, near, kv[slot][:, 0], start=True, stop=True)
                nc.tensor.matmul(y1, near, kv[slot][:, 1], start=True, stop=False)
                nc.tensor.matmul(y1, far, kv[slot][:, 0], start=False, stop=True).then_inc(conv_done, 1)

            convolve(0, 0, 16, None)
            convolve(1, 1, 16, None)
            with pe.Fori(1, HEADS // 2) as i:
                for slot in range(2):
                    convolve(2 * i + slot, slot, 16 * (i + 1), 2 * i + slot - 1)
            pe.wait_ge(head_done, HEADS)
            pe.wait_ge(q_copied, 4)
            for b in range(B):
                for blk in range(KB):
                    col = (b % 2) * D + blk * P
                    last = nc.tensor.transpose(bank[b // 2][:, col:col + P], oT[:, blk, b, :], ident[:])
                if b % 2:
                    last.then_inc(o_turned, 1)

            def three_passes(out, w, xs, start, stop):
                (wh, wl), (xh, xl) = w, xs
                nc.tensor.matmul(out, wh, xh, start=start, stop=False)
                nc.tensor.matmul(out, wh, xl, start=False, stop=False)
                return nc.tensor.matmul(out, wl, xh, start=False, stop=stop)

            for n in range(2):
                f, ne, upe = ffns[n], EXPERTS[n], UPE[n]
                pe.wait_ge(x_added, (X_ATT0, X_ATT1)[n])
                for c in range(4):
                    half, k = c // 2, c % 2
                    for m in range(4):
                        b = 4 * half + m
                        pe.wait_ge(normed, (8 if n == 0 else 24) + b + 1)
                        last = nc.tensor.transpose(bank[c][:, m * P:(m + 1) * P], h_sb[:, b, k * P:(k + 1) * P],
                                                   ident[:])
                    last.then_inc(hT_turned, 1)
                pe.wait_ge(rw_split, n + 1)
                for half in range(2):
                    pe.wait_ge(hT_lo_made, 4 * n + 2 * half + 2)
                    cols = slice(half * HALF, (half + 1) * HALF)
                    for k in range(KB):
                        for x in (hT_hi, hT_lo):
                            last = nc.tensor.matmul(bank[4 + half][0:2 * ne, :], rw[n][:, k], x[:, k, cols],
                                                    start=(k == 0 and x is hT_hi), stop=(k == KB - 1 and x is hT_lo))
                    last.then_inc(lgT_done, 1)
                for b in range(B):
                    if b % 4 == 0:
                        pe.wait_ge(lgT_copied, 2 * n + b // 4 + 1)
                    last = nc.tensor.transpose(bank[6][:, b * 2 * ne:(b + 1) * 2 * ne],
                                               lgT[0:2 * ne, b * P:(b + 1) * P], ident[0:2 * ne, 0:2 * ne])
                last.then_inc(logits_done, 1)

                def shared_up(q):
                    u, half = q // 2, q % 2
                    pe.wait_ge(s_w_split, u + 1)
                    if q:
                        pe.wait_ge(s_hid, q)
                    cols = slice(half * HALF, (half + 1) * HALF)
                    for m, done in enumerate((s_g_done, s_u_done)):
                        for k in range(KB):
                            wc = slice((m * KB + k) * P, (m * KB + k + 1) * P)
                            last = three_passes(bank[4 + m][:], (w_hi[u][:, wc], w_lo[u][:, wc]),
                                                (hT_hi[:, k, cols], hT_lo[:, k, cols]), k == 0, k == KB - 1)
                        last.then_inc(done, 1)

                def shared_down(q):
                    u, half = q // 2, q % 2
                    pe.wait_ge(s_hid, q + 1)
                    for k in range(KB):
                        last = nc.tensor.matmul(bank[2 * k + half][:], down_raw[u][:, k * P:(k + 1) * P],
                                                hid[q % 2][:], start=(u == 0), stop=(u == 1))
                    last.then_inc(s_down, 1)

                pe.wait_ge(mask_made, n + 1)
                pe.wait_ge(consts_made, 1)
                mk = mask[:, :, 0:ne]
                nc.tensor.matmul(bank[7][:, 0:B * ne], before[:], mk, start=True, stop=True)
                nc.tensor.matmul(bank[7][:, 256:256 + B * ne], ones[:], mk, start=True, stop=True)\
                    .then_inc(ranked, 1)
                if n == 1:
                    for q in range(4):
                        shared_up(q)
                        if q:
                            shared_down(q - 1)
                    shared_down(3)
                    pe.wait_ge(yT_copied, 4)
                    for b in range(B):
                        for k in range(KB):
                            col = (b % 2) * D + k * P
                            last = nc.tensor.transpose(bank[4 + b // 2][:, col:col + P],
                                                       yT[:, k, b * P:(b + 1) * P], ident[:])
                        if b % 2:
                            last.then_inc(y_turned, 1)
                    pe.wait_ge(x_added, X_ATT1 + 4)
                turns, more = load_turns(pe, n)

                def turn_rows(i, r, ahead):
                    c, first_unit, _, slot, filled = chunk_of(n, i, r, ahead)
                    if not first_unit:
                        return
                    pe.wait_ge(f.rows_in[slot], 16 * filled + 16)
                    for t in range(TILES):
                        for k in range(KB):
                            col = (k * TILES + t) * P
                            last = nc.tensor.transpose(bank[2 + slot % 2][:, col:col + P],
                                                       rowbuf[slot][:, t, k * P:(k + 1) * P], ident[:])
                    last.then_inc(f.xT_turned, 1)

                def up(i, r, first):
                    s = 4 * i + r
                    c, _, _, cslot, _ = chunk_of(n, i, r, 0)
                    pe.wait_ge(f.w_split, s + 1)
                    pe.wait_ge(f.x_split, c + 1)
                    if not (first and r < 2):
                        pe.wait_ge(f.hid_made, s - 1)
                    par = cslot % 2
                    for m in range(2):
                        for k in range(KB):
                            wc = slice((m * KB + k) * P, (m * KB + k + 1) * P)
                            last = three_passes(bank[r % 2][:, m * TILES * P:(m + 1) * TILES * P],
                                                (w_hi[r % 2][:, wc], w_lo[r % 2][:, wc]),
                                                (xT_hi[par][:, k], xT_lo[par][:, k]), k == 0, k == KB - 1)
                    last.then_inc(f.up_done, 1)

                def down(i, r, ahead):
                    s = 4 * i + r + ahead
                    c, first_unit, last_unit, cslot, _ = chunk_of(n, i, r, ahead)
                    slot, filled = step_slot(i, r, ahead)
                    pe.wait_ge(f.hid_made, s + 1)
                    pe.wait_ge(f.down_in[slot], 16 * filled + 16)
                    if first_unit and not (isinstance(c, int) and c < 2):
                        pe.wait_ge(f.y_made, c - 1)
                    for t in range(TILES):
                        last = nc.tensor.matmul(bank[4 + cslot % 2][:, t * D:(t + 1) * D],
                                                hid[slot % 2][:, t * P:(t + 1) * P], down_raw[slot][:],
                                                start=first_unit and t == 0, stop=last_unit and t == TILES - 1,
                                                skip_group_check=True)
                    last.then_inc(f.down_done, 1)

                turn_rows(0, 0, 0)
                if upe == 1:
                    turn_rows(0, 1, 0)

                def step(i, r, first, last):
                    up(i, r, first)
                    if not (last and r >= 2):
                        c, first_unit, _, _, _ = chunk_of(n, i, r, 2)
                        if first_unit and not (isinstance(c, int) and c < 2):
                            pe.wait_ge(f.x_split, c - 1)
                        turn_rows(i, r, 2)
                    if not (first and r == 0):
                        down(i, r, -1)

                run_steps(pe, n, step, more)
                down(turns, 0, -1)
                if n == 1:
                    continue

                pe.wait_ge(par_in, 160)
                pe.wait_ge(ctx_in, 16)
                pe.wait_ge(x_added, X_FFN0)
                for c in range(4):
                    nc.tensor.matmul(bank[c][0:LAT, :], theta_sb[:],
                                     ctx_sb[:, 2 * c:2 * c + 2].rearrange("p b t -> p (b t)"), start=True, stop=True)\
                        .then_inc(th_done, 1)
                for c in range(4):
                    pe.wait_ge(normed, 16 + 2 * c + 2)
                    nc.tensor.matmul(bank[4 + c][0:LAT, :], phi_sb[:],
                                     h_sb[:, 2 * c:2 * c + 2].rearrange("p b t -> p (b t)"), start=True, stop=True)\
                        .then_inc(ph_done, 1)
                pe.wait_ge(th_copied, 4)
                for b in range(B):
                    for k in range(KB):
                        col = ((b % 4) * KB + k) * LAT
                        last = nc.tensor.matmul(bank[b // 4][:, col:col + LAT], h_sb[:, b, k * P:(k + 1) * P],
                                                gw_sb[:], start=True, stop=True)
                    if b % 4 == 3:
                        last.then_inc(gx_done, 1)
                pe.wait_ge(ph_copied, 4)

                def scores(b):
                    if b >= 2:
                        pe.wait_ge(exp_made, b - 1)
                    for t in range(KB):
                        last = nc.tensor.matmul(bank[4 + b % 2][:, t * D:(t + 1) * D], thT[:, b, t * P:(t + 1) * P],
                                                phT[:, b, :], start=True, stop=True)
                    last.then_inc(sc_done, 1)

                def turn_probs(b):
                    pe.wait_ge(prob_made, b + 1)
                    if b >= 2:
                        pe.wait_ge(pT_copied, b - 1)
                    for k in range(KB):
                        for t in range(KB):
                            col = k * D + t * P
                            last = nc.tensor.transpose(bank[6 + b % 2][:, col:col + P],
                                                       prob[b % 2][:, t, k * P:(k + 1) * P], ident[:])
                    last.then_inc(pT_turned, 1)

                def weigh(b):
                    pe.wait_ge(pT_copied, b + 1)
                    if b == 0:
                        pe.wait_ge(gx_copied, 2)
                    if b >= 2:
                        pe.wait_ge(tx_copied, b - 1)
                    for k in range(KB):
                        last = nc.tensor.matmul(bank[2 + b % 2][0:LAT, 0:D], gx[:, b, k, :], probT[b % 2][:, k, :],
                                                start=(k == 0), stop=(k == KB - 1))
                    last.then_inc(tx_done, 1)

                scores(0)
                for b in range(B):
                    if b + 1 < B:
                        scores(b + 1)
                    turn_probs(b)
                    if b >= 1:
                        weigh(b - 1)
                weigh(B - 1)
                pe.wait_ge(consts_made, 1)
                pe.wait_ge(mean_in, 1)
                nc.tensor.matmul(bank[0][0:LAT, 0:B], avg[:], mv2[:, :, 0], start=True, stop=True)\
                    .then_inc(mean_done, 1)
                pe.wait_ge(dev_in, 1)
                nc.tensor.matmul(bank[1][0:LAT, 0:B], avg[:], spread[:], start=True, stop=True).then_inc(dev_done, 1)
                for c in range(4):
                    pe.wait_ge(relu_made, c + 1)
                    nc.tensor.matmul(bank[4 + c][:], outw_sb[:], tx[:, 2 * c:2 * c + 2].rearrange("p b t -> p (b t)"),
                                     start=True, stop=True).then_inc(w_done, 1)


def kernel(x, ctx_2048, L0_xattn_ssm_kernel, L0_xattn_D, L0_ffn_Wr, L0_ffn_Wg, L0_ffn_Wu, L0_ffn_Wd,
           L1_xattn_theta_w, L1_xattn_theta_b, L1_xattn_phi_w, L1_xattn_phi_b, L1_xattn_g_w, L1_xattn_g_b,
           L1_xattn_ln_gamma, L1_xattn_ln_beta, L1_xattn_out_w, L1_xattn_out_b, L1_ffn_gate_w, L1_ffn_w11,
           L1_ffn_w33, L1_ffn_w22, L1_ffn_sw1, L1_ffn_sw2, L1_ffn_sw3):
    import numpy as np
    import concourse.bacc as bacc
    from concourse.bass_utils import run_bass_kernel_spmd

    def arr(a):
        return np.ascontiguousarray(np.asarray(a))

    def by_hidden(w):
        return w.reshape(-1, KB, P, P).transpose(0, 2, 1, 3).reshape(-1, P, KB * P)

    def halves(w):
        return w.reshape(-1, D, KB, P).transpose(0, 2, 1, 3).reshape(-1, D, P)

    wg, wu, wd = (np.asarray(a) for a in (L0_ffn_Wg, L0_ffn_Wu, L0_ffn_Wd))
    up0 = np.concatenate([by_hidden(halves(wg)), by_hidden(halves(wu))], axis=2)
    w1, w3, w2, s1, s2, s3 = (np.asarray(a) for a in (L1_ffn_w11, L1_ffn_w33, L1_ffn_w22, L1_ffn_sw1, L1_ffn_sw2,
                                                      L1_ffn_sw3))
    gate1 = np.concatenate([by_hidden(w1.transpose(0, 2, 1)), by_hidden(halves(s1.T[None]))])
    up1 = np.concatenate([by_hidden(w3.transpose(0, 2, 1)), by_hidden(halves(s3.T[None]))])
    down1 = np.concatenate([w2.transpose(0, 2, 1), s2.T.reshape(2, P, D)])
    ctx = np.asarray(ctx_2048)
    ctxr = ctx.transpose(2, 0, 1).reshape(KB, P, B, P)[:, ::-1]
    filt = np.pad(np.asarray(L0_xattn_ssm_kernel), ((0, 0), (P - 1, KPAD - (P - 1) - D)))
    arrays = {
        "x": arr(x), "ctx": arr(ctx), "ctxr": arr(ctxr), "filt": arr(filt),
        "skip": arr(np.asarray(L0_xattn_D).reshape(HEADS, 1)), "wr": arr(L0_ffn_Wr), "up0": arr(up0),
        "down0": arr(wd.reshape(UNITS0, P, D)),
        "theta": arr(np.asarray(L1_xattn_theta_w).T), "theta_b": arr(np.asarray(L1_xattn_theta_b).reshape(LAT, 1)),
        "phi": arr(np.asarray(L1_xattn_phi_w).T), "phi_b": arr(np.asarray(L1_xattn_phi_b).reshape(LAT, 1)),
        "g": arr(np.asarray(L1_xattn_g_w).T), "g_b": arr(L1_xattn_g_b),
        "gamma": arr(L1_xattn_ln_gamma), "beta": arr(L1_xattn_ln_beta),
        "outw": arr(np.asarray(L1_xattn_out_w).T), "outb": arr(np.asarray(L1_xattn_out_b).reshape(P, 1)),
        "gate": arr(np.asarray(L1_ffn_gate_w).T), "up1": arr(np.concatenate([gate1, up1], axis=2)),
        "down1": arr(down1),
    }
    nc = bacc.Bacc("TRN2", target_bir_lowering=False, num_devices=1)
    f32 = mybir.dt.float32
    ins = [nc.dram_tensor(f"in_{k}", a.shape, mybir.dt.from_np(a.dtype), kind="ExternalInput").ap()
           for k, a in arrays.items()]
    out = nc.dram_tensor("out", (B, S, D), f32, kind="ExternalOutput").ap()
    scratch = [nc.dram_tensor(name, shape, f32, kind="Internal").ap() for name, shape in (
        ("filt_s", (HEADS, KPAD)), ("rows_s", ((MAXC[0] + MAXC[1]) * CHUNK, ROW)),
        ("y0_s", (TOPK[0] * TOK, D)), ("y1_s", (TOPK[1] * TOK, D)))]
    build(nc, *ins, out, *scratch)
    r = run_bass_kernel_spmd(nc, [{f"in_{k}": a for k, a in arrays.items()}], core_ids=[0])
    return r.results[0]["out"]
```

```python
from contextlib import ExitStack

import concourse.bass as bass
from concourse import mybir

P = 128
B, S, D = 8, 128, 256
TOK = B * S
KB = D // P
HALF = TOK // 2
HEADS, HD = 16, 8
PAIRS = HD * HD
KPAD = P - 1 + D + 1
UP_W = 2 * D
LAT = 64
E0, UNITS0 = 8, 16
E1, UNITS1 = 32, 34
GROUPS, GSIZE, TOPG, TOPK1 = 8, 4, 4, 6
ROUTE_SCALE = 2.5
SWIGLU_LIMIT = 7.0
EPS = 1e-5
CHUNK, TILES = 256, 2
TOPK = (2, TOPK1)
EXPERTS = (E0, E1)
UPE = (2, 1)
MAXC = tuple(-(-(TOK * k // CHUNK + e) * u // 4) * 4 // u for k, e, u in zip(TOPK, EXPERTS, UPE))
BASEC = (0, MAXC[0])
ROW = D + 4
NOWHERE = 1 << 24
LOWEST = -3.0e38
TAKEN = 9.0
PAD = -5.0


def build(nc, x_d, ctx_d, ctxr_d, filt_d, skip_d, wr_d, up0_d, down0_d, theta_d, theta_b_d, phi_d, phi_b_d, g_d, g_b_d,
          gamma_d, beta_d, outw_d, outb_d, gate_d, up1_d, down1_d, out_d, filt_s, rows_s, y0_s, y1_s):
    f32, f32r, i32 = mybir.dt.float32, mybir.dt.float32r, mybir.dt.int32
    ACT = mybir.ActivationFunctionType
    ALU = mybir.AluOpType
    AX = mybir.AxisListType

    def view(t, offset, dims):
        base = t[:]
        return bass.AP(base.tensor, base.offset + offset, [list(base.ap[0])] + [list(d) for d in dims])

    with ExitStack() as stack:
        def sb(name, shape, dt=f32):
            return stack.enter_context(nc.sbuf_tensor(name, shape, dt))

        def sem(name):
            return stack.enter_context(nc.semaphore(name))

        x_sb = sb("x_sb", [P, B, D])
        h_sb = sb("h_sb", [P, B, D])
        ctx_sb = sb("ctx_sb", [P, B, D])
        ident = sb("ident", [P, P])
        filt_row = sb("filt_row", [HEADS, KPAD])
        skip_col = sb("skip_col", [HEADS, 1])
        stats = sb("stats", [P, B, 6])
        mv = sb("mv", [P, B, 2])
        veps = sb("veps", [P, B])
        rstd = sb("rstd", [P, B])
        shift = sb("shift", [P, B])
        minus_half = sb("minus_half", [P, 1])
        hT_hi = sb("hT_hi", [P, KB, TOK], f32r)
        hT_lo = sb("hT_lo", [P, KB, TOK], f32r)
        wr_sb = sb("wr_sb", [P, KB, E0])
        gate_sb = sb("gate_sb", [P, KB, E1])
        rw = [sb(f"rw{i}", [P, KB, 2 * e], f32r) for i, e in enumerate(EXPERTS)]
        up_raw = [sb(f"up_raw{i}", [P, UP_W]) for i in range(4)]
        down_raw = [sb(f"down_raw{i}", [P, D]) for i in range(4)]
        w_hi = [sb(f"w_hi{i}", [P, UP_W], f32r) for i in range(2)]
        w_lo = [sb(f"w_lo{i}", [P, UP_W], f32r) for i in range(2)]
        yT = sb("yT", [P, KB, TOK])
        oT = yT[:].rearrange("p k (b c) -> p k b c", b=B)
        logit = sb("logit", [P, B, 2 * E0])
        top8 = sb("top8", [P, B, 8])
        ex = sb("ex", [P, B, E0])
        marked = sb("marked", [P, B, 2 * E0])
        score = sb("score", [P, B, E1 + 8])
        gmax = sb("gmax", [P, B, 2 * GROUPS])
        gmask = sb("gmask", [P, B, GROUPS])
        gneg = sb("gneg", [P, B, GROUPS])
        allowed = sb("allowed", [P, B, E1 + 8])
        marked1 = sb("marked1", [P, B, E1 + 8])
        gates = [sb("gates0", [P, B, E0]), sb("gates1", [P, B, E1])]
        gsum = sb("gsum", [P, B])
        grec = sb("grec", [P, B])
        lgT = sb("lgT", [2 * E1, TOK])
        mask = sb("mask", [P, B, E1])
        rank = [sb(f"rank{i}", [P, B, 16 + E1]) for i in range(2)]
        nth = sb("nth", [P, B, E1])
        cum = [sb(f"cum{i}", [P, 4 + B, E1]) for i in range(2)]
        chunks = sb("chunks", [P, E1])
        cend = [sb(f"cend{i}", [P, 16 + E1]) for i in range(2)]
        past = sb("past", [1, MAXC[1] + 2, E1])
        sbase = sb("sbase", [P, E1])
        before = sb("before", [P, P])
        ones = sb("ones", [P, P])
        slot_f = sb("slot_f", [P, B, E1])
        pick = [sb(f"pick{i}", [P, B, E1]) for i in range(2)]
        slot_k = sb("slot_k", [P, B])
        slot_i = sb("slot_i", [P, TOPK1, B], i32)
        chunk_no = sb("chunk_no", [1, MAXC[1] + 2])
        expert_f = sb("expert_f", [1, MAXC[1] + 2])
        experts_i = [sb(f"experts_i{i}", [1, MAXC[1]], i32) for i in range(2)]
        more_f = sb("more_f", [1, 1])
        more_i = [sb(f"more_i{i}", [1, 1], i32) for i in range(2)]
        staged = sb("staged", [P, B, TOPK1, ROW])
        empty = sb("empty", [P, ROW])
        y_in = [h_sb[:], yT[:].rearrange("p k (b c) -> p (k b c)", b=B).rearrange("p (b d) -> p b d", b=B)]
        theta_sb = sb("theta_sb", [P, LAT])
        phi_sb = sb("phi_sb", [P, LAT])
        gw_sb = sb("gw_sb", [P, LAT])
        theta_b = sb("theta_b", [LAT, 1])
        phi_b = sb("phi_b", [LAT, 1])
        g_b = sb("g_b", [P, LAT])
        gamma_sb = sb("gamma_sb", [LAT, D])
        beta_sb = sb("beta_sb", [LAT, D])
        outw_sb = sb("outw_sb", [LAT, P])
        outb_sb = sb("outb_sb", [P, 1])
        nmax = sb("nmax", [P, B, KB])
        psum_row = sb("psum_row", [P, B, KB])
        prec = sb("prec", [P, B, KB])
        idle = sb("idle", [1, 4])
        tick = sb("tick", [1, 1])
        stats2 = sb("stats2", [LAT, B, 6])
        mv2 = sb("mv2", [LAT, B, 2])
        mean_all = sb("mean_all", [LAT, B])
        dev = sb("dev", [LAT, B])
        spread = sb("spread", [LAT, B])
        veps2 = sb("veps2", [LAT, B])
        rstd2 = sb("rstd2", [LAT, B])
        shift2 = sb("shift2", [LAT, B])
        avg = sb("avg", [LAT, LAT])

        thT = sb("thT", [LAT, B, D])

        scope = stack.enter_context(ExitStack())

        def scoped(name, shape, dt=f32):
            return scope.enter_context(nc.sbuf_tensor(name, shape, dt))

        ctxr_sb = scoped("ctxr_sb", [P, KB, B, P])
        toep = [scoped(f"toep{i}", [P, D]) for i in range(2)]
        kv = [scoped(f"kv{i}", [P, KB, B * PAIRS]) for i in range(2)]
        qT = scoped("qT", [P, KB, HEADS, B * HD])
        prod = [scoped(f"prod{i}", [P, KB, B * PAIRS]) for i in range(2)]
        scope.close()
        phT = scoped("phT", [LAT, B, D])
        gx = scoped("gx", [P, B, KB, LAT])
        prob = [scoped(f"prob{i}", [P, KB, D]) for i in range(2)]
        probT = [scoped(f"probT{i}", [P, KB, D]) for i in range(2)]
        tx = scoped("tx", [LAT, B, D])
        scope.close()
        up_copy = [scoped(f"up_copy{i}", [P, HALF]) for i in range(2)]
        silu_g = [scoped(f"silu_g{i}", [P, HALF]) for i in range(2)]
        hid = [scoped(f"hid{i}", [P, HALF]) for i in range(2)]
        rowbuf = [scoped(f"rowbuf{i}", [P, TILES, ROW]) for i in range(4)]
        meta = [scoped(f"meta{i}", [P, TILES, 2]) for i in range(4)]
        place = [scoped(f"place{i}", [P, TILES], i32) for i in range(4)]
        xT_hi = [scoped(f"xT_hi{i}", [P, KB, TILES * P], f32r) for i in range(2)]
        xT_lo = [scoped(f"xT_lo{i}", [P, KB, TILES * P], f32r) for i in range(2)]
        y_sb = [scoped(f"y_sb{i}", [P, TILES, D]) for i in range(4)]

        bank = [stack.enter_context(nc.psum_tensor(f"bank{i}", [P, 512], f32)) for i in range(8)]

        x_in, filt_in, skip_in, ctx_in, par_in, rw_in = (sem(n) for n in (
            "x_in", "filt_in", "skip_in", "ctx_in", "par_in", "rw_in"))
        ctxr_in = sem("ctxr_in")
        filt_summed, filt_out = sem("filt_summed"), sem("filt_out")
        toep_in = [sem(f"toep_in{i}") for i in range(2)]
        ident_made, consts_made, dve_consts = sem("ident_made"), sem("consts_made"), sem("dve_consts")
        dve_step = sem("dve_step")
        var_ready, rstd_ready, shift_ready = sem("var_ready"), sem("rstd_ready"), sem("shift_ready")
        normed = [sem("normed_v"), sem("normed_a")]
        q_turned, q_copied = sem("q_turned"), sem("q_copied")
        kv_made, conv_done, prod_made, head_done = sem("kv_made"), sem("conv_done"), sem("prod_made"), sem("head_done")
        o_turned, x_added = sem("o_turned"), sem("x_added")
        hT_turned, hT_hi_made, hT_lo_made = sem("hT_turned"), sem("hT_hi_made"), sem("hT_lo_made")
        rw_hi_made, rw_split = sem("rw_hi_made"), sem("rw_split")
        lgT_done, lgT_copied, mask_made, ranked = sem("lgT_done"), sem("lgT_copied"), sem("mask_made"), sem("ranked")
        cum_made = sem("cum_made")
        nth_made, pool_step = sem("nth_made"), sem("pool_step")
        table_made, h_staged, slots_made = (sem(n) for n in ("table_made", "h_staged", "slots_made"))
        rows_sent = [sem(f"rows_sent{k}") for k in range(TOPK1)]
        s_u_copied = sem("s_u_copied")
        rows_init, init_made, ids_made = sem("rows_init"), sem("init_made"), sem("ids_made")
        logits_done, act_gate_in, act_gate_out = sem("logits_done"), sem("act_gate_in"), sem("act_gate_out")
        y_in_done, y_in_used = [sem(f"y_in_done{i}") for i in range(2)], sem("y_in_used")
        s_up_in, s_w_hi, s_w_split, s_g_done, s_u_done, s_silu, s_hid, s_down, yT_copied, y_turned = (sem(n) for n in (
            "s_up_in", "s_w_hi", "s_w_split", "s_g_done", "s_u_done", "s_silu", "s_hid", "s_down", "yT_copied",
            "y_turned"))

        class Ffn:

            def __init__(self, n):
                self.up_in = [sem(f"up_in{n}_{i}") for i in range(4)]
                self.down_in = [sem(f"down_in{n}_{i}") for i in range(4)]
                self.rows_in = [sem(f"rows_in{n}_{i}") for i in range(4)]
                self.sent = [sem(f"sent{n}_{i}") for i in range(4)]
                (self.w_hi_made, self.w_split, self.xT_turned, self.x_hi_made, self.x_split, self.up_done,
                 self.silu_made, self.hid_made, self.down_done, self.y_made, self.ticked) = (
                    sem(f"{name}{n}") for name in (
                        "w_hi_made", "w_split", "xT_turned", "x_hi_made", "x_split", "up_done", "silu_made",
                        "hid_made", "down_done", "y_made", "ticked"))

        ffns = [Ffn(0), Ffn(1)]
        th_done, th_copied, ph_done, ph_copied, gx_done, gx_copied = (sem(n) for n in (
            "th_done", "th_copied", "ph_done", "ph_copied", "gx_done", "gx_copied"))
        sc_done, max_made, exp_made, prob_made, pT_turned, pT_copied, tx_done, tx_copied, tx_stats = (sem(n) for n in (
            "sc_done", "max_made", "exp_made", "prob_made", "pT_turned", "pT_copied", "tx_done", "tx_copied",
            "tx_stats"))
        mean_in, mean_done, dev_in, dev_done, var2_ready, rstd2_ready, shift_made = (sem(n) for n in (
            "mean_in", "mean_done", "dev_in", "dev_done", "var2_ready", "rstd2_ready", "shift_made"))
        zb_made2 = sem("zb_made2")
        z_made, zg_made, zb_made, relu_made, w_done, ctx_added = (sem(n) for n in (
            "z_made", "zg_made", "zb_made", "relu_made", "w_done", "ctx_added"))
        out_done = sem("out_done")

        block = stack.enter_context(nc.Block())
        up_d, down_d, y_s = [up0_d, up1_d], [down0_d, down1_d], [y0_s, y1_s]
        MAXT = [MAXC[n] * UPE[n] // 4 for n in range(2)]
        MINT = [EXPERTS[n] * UPE[n] // 4 for n in range(2)]

        def step_slot(i, r, ahead):
            return (r + ahead) % 4, i + (r + ahead) // 4

        def chunk_of(n, i, r, ahead):
            t = r + ahead
            if UPE[n] == 1:
                return 4 * i + t, True, True, t % 4, i + t // 4
            return 2 * i + t // 2, t % 2 == 0, t % 2 == 1, (t // 2) % 2, i + t // 4

        def run_steps(eng, n, step, more):
            peeled = UPE[n]
            for i in range(peeled):
                for r in range(4):
                    step(i, r, i == 0, False)
            with eng.Fori(peeled, more + (MINT[n] - 1)) as i:
                for r in range(4):
                    step(i, r, False, False)
            for r in range(4):
                step(more + (MINT[n] - 1), r, False, True)

        def is_zero(count):
            return isinstance(count, int) and count == 0

        def load_turns(eng, n):
            eng.wait_ge(table_made, n + 1)
            more = eng.value_load(more_i[n][0:1, 0:1], min_val=0, max_val=MAXT[n] - MINT[n])
            return more + MINT[n], more

        def wait_normed(eng, k, batches):
            eng.wait_ge(normed[0], 4 * k + min(batches, 4))
            if batches > 4:
                eng.wait_ge(normed[1], 4 * k + batches - 4)

        SCORES = (4, 5, 0)
        OUT = (2, 3, 4, 5)

        X_ATT0, X_FFN0, X_ATT1, X_END = 4, 8, 12, 20

        @block.sync
        def _(sp):
            sp.dma_start(filt_row[:], filt_d).then_inc(filt_in, 16)
            sp.dma_start(skip_col[:], skip_d).then_inc(filt_in, 16)
            sp.dma_start(ctxr_sb[:, 0], ctxr_d[0]).then_inc(ctxr_in, 16)
            sp.dma_start(ctxr_sb[:, 1], ctxr_d[1]).then_inc(ctxr_in, 16)
            sp.wait_ge(filt_summed, 1)
            sp.dma_start(filt_s, filt_row[:]).then_inc(filt_out, 16)
            sp.wait_ge(filt_out, 16)

            def load_toeplitz(h, slot):
                src = bass.AP(filt_s.tensor, filt_s.offset + h * KPAD, [[1, P], [1, D]])
                sp.dma_start(toep[slot][:], src).then_inc(toep_in[slot], 16)

            load_toeplitz(0, 0)
            load_toeplitz(1, 1)

            sp.dma_start(ctx_sb[:], ctx_d.rearrange("b s d -> s b d")).then_inc(ctx_in, 16)

            rows_v = rows_s.rearrange("(c t p) w -> p (c t) w", t=TILES, p=P)

            def empty_rows(chunk, count):
                sp.dma_start(rows_v[:, bass.ds(chunk * TILES, count * TILES)],
                             empty[:].unsqueeze(1).to_broadcast([P, count * TILES, ROW])).then_inc(rows_init, 16)

            INIT = MAXC[0] // (HEADS // 2)
            sp.wait_ge(init_made, 1)
            empty_rows(0, INIT)
            with sp.Fori(1, HEADS // 2) as i:
                for slot in range(2):
                    sp.wait_ge(conv_done, 2 * i + slot - 1)
                    load_toeplitz(2 * i + slot, slot)
                empty_rows(i * INIT, INIT)

            for n in range(2):
                f, upe = ffns[n], UPE[n]
                if n == 1:
                    for u in range(2):
                        sp.dma_start(up_raw[u][:], up1_d[E1 + u]).then_inc(s_up_in, 16)
                        sp.dma_start(down_raw[u][:], down1_d[E1 + u]).then_inc(s_up_in, 16)
                    for c in range(0, MAXC[1], 8):
                        empty_rows(BASEC[1] + c, 8)
                turns, more = load_turns(sp, n)

                def wait_sent(c):
                    for k in range(TOPK[n]) if n == 0 else (min(c, TOPK1 - 1),):
                        sp.wait_ge(rows_sent[k], 16 * B * (2 if n == 1 and k < TOPK[0] else 1))

                if n == 1:
                    sp.wait_ge(s_w_split, 2)
                rows = rows_s.rearrange("(c t p) w -> c p t w", t=TILES, p=P)
                def units(i, r):
                    c = chunk_of(n, i, r, 0)[0]
                    both = sp.value_load(experts_i[n][0:1, bass.ds(c, 1)], min_val=0, max_val=EXPERTS[n] ** 2 - 1)
                    return (both % EXPERTS[n]) * upe, (both // EXPERTS[n]) * upe

                def of_unit(w, u):
                    return w[n][bass.ds(u, 1)].squeeze(0)

                def rows_of(i, r, ahead):
                    return rows[bass.ds(BASEC[n] + chunk_of(n, i, r, ahead)[0], 1)].squeeze(0)

                def load(dst, src, done):
                    sp.dma_start(dst[:], src).then_inc(done, 16)

                for r in range(2):
                    if r < 2 // upe:
                        wait_sent(r)
                        load(rowbuf[r], rows_of(0, r * upe, 0), f.rows_in[r])
                    load(up_raw[r], of_unit(up_d, units(0, r)[0] + r % upe), f.up_in[r])

                held = [None]

                def step(i, r, first, last):
                    s = 4 * i + r
                    if r % upe == 0:
                        held[0] = units(i, r)
                    here, later = held[0]
                    down_src = of_unit(down_d, here + r % upe)
                    if not (last and r >= 2):
                        c, first_unit, _, cslot, _ = chunk_of(n, i, r, 2)
                        slot, _ = step_slot(i, r, 2)
                        up_src, rows_src = of_unit(up_d, later + r % upe), rows_of(i, r, 2)
                        if not first:
                            sp.wait_ge(f.w_split, s - 1)
                            sp.wait_ge(f.x_split, c - (3 if upe == 1 else 1))
                        elif r >= 2:
                            sp.wait_ge(f.w_split, r - 1)
                            if upe == 1:
                                sp.wait_ge(f.x_split, r - 1)
                            else:
                                sp.wait_ge(f.x_split, 1)
                        if n == 1 and first:
                            wait_sent(c)
                        if first_unit:
                            load(rowbuf[cslot], rows_src, f.rows_in[cslot])
                        load(up_raw[slot], up_src, f.up_in[slot])
                    if not first:
                        sp.wait_ge(f.down_done, s - 3)
                    elif n == 1 and r == 0:
                        sp.wait_ge(s_down, 4)
                    load(down_raw[r], down_src, f.down_in[r])

                run_steps(sp, n, step, more)
                for slot in range(4 // upe):
                    sp.wait_ge(f.sent[slot], 32 * turns)
                base = n * TOPK[0]
                for k in range(TOPK[n]):
                    if k >= 2:
                        sp.wait_ge(y_in_used, base + k - 1)
                    sp.dma_start(y_in[k % 2], y_s[n][k * TOK:(k + 1) * TOK].rearrange("(b p) d -> p b d", p=P))\
                        .then_inc(y_in_done[k % 2], 16)
            for q in range(4):
                sp.wait_ge(x_added, X_END - 3 + q)
                sp.dma_start(out_d.rearrange("b s d -> s b d")[:, 2 * q:2 * q + 2], x_sb[:, 2 * q:2 * q + 2])\
                    .then_inc(out_done, 16)
            sp.wait_ge(out_done, 64)

        @block.gpsimd
        def _(pool):
            nc.gpsimd.memset(ident[:], 0.0).then_inc(ident_made, 1)
            pool.wait_ge(ident_made, 1)
            nc.gpsimd.affine_select(out=ident[:], in_=ident[:], compare_op=ALU.not_equal, fill=1.0, base=0,
                                    pattern=[[-1, P]], channel_multiplier=1).then_inc(ident_made, 1)
            nc.gpsimd.memset(empty[:], 0.0).then_inc(ids_made, 1)
            pool.wait_ge(ids_made, 1)
            nc.gpsimd.memset(empty[:, D + 1:D + 2].bitcast(i32), NOWHERE).then_inc(init_made, 1)
            nc.gpsimd.memset(minus_half[:], -0.5).then_inc(ids_made, 1)

            def power(k):
                pool.wait_ge(var_ready, k + 1)
                nc.gpsimd.tensor_tensor(rstd[:], veps[:], minus_half[:].to_broadcast([P, B]), ALU.pow)\
                    .then_inc(rstd_ready, 1)

            pool.wait_ge(ids_made, 2)
            power(0)
            pool.wait_ge(ctxr_in, 32)

            def products(h, slot):
                for blk in range(KB):
                    rows = ctxr_sb[:, blk].rearrange("p b (h j) -> p b h j", j=HD)[:, :, bass.ds(h, 1), :]\
                        .rearrange("p b o j -> p b (o j)")
                    k = rows.unsqueeze(3).to_broadcast([P, B, HD, HD])
                    v = rows.unsqueeze(2).to_broadcast([P, B, HD, HD])
                    last = nc.gpsimd.tensor_tensor(
                        kv[slot][:, blk].rearrange("p (b i j) -> p b i j", i=HD, j=HD), k, v, ALU.mult)
                last.then_inc(kv_made, 1)

            products(0, 0)
            products(1, 1)
            with pool.Fori(1, HEADS // 2) as i:
                for slot in range(2):
                    pool.wait_ge(conv_done, 2 * i + slot - 1)
                    products(2 * i + slot, slot)
            nc.gpsimd.memset(ones[:], 1.0).then_inc(ids_made, 1)
            pool.wait_ge(ids_made, 3)
            nc.gpsimd.affine_select(out=before[:], in_=ones[:], compare_op=ALU.is_gt, fill=0.0, base=0,
                                    pattern=[[1, P]], channel_multiplier=-1)
            nc.gpsimd.iota(chunk_no[:], pattern=[[1, MAXC[1] + 2]], base=0, channel_multiplier=0,
                           allow_small_or_imprecise_dtypes=True)
            nc.gpsimd.iota(staged[:, :, :, D + 1].bitcast(i32), pattern=[[P, B], [TOK, TOPK1]], base=0,
                           channel_multiplier=1)
            nc.gpsimd.memset(staged[:, :, :, D + 2:ROW], 0.0)
            nc.gpsimd.memset(avg[:], 1.0 / LAT).then_inc(consts_made, 1)

            pool_count = [0]
            pool.wait_ge(dve_consts, 1)
            for n in range(2):
                f = ffns[n]
                if n == 1:
                    for u in range(2):
                        pool.wait_ge(s_w_hi, u + 1)
                        nc.gpsimd.tensor_tensor(w_lo[u][:], up_raw[u][:], w_hi[u][:].bitcast(f32), ALU.subtract)\
                            .then_inc(s_w_split, 1)
                power(1 if n == 0 else 3)
                ne = EXPERTS[n]
                pool.wait_ge(mask_made, n + 1)
                src, far = mask[:, :, 0:ne], 1
                nc.gpsimd.tensor_copy(rank[0][:, :, 16:16 + ne], src).then_inc(pool_step, 1)
                pool_count[0] += 1
                at = 0
                while far < ne:
                    pool.wait_ge(pool_step, pool_count[0])
                    nc.gpsimd.tensor_tensor(rank[1 - at][:, :, 16:16 + ne], rank[at][:, :, 16:16 + ne],
                                            rank[at][:, :, 16 - far:16 - far + ne], ALU.add).then_inc(pool_step, 1)
                    pool_count[0] += 1
                    at, far = 1 - at, 2 * far
                pool.wait_ge(pool_step, pool_count[0])
                nc.gpsimd.tensor_tensor(nth[:, :, 0:ne], rank[at][:, :, 16:16 + ne], src, ALU.mult)\
                    .then_inc(nth_made, 1)
                pool.wait_ge(rows_init, 16 * (HEADS // 2 + n * MAXC[1] // 8))
                for k in range(TOPK[n]):
                    pool.wait_ge(slots_made, n * TOPK[0] + k + 1)
                    for b in range(B):
                        if k == 0:
                            pool.wait_ge(h_staged, n * B + b + 1)
                        nc.gpsimd.indirect_dma_start(
                            out=rows_s, out_offset=bass.IndirectOffsetOnAxis(ap=slot_i[:, k, b:b + 1], axis=0),
                            in_=staged[:, b, k, :], in_offset=None).then_inc(rows_sent[k], 16)
                turns, more = load_turns(pool, n)

                def send(i, r, ahead):
                    c, _, last_unit, slot, _ = chunk_of(n, i, r, ahead)
                    if not last_unit:
                        return
                    if not is_zero(c):
                        pool.wait_ge(f.ticked, c)
                    pool.wait_ge(f.y_made, c + 1)
                    nc.gpsimd.tensor_tensor(tick[:], ident[0:1, 0:1], ident[0:1, 0:1], ALU.mult).then_inc(f.ticked, 1)
                    for t in range(TILES):
                        nc.gpsimd.indirect_dma_start(
                            out=y_s[n], out_offset=bass.IndirectOffsetOnAxis(ap=place[slot][:, t:t + 1], axis=0),
                            in_=y_sb[slot][:, t, :], in_offset=None, bounds_check=TOPK[n] * TOK - 1,
                            oob_is_err=False).then_inc(f.sent[slot], 16)

                def step(i, r, first, last):
                    if not (first and r == 0):
                        send(i, r, -1)

                run_steps(pool, n, step, more)
                send(turns, 0, -1)
                if n == 0:
                    power(2)
                    wait_normed(pool, 2, B)
                    pool.wait_ge(ctx_in, 16)
                    nc.gpsimd.tensor_tensor(x_sb[:], x_sb[:], ctx_sb[:], ALU.add).then_inc(ctx_added, 1)

                    def power2(g):
                        pool.wait_ge(var2_ready, g + 1)
                        bs = slice(4 * g, 4 * g + 4)
                        nc.gpsimd.tensor_tensor(rstd2[:, bs], veps2[:, bs], minus_half[0:LAT].to_broadcast([LAT, 4]),
                                                ALU.pow).then_inc(rstd2_ready, 1)

                    def gamma(c):
                        pool.wait_ge(z_made, 2 * c + 2)
                        chunk = tx[:, 2 * c:2 * c + 2]
                        nc.gpsimd.tensor_tensor(chunk, chunk, gamma_sb[:].unsqueeze(1).to_broadcast([LAT, 2, D]),
                                                ALU.mult).then_inc(zg_made, 1)

                    def beta(c):
                        pool.wait_ge(zg_made, c + 1)
                        chunk = tx[:, 2 * c:2 * c + 2]
                        nc.gpsimd.tensor_tensor(chunk, chunk, beta_sb[:].unsqueeze(1).to_broadcast([LAT, 2, D]),
                                                ALU.add).then_inc(zb_made, 1)

                    power2(0)
                    gamma(0)
                    power2(1)
                    beta(0)
                    gamma(1)
                    beta(1)

        @block.scalar
        def _(act):
            act.dma_start(x_sb[:], x_d.rearrange("b s d -> s b d")).then_inc(x_in, 16)
            act.dma_start(wr_sb[:], wr_d.rearrange("(k p) e -> p k e", p=P)).then_inc(rw_in, 16)
            act.dma_start(gate_sb[:], gate_d.rearrange("(k p) e -> p k e", p=P)).then_inc(rw_in, 16)
            for dst, src in ((theta_sb[:], theta_d), (phi_sb[:], phi_d), (gw_sb[:], g_d), (theta_b[:], theta_b_d),
                             (phi_b[:], phi_b_d), (g_b[:], g_b_d.partition_broadcast(P)),
                             (gamma_sb[:], gamma_d), (beta_sb[:], beta_d), (outw_sb[:], outw_d),
                             (outb_sb[:], outb_d)):
                act.dma_start(dst, src).then_inc(par_in, 16)

            def normalise_half(k):
                act.wait_ge(shift_ready, k + 1)
                for b in range(B // 2, B):
                    nc.scalar.activation(h_sb[:, b], x_sb[:, b], ACT.Identity, bias=shift[:, b:b + 1],
                                         scale=rstd[:, b:b + 1]).then_inc(normed[1], 1)

            def load_table(func, place):
                nc.scalar.activation(idle[:, place:place + 1], ident[0:1, 0:1], func)

            normalise_half(0)
            act.wait_ge(rw_in, 32)
            for n, w in enumerate((wr_sb, gate_sb)):
                nc.scalar.activation(rw[n][:, :, 0:EXPERTS[n]], w[:], ACT.Copy).then_inc(rw_hi_made, 1)
            act.wait_ge(ident_made, 2)
            for c in range(4):
                act.wait_ge(q_turned, c + 1)
                for blk in range(KB):
                    src = bank[c][:].rearrange("p (b k h i) -> p k b h i", b=2, k=KB, i=HD)[:, blk]
                    dst = qT[:, blk].rearrange("p h (b i) -> p b h i", i=HD)[:, 2 * c:2 * c + 2]
                    last = nc.scalar.activation(dst, src, ACT.Copy)
                last.then_inc(q_copied, 1)

            for n in range(2):
                f, ne = ffns[n], EXPERTS[n]
                load_table((ACT.Exp, ACT.Sigmoid)[n], 2 * n)
                if n == 1:
                    act.wait_ge(s_up_in, 64)
                    for u in range(2):
                        nc.scalar.activation(w_hi[u][:], up_raw[u][:], ACT.Copy).then_inc(s_w_hi, 1)
                normalise_half(1 if n == 0 else 3)
                for c in range(4):
                    act.wait_ge(hT_turned, 4 * n + c + 1)
                    half, k = c // 2, c % 2
                    nc.scalar.activation(hT_hi[:, k, half * HALF:(half + 1) * HALF], bank[c][:], ACT.Copy)\
                        .then_inc(hT_hi_made, 1)
                for c in range(2):
                    act.wait_ge(lgT_done, 2 * n + c + 1)
                    nc.scalar.activation(lgT[0:2 * ne, c * HALF:(c + 1) * HALF], bank[4 + c][0:2 * ne, :], ACT.Copy)\
                        .then_inc(lgT_copied, 1)
                if n == 0:
                    act.wait_ge(act_gate_in, 1)
                    nc.scalar.activation(ex[:], ex[:], ACT.Exp).then_inc(act_gate_out, 1)
                else:
                    act.wait_ge(act_gate_in, 2)
                    nc.scalar.activation(score[:, :, 0:E1], score[:, :, 0:E1], ACT.Sigmoid).then_inc(act_gate_out, 1)
                def shared_silu(q):
                    act.wait_ge(s_g_done, q + 1)
                    if q >= 2:
                        act.wait_ge(s_hid, q - 1)
                    nc.scalar.activation(silu_g[q % 2][:], bank[4][:], ACT.Silu).then_inc(s_silu, 1)
                    act.wait_ge(s_u_done, q + 1)
                    nc.scalar.activation(up_copy[q % 2][:], bank[5][:], ACT.Copy).then_inc(s_u_copied, 1)

                for b in range(B):
                    if n == 1 and b % 2 == 0 and b < 4:
                        shared_silu(b // 2)
                    nc.scalar.activation(staged[:, b, 0:TOPK[n], 0:D],
                                         h_sb[:, b].unsqueeze(1).to_broadcast([P, TOPK[n], D]), ACT.Copy)\
                        .then_inc(h_staged, 1)
                if n == 0:
                    load_table(ACT.Silu, 1)
                if n == 1:
                    shared_silu(2)
                    shared_silu(3)
                    for c in range(4):
                        act.wait_ge(s_down, 4)
                        half, k = c % 2, c // 2
                        nc.scalar.activation(yT[:, k, half * HALF:(half + 1) * HALF], bank[c][:], ACT.Copy)\
                            .then_inc(yT_copied, 1)
                turns, more = load_turns(act, n)

                def high_parts(i, r, ahead):
                    c, first_unit, _, cslot, _ = chunk_of(n, i, r, ahead)
                    if first_unit:
                        act.wait_ge(f.xT_turned, c + 1)
                        par = cslot % 2
                        nc.scalar.activation(xT_hi[par][:].rearrange("p k c -> p (k c)"), bank[2 + par][:], ACT.Copy)\
                            .then_inc(f.x_hi_made, 1)
                    slot, filled = step_slot(i, r, ahead)
                    act.wait_ge(f.up_in[slot], 16 * filled + 16)
                    nc.scalar.activation(w_hi[slot % 2][:], up_raw[slot][:], ACT.Copy).then_inc(f.w_hi_made, 1)

                def take_y(i, r, ahead):
                    c, _, last_unit, slot, _ = chunk_of(n, i, r, ahead)
                    if not last_unit:
                        return
                    act.wait_ge(f.down_done, 4 * i + r + ahead + 1)
                    for t in range(TILES):
                        last = nc.scalar.activation(y_sb[slot][:, t], bank[4 + slot % 2][:, t * D:(t + 1) * D],
                                                    ACT.Copy, scale=meta[slot][:, t, 0:1])
                    last.then_inc(f.y_made, 1)

                high_parts(0, 0, 0)
                high_parts(0, 1, 0)

                def step(i, r, first, last):
                    s = 4 * i + r
                    act.wait_ge(f.up_done, s + 1)
                    nc.scalar.activation(silu_g[r % 2][:, 0:TILES * P], bank[r % 2][:, 0:TILES * P], ACT.Silu)\
                        .then_inc(f.silu_made, 1)
                    if not (last and r >= 2):
                        high_parts(i, r, 2)
                    if not (first and r == 0):
                        take_y(i, r, -1)

                run_steps(act, n, step, more)
                take_y(turns, 0, -1)
                if n == 1:
                    continue

                act.wait_ge(par_in, 160)
                for c in range(4):
                    act.wait_ge(th_done, c + 1)
                    nc.scalar.activation(thT[:, 2 * c:2 * c + 2].rearrange("p b t -> p (b t)"), bank[c][0:LAT, :],
                                         ACT.Identity, bias=theta_b[:]).then_inc(th_copied, 1)
                normalise_half(2)
                for c in range(4):
                    act.wait_ge(ph_done, c + 1)
                    nc.scalar.activation(phT[:, 2 * c:2 * c + 2].rearrange("p b t -> p (b t)"), bank[4 + c][0:LAT, :],
                                         ACT.Identity, bias=phi_b[:]).then_inc(ph_copied, 1)

                def exps(b):
                    act.wait_ge(max_made, b + 1)
                    if b >= 2:
                        act.wait_ge(pT_turned, b - 1)
                    for t in range(KB):
                        last = nc.scalar.activation(prob[b % 2][:, t], bank[SCORES[b % 3]][:, t * D:(t + 1) * D],
                                                    ACT.Exp, bias=nmax[:, b, t:t + 1],
                                                    accum_out=psum_row[:, b, t:t + 1])
                    last.then_inc(exp_made, 1)

                def copy_pT(b):
                    act.wait_ge(pT_turned, b + 1)
                    if b >= 2:
                        act.wait_ge(tx_done, b - 1)
                    nc.scalar.activation(probT[b % 2][:].rearrange("p k t -> p (k t)"), bank[6 + b % 2][:], ACT.Copy)\
                        .then_inc(pT_copied, 1)

                def copy_tx(b):
                    act.wait_ge(tx_done, b + 1)
                    nc.scalar.activation(tx[:, b], bank[2 + b % 2][0:LAT, 0:D], ACT.Copy).then_inc(tx_copied, 1)

                def spread_out(g):
                    act.wait_ge(shift_made, g + 1)
                    for b in range(4 * g, 4 * g + 4):
                        nc.scalar.activation(tx[:, b], tx[:, b], ACT.Identity, scale=rstd2[:, b:b + 1],
                                             bias=shift2[:, b:b + 1]).then_inc(z_made, 1)

                def rectify(g):
                    for c in (2 * g, 2 * g + 1):
                        act.wait_ge((zb_made, zb_made2)[g], c - 2 * g + 1)
                        nc.scalar.activation(tx[:, 2 * c:2 * c + 2], tx[:, 2 * c:2 * c + 2], ACT.Relu)\
                            .then_inc(relu_made, 1)

                exps(0)
                for b in range(B):
                    if b + 1 < B:
                        exps(b + 1)
                    copy_pT(b)
                    if b >= 1:
                        copy_tx(b - 1)
                copy_tx(B - 1)
                spread_out(0)
                spread_out(1)
                rectify(0)
                rectify(1)

        @block.vector
        def _(dve):
            count = [0]

            def link(ins):
                count[0] += 1
                ins.then_inc(dve_step, 1)
                dve.wait_ge(dve_step, count[0])

            def layer_norm(k, added):
                for b in range(B):
                    if added and b % 2 == 0:
                        dve.wait_ge(x_added, added - 3 + b // 2)
                    last = nc.vector.bn_stats(stats[:, b, :], x_sb[:, b, :])
                link(last)
                for b in range(B):
                    last = nc.vector.bn_aggr(mv[:, b, :], stats[:, b, :])
                link(last)
                nc.vector.tensor_scalar(veps[:], mv[:, :, 1], EPS, None, ALU.add).then_inc(var_ready, 1)
                dve.wait_ge(rstd_ready, k + 1)
                nc.vector.scalar_tensor_tensor(out=shift[:], in0=mv[:, :, 0], scalar=-1.0, in1=rstd[:],
                                               op0=ALU.mult, op1=ALU.mult).then_inc(shift_ready, 1)
                for b in range(B // 2):
                    nc.vector.tensor_scalar(h_sb[:, b, :], x_sb[:, b, :], mv[:, b, 0:1], rstd[:, b:b + 1],
                                            ALU.subtract, ALU.mult).then_inc(normed[0], 1)

            def add_banks(turned, wait, first_bank):
                for c in range(4):
                    dve.wait_ge(turned, wait + c)
                    dst = x_sb[:, 2 * c:2 * c + 2].rearrange("p b d -> p (b d)")
                    ins = nc.vector.tensor_tensor(dst, dst, bank[first_bank + c][:], ALU.add)
                    ins.then_inc(x_added, 1)

            dve.wait_ge(filt_in, 32)
            nc.vector.tensor_tensor(filt_row[:, P - 1:P], filt_row[:, P - 1:P], skip_col[:], ALU.add)\
                .then_inc(filt_summed, 1)
            dve.wait_ge(x_in, 16)
            layer_norm(0, 0)
            nc.vector.memset(logit[:, :, E0:2 * E0], LOWEST)
            for i in range(2):
                nc.vector.memset(rank[i][:, :, 0:16], 0.0)
                nc.vector.memset(cend[i][:, 0:16], 0.0)
                nc.vector.memset(cum[i][:, 0:4], 0.0)
            nc.vector.memset(gmax[:, :, GROUPS:2 * GROUPS], PAD)
            nc.vector.memset(allowed[:, :, E1:E1 + 8], PAD).then_inc(dve_consts, 1)
            for n, w in enumerate((wr_sb, gate_sb)):
                dve.wait_ge(rw_hi_made, n + 1)
                e = EXPERTS[n]
                nc.vector.tensor_tensor(rw[n][:, :, e:2 * e], w[:], rw[n][:, :, 0:e].bitcast(f32), ALU.subtract)\
                    .then_inc(rw_split, 1)

            dve.wait_ge(q_copied, 4)

            def head(h, slot):
                dve.wait_ge(conv_done, h + 1)
                q = qT[:, :, bass.ds(h, 1), :].rearrange("p k o n -> p k (o n)").unsqueeze(3)\
                    .to_broadcast([P, KB, B * HD, HD])
                for blk in range(KB):
                    ins = nc.vector.tensor_tensor(
                        prod[slot][:, blk].rearrange("p (n j) -> p n j", j=HD),
                        bank[4 + 2 * slot + blk][:].rearrange("p (n j) -> p n j", j=HD), q[:, blk], ALU.mult)
                ins.then_inc(prod_made, 1)
                dve.wait_ge(prod_made, h + 1)
                o = oT.rearrange("p k b (h j) -> p (k b) h j", j=HD)[:, :, bass.ds(h, 1), :]\
                    .rearrange("p n o j -> p n (o j)")
                nc.vector.tensor_reduce(o, prod[slot][:].rearrange("p k (b i j) -> p (k b) j i", i=HD, j=HD),
                                        AX.X, ALU.add).then_inc(head_done, 1)

            with dve.Fori(0, HEADS // 2) as i:
                for slot in range(2):
                    head(2 * i + slot, slot)
            add_banks(o_turned, 1, 0)

            def sum_over_blocks(n):
                ne = EXPERTS[n]
                dve.wait_ge(mask_made, n + 1)
                link(nc.vector.tensor_copy(cum[0][:, 4:4 + B, 0:ne], mask[:, :, 0:ne]))
                for at, far in ((0, 1), (1, 2), (0, 4)):
                    ins = nc.vector.tensor_tensor(cum[1 - at][:, 4:4 + B, 0:ne], cum[at][:, 4:4 + B, 0:ne],
                                                  cum[at][:, 4 - far:4 - far + B, 0:ne], ALU.add)
                    if far < 4:
                        link(ins)
                ins.then_inc(cum_made, 1)

            for n in range(2):
                f, upe = ffns[n], UPE[n]
                layer_norm(1 if n == 0 else 3, (X_ATT0, X_ATT1)[n])
                for c in range(4):
                    dve.wait_ge(hT_hi_made, 4 * n + c + 1)
                    half, k = c // 2, c % 2
                    cols = slice(half * HALF, (half + 1) * HALF)
                    nc.vector.tensor_tensor(hT_lo[:, k, cols], bank[c][:], hT_hi[:, k, cols].bitcast(f32),
                                            ALU.subtract).then_inc(hT_lo_made, 1)
                g = gates[n]
                if n == 0:
                    dve.wait_ge(logits_done, 1)
                    lg = bank[6][:, 0:2 * B * E0].rearrange("p (b m e) -> p b m e", m=2, e=E0)
                    link(nc.vector.tensor_copy(logit[:, :, 0:E0], lg[:, :, 0]))
                    link(nc.vector.tensor_tensor(logit[:, :, 0:E0], logit[:, :, 0:E0], lg[:, :, 1], ALU.add))
                    for b in range(B):
                        last = nc.vector.max(out=top8[:, b, :], in_=logit[:, b, 0:E0])
                    link(last)
                    nc.vector.tensor_tensor(ex[:], logit[:, :, 0:E0], top8[:, :, 0:1].to_broadcast([P, B, E0]),
                                            ALU.subtract).then_inc(act_gate_in, 1)
                    dve.wait_ge(act_gate_in, 1)
                    link(nc.vector.memset(top8[:, :, 2:8], LOWEST))
                    for b in range(B):
                        last = nc.vector.match_replace(out=marked[:, b, :], in_to_replace=top8[:, b, :],
                                                       in_values=logit[:, b, :], imm_value=-LOWEST)
                    link(last)
                    nc.vector.tensor_scalar(mask[:, :, 0:E0], marked[:, :, 0:E0], -LOWEST, None, ALU.is_equal)\
                        .then_inc(mask_made, 1)
                    sum_over_blocks(n)
                    dve.wait_ge(act_gate_out, 1)
                    link(nc.vector.scalar_tensor_tensor(out=g[:], in0=marked[:, :, 0:E0], scalar=-LOWEST, in1=ex[:],
                                                        op0=ALU.is_equal, op1=ALU.mult))
                    link(nc.vector.tensor_reduce(gsum[:], g[:], AX.X, ALU.add))
                    link(nc.vector.reciprocal(grec[:], gsum[:]))
                    link(nc.vector.tensor_tensor(g[:], g[:], grec[:].unsqueeze(2).to_broadcast([P, B, E0]), ALU.mult))
                else:
                    dve.wait_ge(logits_done, 2)
                    lg = bank[6][:].rearrange("p (b m e) -> p b m e", m=2, e=E1)
                    link(nc.vector.tensor_copy(score[:, :, 0:E1], lg[:, :, 0]))
                    nc.vector.tensor_tensor(score[:, :, 0:E1], score[:, :, 0:E1], lg[:, :, 1], ALU.add)\
                        .then_inc(act_gate_in, 1)
                    dve.wait_ge(act_gate_out, 2)
                    s4 = score[:, :, 0:E1].rearrange("p b (g i) -> p b g i", i=GSIZE)
                    link(nc.vector.tensor_reduce(gmax[:, :, 0:GROUPS], s4, AX.X, ALU.max))
                    for b in range(B):
                        last = nc.vector.max(out=top8[:, b, :], in_=gmax[:, b, 0:GROUPS])
                    link(last)
                    link(nc.vector.memset(top8[:, :, TOPG:8], PAD))
                    for b in range(B):
                        last = nc.vector.match_replace(out=marked[:, b, :], in_to_replace=top8[:, b, :],
                                                       in_values=gmax[:, b, :], imm_value=TAKEN)
                    link(last)
                    link(nc.vector.tensor_scalar(gmask[:], marked[:, :, 0:GROUPS], TAKEN, None, ALU.is_equal))
                    link(nc.vector.tensor_scalar(gneg[:], gmask[:], -1.0, None, ALU.add))
                    a4 = allowed[:, :, 0:E1].rearrange("p b (g i) -> p b g i", i=GSIZE)
                    for bh in range(2):
                        bs = slice(4 * bh, 4 * bh + 4)
                        last = nc.vector.tensor_tensor(
                            a4[:, bs], s4[:, bs],
                            gmask[:, bs].unsqueeze(3).to_broadcast([P, 4, GROUPS, GSIZE]), ALU.mult)
                    link(last)
                    for bh in range(2):
                        bs = slice(4 * bh, 4 * bh + 4)
                        last = nc.vector.tensor_tensor(
                            a4[:, bs], a4[:, bs],
                            gneg[:, bs].unsqueeze(3).to_broadcast([P, 4, GROUPS, GSIZE]), ALU.add)
                    link(last)
                    for b in range(B):
                        last = nc.vector.max(out=top8[:, b, :], in_=allowed[:, b, 0:E1])
                    link(last)
                    link(nc.vector.memset(top8[:, :, TOPK1:8], PAD))
                    for b in range(B):
                        last = nc.vector.match_replace(out=marked1[:, b, :], in_to_replace=top8[:, b, :],
                                                       in_values=allowed[:, b, :], imm_value=TAKEN)
                    link(last)
                    nc.vector.tensor_scalar(mask[:], marked1[:, :, 0:E1], TAKEN, None, ALU.is_equal)\
                        .then_inc(mask_made, 1)
                    sum_over_blocks(n)
                    link(nc.vector.scalar_tensor_tensor(out=g[:], in0=marked1[:, :, 0:E1], scalar=TAKEN,
                                                        in1=score[:, :, 0:E1], op0=ALU.is_equal, op1=ALU.mult))
                    link(nc.vector.tensor_reduce(gsum[:], g[:], AX.X, ALU.add))
                    link(nc.vector.reciprocal(grec[:], gsum[:]))
                    link(nc.vector.scalar_tensor_tensor(out=g[:], in0=g[:], scalar=ROUTE_SCALE,
                                                        in1=grec[:].unsqueeze(2).to_broadcast([P, B, E1]),
                                                        op0=ALU.mult, op1=ALU.mult))

                ne = EXPERTS[n]
                dve.wait_ge(mask_made, n + 1)
                dve.wait_ge(ranked, n + 1)
                dve.wait_ge(consts_made, 1)
                within = bank[7][:, 0:B * ne].rearrange("p (b e) -> p b e", e=ne)
                have = bank[7][:, B * ne:(B + 1) * ne]
                ch, base = chunks[:, 0:ne], sbase[:, 0:ne]
                link(nc.vector.tensor_scalar(ch, have, float(CHUNK), 1.0, ALU.is_gt, ALU.add))
                for more in range(2, TOK // CHUNK):
                    link(nc.vector.scalar_tensor_tensor(out=ch, in0=have, scalar=float(more * CHUNK), in1=ch,
                                                        op0=ALU.is_gt, op1=ALU.add))
                link(nc.vector.tensor_copy(cend[0][:, 16:16 + ne], ch))
                at, far = 0, 1
                while far < ne:
                    link(nc.vector.tensor_tensor(cend[1 - at][:, 16:16 + ne], cend[at][:, 16:16 + ne],
                                                 cend[at][:, 16 - far:16 - far + ne], ALU.add))
                    at, far = 1 - at, 2 * far
                ce = cend[at][:, 16:16 + ne]
                link(nc.vector.tensor_tensor(base, ce, ch, ALU.subtract))
                link(nc.vector.tensor_scalar(base, base, float(CHUNK), float(BASEC[n] * CHUNK), ALU.mult, ALU.add))
                sf = slot_f[:, :, 0:ne]
                link(nc.vector.tensor_tensor(sf, within, base.unsqueeze(1).to_broadcast([P, B, ne]), ALU.add))
                dve.wait_ge(nth_made, n + 1)
                def chunk_table():
                    ahead = 2 // UPE[n]
                    maxc = MAXC[n] + ahead
                    link(nc.vector.tensor_tensor(past[:, 0:maxc, 0:ne], ce[0:1].unsqueeze(1)
                                                 .to_broadcast([1, maxc, ne]),
                                                 chunk_no[:, 0:maxc].unsqueeze(2).to_broadcast([1, maxc, ne]), ALU.is_le))
                    link(nc.vector.tensor_reduce(expert_f[:, 0:maxc], past[:, 0:maxc, 0:ne], AX.X, ALU.add))
                    link(nc.vector.tensor_scalar(expert_f[:, 0:maxc], expert_f[:, 0:maxc], float(ne - 1), None, ALU.min))
                    link(nc.vector.scalar_tensor_tensor(out=experts_i[n][:, 0:MAXC[n]], in0=expert_f[:, ahead:maxc],
                                                        scalar=float(ne), in1=expert_f[:, 0:MAXC[n]],
                                                        op0=ALU.mult, op1=ALU.add))
                    per_turn = 4 // UPE[n]
                    link(nc.vector.tensor_scalar(expert_f[:, 0:MAXT[n]], chunk_no[:, 0:MAXT[n]], float(per_turn),
                                                 None, ALU.mult))
                    link(nc.vector.tensor_scalar(expert_f[:, 0:MAXT[n]], expert_f[:, 0:MAXT[n]],
                                                 ce[0:1, ne - 1:ne], None, ALU.is_lt))
                    link(nc.vector.tensor_reduce(more_f[:], expert_f[:, MINT[n]:MAXT[n]], AX.X, ALU.add))
                    nc.vector.tensor_copy(more_i[n][:], more_f[:]).then_inc(table_made, 1)

                def shared_hid(q):
                    dve.wait_ge(s_u_copied, q + 1)
                    if q >= 2:
                        dve.wait_ge(s_down, q - 1)
                    nc.vector.tensor_tensor(hid[q % 2][:], silu_g[q % 2][:], up_copy[q % 2][:], ALU.mult)\
                        .then_inc(s_hid, 1)

                for k in range(TOPK[n]):
                    if k == 1:
                        if n == 1:
                            shared_hid(0)
                            shared_hid(1)
                        chunk_table()
                    if k in (3, 4):
                        shared_hid(k - 1)
                    for values, buf in ((sf, pick[0]), (g[:], pick[1])):
                        pk = buf[:, :, 0:ne]
                        link(nc.vector.scalar_tensor_tensor(out=pk, in0=nth[:, :, 0:ne], scalar=float(k + 1),
                                                            in1=values, op0=ALU.is_equal, op1=ALU.mult))
                        if values is sf:
                            link(nc.vector.tensor_reduce(slot_k[:], pk, AX.X, ALU.add))
                            link(nc.vector.tensor_copy(slot_i[:, k, :], slot_k[:]))
                        else:
                            nc.vector.tensor_reduce(staged[:, :, k, D], pk, AX.X, ALU.add).then_inc(slots_made, 1)
                if n == 1:
                    add_banks(y_turned, 1, 4)

                turns, more = load_turns(dve, n)

                def low_parts(i, r, ahead):
                    c, first_unit, _, cslot, _ = chunk_of(n, i, r, ahead)
                    if first_unit:
                        dve.wait_ge(f.x_hi_made, c + 1)
                        par = cslot % 2
                        if not (isinstance(c, int) and c < 4 // upe):
                            dve.wait_ge(f.y_made, c - 4 // upe + 1)
                        nc.vector.tensor_copy(meta[cslot][:], rowbuf[cslot][:, :, D:D + 2])
                        nc.vector.tensor_tensor(xT_lo[par][:].rearrange("p k c -> p (k c)"), bank[2 + par][:],
                                                xT_hi[par][:].rearrange("p k c -> p (k c)").bitcast(f32),
                                                ALU.subtract).then_inc(f.x_split, 1)
                    slot, _ = step_slot(i, r, ahead)
                    dve.wait_ge(f.w_hi_made, 4 * i + r + ahead + 1)
                    nc.vector.tensor_tensor(w_lo[slot % 2][:], up_raw[slot][:], w_hi[slot % 2][:].bitcast(f32),
                                            ALU.subtract).then_inc(f.w_split, 1)

                low_parts(0, 0, 0)
                low_parts(0, 1, 0)

                def step(i, r, first, last):
                    s = 4 * i + r
                    _, _, last_unit, cslot, filled = chunk_of(n, i, r, 0)
                    dve.wait_ge(f.silu_made, s + 1)
                    if last_unit:
                        if not is_zero(filled):
                            dve.wait_ge(f.sent[cslot], 32 * filled)
                        nc.vector.tensor_copy(place[cslot][:], meta[cslot][:, :, 1].bitcast(i32))
                    up_v, sg = bank[r % 2][:, TILES * P:2 * TILES * P], silu_g[r % 2][:, 0:TILES * P]
                    out = hid[r % 2][:, 0:TILES * P]
                    if n == 0:
                        ins = nc.vector.scalar_tensor_tensor(out=out, in0=sg, scalar=SWIGLU_LIMIT, in1=up_v,
                                                             op0=ALU.min, op1=ALU.mult)
                    else:
                        ins = nc.vector.tensor_tensor(out, sg, up_v, ALU.mult)
                    ins.then_inc(f.hid_made, 1)
                    if not (last and r >= 2):
                        low_parts(i, r, 2)

                run_steps(dve, n, step, more)
                base_k = n * TOPK[0]
                for k in range(TOPK[n]):
                    dve.wait_ge(y_in_done[k % 2], 16 * (n * TOPK[0] // 2 + k // 2 + 1))
                    if k:
                        dve.wait_ge(y_in_used, base_k + k)
                    if k < TOPK[n] - 1:
                        ins = nc.vector.tensor_tensor(x_sb[:], x_sb[:], y_in[k % 2], ALU.add)
                        ins.then_inc(y_in_used, 1)
                    else:
                        for c in range(4):
                            part = x_sb[:, 2 * c:2 * c + 2]
                            nc.vector.tensor_tensor(part, part, y_in[k % 2][:, 2 * c:2 * c + 2], ALU.add)\
                                .then_inc(x_added, 1)
                        dve.sem_inc(y_in_used, 1)
                if n == 1:
                    continue

                layer_norm(2, X_FFN0)
                dve.wait_ge(par_in, 160)
                for c in range(2):
                    dve.wait_ge(gx_done, c + 1)
                    nc.vector.tensor_tensor(gx[:, 4 * c:4 * c + 4].rearrange("p b k l -> p (b k) l"),
                                            bank[c][:].rearrange("p (n l) -> p n l", l=LAT),
                                            g_b[:].unsqueeze(1).to_broadcast([P, 4 * KB, LAT]), ALU.add)\
                        .then_inc(gx_copied, 1)

                def row_max(b):
                    dve.wait_ge(sc_done, b + 1)
                    nc.vector.tensor_reduce(nmax[:, b, :], bank[SCORES[b % 3]][:].rearrange("p (k t) -> p k t", k=KB),
                                            AX.X, ALU.max, negate=True).then_inc(max_made, 1)

                def normalise(b):
                    dve.wait_ge(exp_made, b + 1)
                    link(nc.vector.reciprocal(prec[:, b, :], psum_row[:, b, :]))
                    for t in range(KB):
                        last = nc.vector.tensor_scalar(prob[b % 2][:, t], prob[b % 2][:, t], prec[:, b, t:t + 1],
                                                       None, ALU.mult)
                    last.then_inc(prob_made, 1)

                def tx_statistics(b):
                    dve.wait_ge(tx_copied, b + 1)
                    nc.vector.bn_stats(stats2[:, b, :], tx[:, b, :]).then_inc(tx_stats, 1)

                def mean_rows(g):
                    dve.wait_ge(tx_stats, 4 * g + 4)
                    for b in range(4 * g, 4 * g + 4):
                        last = nc.vector.bn_aggr(mv2[:, b, :], stats2[:, b, :])
                    last.then_inc(mean_in, 1)

                def spread_rows(g):
                    bs = slice(4 * g, 4 * g + 4)
                    dve.wait_ge(mean_done, g + 1)
                    link(nc.vector.tensor_copy(mean_all[:, bs], bank[1][0:LAT, 16 * g:16 * g + 4]))
                    link(nc.vector.tensor_tensor(dev[:, bs], mv2[:, bs, 0], mean_all[:, bs], ALU.subtract))
                    link(nc.vector.tensor_tensor(dev[:, bs], dev[:, bs], dev[:, bs], ALU.mult))
                    nc.vector.tensor_tensor(spread[:, bs], dev[:, bs], mv2[:, bs, 1], ALU.add).then_inc(dev_in, 1)

                def variance(g):
                    bs = slice(4 * g, 4 * g + 4)
                    dve.wait_ge(dev_done, g + 1)
                    nc.vector.tensor_scalar(veps2[:, bs], bank[1][0:LAT, 16 * g + 8:16 * g + 12], EPS, None, ALU.add)\
                        .then_inc(var2_ready, 1)

                def shifts(g):
                    bs = slice(4 * g, 4 * g + 4)
                    dve.wait_ge(rstd2_ready, g + 1)
                    nc.vector.scalar_tensor_tensor(out=shift2[:, bs], in0=mean_all[:, bs], scalar=-1.0,
                                                   in1=rstd2[:, bs], op0=ALU.mult, op1=ALU.mult)\
                        .then_inc(shift_made, 1)

                def affine():
                    for c in (2, 3):
                        dve.wait_ge(z_made, 2 * c + 2)
                        chunk = tx[:, 2 * c:2 * c + 2]
                        link(nc.vector.tensor_tensor(chunk, chunk, gamma_sb[:].unsqueeze(1).to_broadcast([LAT, 2, D]),
                                                     ALU.mult))
                        nc.vector.tensor_tensor(chunk, chunk, beta_sb[:].unsqueeze(1).to_broadcast([LAT, 2, D]),
                                                ALU.add).then_inc(zb_made2, 1)

                def add_out(g):
                    dve.wait_ge(ctx_added, 1)
                    for c in (2 * g, 2 * g + 1):
                        dve.wait_ge(w_done, c + 1)
                        dst = x_sb[:, 2 * c:2 * c + 2].rearrange("p b d -> p (b d)")
                        nc.vector.scalar_tensor_tensor(out=dst, in0=bank[OUT[c]][:], scalar=outb_sb[:], in1=dst,
                                                       op0=ALU.add, op1=ALU.add).then_inc(x_added, 1)

                row_max(0)
                row_max(1)
                for b in range(B):
                    normalise(b)
                    if b + 2 < B:
                        row_max(b + 2)
                    if b >= 2:
                        tx_statistics(b - 2)
                    if b == 5:
                        mean_rows(0)
                    if b == 6:
                        spread_rows(0)
                    if b == 7:
                        variance(0)
                        shifts(0)
                tx_statistics(B - 2)
                tx_statistics(B - 1)
                mean_rows(1)
                spread_rows(1)
                variance(1)
                shifts(1)
                affine()
                add_out(0)
                add_out(1)

        @block.tensor
        def _(pe):
            pe.wait_ge(ident_made, 2)
            for b in range(B):
                wait_normed(pe, 0, b + 1)
                for blk in range(KB):
                    col = (b % 2) * D + blk * P
                    last = nc.tensor.transpose(bank[b // 2][:, col:col + P], h_sb[:, b, blk * P:(blk + 1) * P],
                                               ident[:])
                if b % 2:
                    last.then_inc(q_turned, 1)

            def convolve(h, slot, toep_wait, free):
                pe.wait_ge(kv_made, h + 1)
                pe.wait_ge(toep_in[slot], toep_wait)
                if free is not None:
                    pe.wait_ge(prod_made, free)
                y0, y1 = bank[4 + 2 * slot][:], bank[5 + 2 * slot][:]
                near, far = toep[slot][:, 0:P], toep[slot][:, P:2 * P]
                nc.tensor.matmul(y0, near, kv[slot][:, 0], start=True, stop=True)
                nc.tensor.matmul(y1, near, kv[slot][:, 1], start=True, stop=False)
                nc.tensor.matmul(y1, far, kv[slot][:, 0], start=False, stop=True).then_inc(conv_done, 1)

            convolve(0, 0, 16, None)
            convolve(1, 1, 16, None)
            with pe.Fori(1, HEADS // 2) as i:
                for slot in range(2):
                    convolve(2 * i + slot, slot, 16 * (i + 1), 2 * i + slot - 1)
            pe.wait_ge(head_done, HEADS)
            pe.wait_ge(q_copied, 4)
            for b in range(B):
                for blk in range(KB):
                    col = (b % 2) * D + blk * P
                    last = nc.tensor.transpose(bank[b // 2][:, col:col + P], oT[:, blk, b, :], ident[:])
                if b % 2:
                    last.then_inc(o_turned, 1)

            def three_passes(out, w, xs, start, stop):
                (wh, wl), (xh, xl) = w, xs
                nc.tensor.matmul(out, wh, xh, start=start, stop=False)
                nc.tensor.matmul(out, wh, xl, start=False, stop=False)
                return nc.tensor.matmul(out, wl, xh, start=False, stop=stop)

            for n in range(2):
                f, ne, upe = ffns[n], EXPERTS[n], UPE[n]
                pe.wait_ge(x_added, (X_ATT0, X_ATT1)[n])
                for c in range(4):
                    half, k = c // 2, c % 2
                    for m in range(4):
                        b = 4 * half + m
                        wait_normed(pe, 1 if n == 0 else 3, b + 1)
                        last = nc.tensor.transpose(bank[c][:, m * P:(m + 1) * P], h_sb[:, b, k * P:(k + 1) * P],
                                                   ident[:])
                    last.then_inc(hT_turned, 1)
                pe.wait_ge(rw_split, n + 1)
                for half in range(2):
                    pe.wait_ge(hT_lo_made, 4 * n + 2 * half + 2)
                    cols = slice(half * HALF, (half + 1) * HALF)
                    for k in range(KB):
                        for x in (hT_hi, hT_lo):
                            last = nc.tensor.matmul(bank[4 + half][0:2 * ne, :], rw[n][:, k], x[:, k, cols],
                                                    start=(k == 0 and x is hT_hi), stop=(k == KB - 1 and x is hT_lo))
                    last.then_inc(lgT_done, 1)
                for b in range(B):
                    if b % 4 == 0:
                        pe.wait_ge(lgT_copied, 2 * n + b // 4 + 1)
                    last = nc.tensor.transpose(bank[6][:, b * 2 * ne:(b + 1) * 2 * ne],
                                               lgT[0:2 * ne, b * P:(b + 1) * P], ident[0:2 * ne, 0:2 * ne])
                last.then_inc(logits_done, 1)

                def shared_up(q):
                    u, half = q // 2, q % 2
                    pe.wait_ge(s_w_split, u + 1)
                    cols = slice(half * HALF, (half + 1) * HALF)
                    for m, done in enumerate((s_g_done, s_u_done)):
                        if q:
                            pe.wait_ge((s_silu, s_u_copied)[m], q)
                        for k in range(KB):
                            wc = slice((m * KB + k) * P, (m * KB + k + 1) * P)
                            last = three_passes(bank[4 + m][:], (w_hi[u][:, wc], w_lo[u][:, wc]),
                                                (hT_hi[:, k, cols], hT_lo[:, k, cols]), k == 0, k == KB - 1)
                        last.then_inc(done, 1)

                def shared_down(q):
                    u, half = q // 2, q % 2
                    pe.wait_ge(s_hid, q + 1)
                    for k in range(KB):
                        last = nc.tensor.matmul(bank[2 * k + half][:], down_raw[u][:, k * P:(k + 1) * P],
                                                hid[q % 2][:], start=(u == 0), stop=(u == 1))
                    last.then_inc(s_down, 1)

                if n == 1:
                    pe.wait_ge(lgT_copied, 4)
                    shared_up(0)
                    shared_up(1)
                pe.wait_ge(mask_made, n + 1)
                pe.wait_ge(consts_made, 1)
                mk = mask[:, :, 0:ne]
                nc.tensor.matmul(bank[7][:, 0:B * ne], before[:], mk, start=True, stop=False, skip_group_check=True)
                pe.wait_ge(cum_made, n + 1)
                nc.tensor.matmul(bank[7][:, 0:(B + 1) * ne], ones[:], cum[1][:, 3:4 + B, 0:ne], start=False,
                                 stop=True, skip_group_check=True).then_inc(ranked, 1)
                if n == 1:
                    shared_down(0)
                    shared_up(2)
                    shared_down(1)
                    shared_up(3)
                    shared_down(2)
                    shared_down(3)
                    pe.wait_ge(yT_copied, 4)
                    for b in range(B):
                        for k in range(KB):
                            col = (b % 2) * D + k * P
                            last = nc.tensor.transpose(bank[4 + b // 2][:, col:col + P],
                                                       yT[:, k, b * P:(b + 1) * P], ident[:])
                        if b % 2:
                            last.then_inc(y_turned, 1)
                    pe.wait_ge(x_added, X_ATT1 + 4)
                turns, more = load_turns(pe, n)

                def turn_rows(i, r, ahead):
                    c, first_unit, _, slot, filled = chunk_of(n, i, r, ahead)
                    if not first_unit:
                        return
                    pe.wait_ge(f.rows_in[slot], 16 * filled + 16)
                    for t in range(TILES):
                        for k in range(KB):
                            col = (k * TILES + t) * P
                            last = nc.tensor.transpose(bank[2 + slot % 2][:, col:col + P],
                                                       rowbuf[slot][:, t, k * P:(k + 1) * P], ident[:])
                    last.then_inc(f.xT_turned, 1)

                def up(i, r, first):
                    s = 4 * i + r
                    c, _, _, cslot, _ = chunk_of(n, i, r, 0)
                    pe.wait_ge(f.w_split, s + 1)
                    pe.wait_ge(f.x_split, c + 1)
                    if not (first and r < 2):
                        pe.wait_ge(f.hid_made, s - 1)
                    par = cslot % 2
                    for m in range(2):
                        for k in range(KB):
                            wc = slice((m * KB + k) * P, (m * KB + k + 1) * P)
                            last = three_passes(bank[r % 2][:, m * TILES * P:(m + 1) * TILES * P],
                                                (w_hi[r % 2][:, wc], w_lo[r % 2][:, wc]),
                                                (xT_hi[par][:, k], xT_lo[par][:, k]), k == 0, k == KB - 1)
                    last.then_inc(f.up_done, 1)

                def down(i, r, ahead):
                    s = 4 * i + r + ahead
                    c, first_unit, last_unit, cslot, _ = chunk_of(n, i, r, ahead)
                    slot, filled = step_slot(i, r, ahead)
                    pe.wait_ge(f.hid_made, s + 1)
                    pe.wait_ge(f.down_in[slot], 16 * filled + 16)
                    if first_unit and not (isinstance(c, int) and c < 2):
                        pe.wait_ge(f.y_made, c - 1)
                    for t in range(TILES):
                        last = nc.tensor.matmul(bank[4 + cslot % 2][:, t * D:(t + 1) * D],
                                                hid[slot % 2][:, t * P:(t + 1) * P], down_raw[slot][:],
                                                start=first_unit and t == 0, stop=last_unit and t == TILES - 1,
                                                skip_group_check=True)
                    last.then_inc(f.down_done, 1)

                turn_rows(0, 0, 0)
                if upe == 1:
                    turn_rows(0, 1, 0)

                def step(i, r, first, last):
                    up(i, r, first)
                    if not (last and r >= 2):
                        c, first_unit, _, _, _ = chunk_of(n, i, r, 2)
                        if first_unit and not (isinstance(c, int) and c < 2):
                            pe.wait_ge(f.x_split, c - 1)
                        turn_rows(i, r, 2)
                    if not (first and r == 0):
                        down(i, r, -1)

                run_steps(pe, n, step, more)
                down(turns, 0, -1)
                if n == 1:
                    continue

                pe.wait_ge(par_in, 160)
                pe.wait_ge(ctx_in, 16)
                pe.wait_ge(f.hid_made, 4 * turns)
                for c in range(4):
                    nc.tensor.matmul(bank[c][0:LAT, :], theta_sb[:],
                                     ctx_sb[:, 2 * c:2 * c + 2].rearrange("p b t -> p (b t)"), start=True, stop=True)\
                        .then_inc(th_done, 1)
                for c in range(4):
                    if c == 0:
                        pe.wait_ge(x_added, X_FFN0)
                    wait_normed(pe, 2, 2 * c + 2)
                    nc.tensor.matmul(bank[4 + c][0:LAT, :], phi_sb[:],
                                     h_sb[:, 2 * c:2 * c + 2].rearrange("p b t -> p (b t)"), start=True, stop=True)\
                        .then_inc(ph_done, 1)
                pe.wait_ge(th_copied, 4)
                for b in range(B):
                    for k in range(KB):
                        col = ((b % 4) * KB + k) * LAT
                        last = nc.tensor.matmul(bank[b // 4][:, col:col + LAT], h_sb[:, b, k * P:(k + 1) * P],
                                                gw_sb[:], start=True, stop=True)
                    if b % 4 == 3:
                        last.then_inc(gx_done, 1)
                pe.wait_ge(ph_copied, 4)

                def scores(b):
                    if b >= 3:
                        pe.wait_ge(exp_made, b - 2)
                    for t in range(KB):
                        last = nc.tensor.matmul(bank[SCORES[b % 3]][:, t * D:(t + 1) * D],
                                                thT[:, b, t * P:(t + 1) * P], phT[:, b, :], start=True, stop=True)
                    last.then_inc(sc_done, 1)

                def turn_probs(b):
                    pe.wait_ge(prob_made, b + 1)
                    if b >= 2:
                        pe.wait_ge(pT_copied, b - 1)
                    for k in range(KB):
                        for t in range(KB):
                            col = k * D + t * P
                            last = nc.tensor.transpose(bank[6 + b % 2][:, col:col + P],
                                                       prob[b % 2][:, t, k * P:(k + 1) * P], ident[:])
                    last.then_inc(pT_turned, 1)

                def weigh(b):
                    pe.wait_ge(pT_copied, b + 1)
                    if b >= 2:
                        pe.wait_ge(tx_copied, b - 1)
                    for k in range(KB):
                        last = nc.tensor.matmul(bank[2 + b % 2][0:LAT, 0:D], gx[:, b, k, :], probT[b % 2][:, k, :],
                                                start=(k == 0), stop=(k == KB - 1))
                    last.then_inc(tx_done, 1)

                def average(done, column, rows):
                    nc.tensor.matmul(bank[1][0:LAT, column:column + 4], avg[:], rows, start=True, stop=True)\
                        .then_inc(done, 1)

                def means(g):
                    pe.wait_ge(mean_in, g + 1)
                    average(mean_done, 16 * g, mv2[:, 4 * g:4 * g + 4, 0])

                def spreads(g):
                    pe.wait_ge(dev_in, g + 1)
                    average(dev_done, 16 * g + 8, spread[:, 4 * g:4 * g + 4])

                def outputs(g):
                    for c in (2 * g, 2 * g + 1):
                        pe.wait_ge(relu_made, c + 1)
                        nc.tensor.matmul(bank[OUT[c]][:], outw_sb[:],
                                         tx[:, 2 * c:2 * c + 2].rearrange("p b t -> p (b t)"),
                                         start=True, stop=True).then_inc(w_done, 1)

                scores(0)
                scores(1)
                pe.wait_ge(gx_copied, 2)
                pe.wait_ge(consts_made, 1)
                for b in range(B):
                    if b + 2 < B:
                        scores(b + 2)
                    turn_probs(b)
                    if b >= 1:
                        weigh(b - 1)
                    if b == 5:
                        means(0)
                    if b == 6:
                        spreads(0)
                weigh(B - 1)
                means(1)
                pe.wait_ge(tx_copied, B)
                spreads(1)
                outputs(0)
                outputs(1)


def kernel(x, ctx_2048, L0_xattn_ssm_kernel, L0_xattn_D, L0_ffn_Wr, L0_ffn_Wg, L0_ffn_Wu, L0_ffn_Wd,
           L1_xattn_theta_w, L1_xattn_theta_b, L1_xattn_phi_w, L1_xattn_phi_b, L1_xattn_g_w, L1_xattn_g_b,
           L1_xattn_ln_gamma, L1_xattn_ln_beta, L1_xattn_out_w, L1_xattn_out_b, L1_ffn_gate_w, L1_ffn_w11,
           L1_ffn_w33, L1_ffn_w22, L1_ffn_sw1, L1_ffn_sw2, L1_ffn_sw3):
    import numpy as np
    import concourse.bacc as bacc
    from concourse.bass_utils import run_bass_kernel_spmd

    def arr(a):
        return np.ascontiguousarray(np.asarray(a))

    def by_hidden(w):
        return w.reshape(-1, KB, P, P).transpose(0, 2, 1, 3).reshape(-1, P, KB * P)

    def halves(w):
        return w.reshape(-1, D, KB, P).transpose(0, 2, 1, 3).reshape(-1, D, P)

    wg, wu, wd = (np.asarray(a) for a in (L0_ffn_Wg, L0_ffn_Wu, L0_ffn_Wd))
    up0 = np.concatenate([by_hidden(halves(wg)), by_hidden(halves(wu))], axis=2)
    w1, w3, w2, s1, s2, s3 = (np.asarray(a) for a in (L1_ffn_w11, L1_ffn_w33, L1_ffn_w22, L1_ffn_sw1, L1_ffn_sw2,
                                                      L1_ffn_sw3))
    gate1 = np.concatenate([by_hidden(w1.transpose(0, 2, 1)), by_hidden(halves(s1.T[None]))])
    up1 = np.concatenate([by_hidden(w3.transpose(0, 2, 1)), by_hidden(halves(s3.T[None]))])
    down1 = np.concatenate([w2.transpose(0, 2, 1), s2.T.reshape(2, P, D)])
    ctx = np.asarray(ctx_2048)
    ctxr = ctx.transpose(2, 0, 1).reshape(KB, P, B, P)[:, ::-1]
    filt = np.pad(np.asarray(L0_xattn_ssm_kernel), ((0, 0), (P - 1, KPAD - (P - 1) - D)))
    arrays = {
        "x": arr(x), "ctx": arr(ctx), "ctxr": arr(ctxr), "filt": arr(filt),
        "skip": arr(np.asarray(L0_xattn_D).reshape(HEADS, 1)), "wr": arr(L0_ffn_Wr), "up0": arr(up0),
        "down0": arr(wd.reshape(UNITS0, P, D)),
        "theta": arr(np.asarray(L1_xattn_theta_w).T), "theta_b": arr(np.asarray(L1_xattn_theta_b).reshape(LAT, 1)),
        "phi": arr(np.asarray(L1_xattn_phi_w).T), "phi_b": arr(np.asarray(L1_xattn_phi_b).reshape(LAT, 1)),
        "g": arr(np.asarray(L1_xattn_g_w).T), "g_b": arr(L1_xattn_g_b),
        "gamma": arr(L1_xattn_ln_gamma), "beta": arr(L1_xattn_ln_beta),
        "outw": arr(np.asarray(L1_xattn_out_w).T), "outb": arr(np.asarray(L1_xattn_out_b).reshape(P, 1)),
        "gate": arr(np.asarray(L1_ffn_gate_w).T), "up1": arr(np.concatenate([gate1, up1], axis=2)),
        "down1": arr(down1),
    }
    nc = bacc.Bacc("TRN2", target_bir_lowering=False, num_devices=1)
    f32 = mybir.dt.float32
    ins = [nc.dram_tensor(f"in_{k}", a.shape, mybir.dt.from_np(a.dtype), kind="ExternalInput").ap()
           for k, a in arrays.items()]
    out = nc.dram_tensor("out", (B, S, D), f32, kind="ExternalOutput").ap()
    scratch = [nc.dram_tensor(name, shape, f32, kind="Internal").ap() for name, shape in (
        ("filt_s", (HEADS, KPAD)), ("rows_s", ((MAXC[0] + MAXC[1]) * CHUNK, ROW)),
        ("y0_s", (TOPK[0] * TOK, D)), ("y1_s", (TOPK[1] * TOK, D)))]
    build(nc, *ins, out, *scratch)
    r = run_bass_kernel_spmd(nc, [{f"in_{k}": a for k, a in arrays.items()}], core_ids=[0])
    return r.results[0]["out"]
```
